# Optimizing a Trainium2 kernel written in Bass

```python
import numpy as np
import jax
import jax.numpy as jnp

def _softmax(x, axis=-1):
    return jax.nn.softmax(x, axis=axis)

def _gelu(x):
    return jax.nn.gelu(x, approximate=True)

def _silu(x):
    return jax.nn.silu(x)

def _sigmoid(x):
    return jax.nn.sigmoid(x)

def _layernorm(x, axis=-1, eps=1e-05):
    m = jnp.mean(x, axis=axis, keepdims=True)
    v = jnp.var(x, axis=axis, keepdims=True)
    return (x - m) / jnp.sqrt(v + eps)

def _scatter_add(tgt, idx, src, axis=0):
    return tgt.at[idx].add(src)

def _segment_sum(src, seg, n):
    return jax.ops.segment_sum(src, seg, n)
kernel_name = 'mk_gnn_preln_d4_gnn_r32_783b6a'

def setup_inputs(seed: int=0):
    np.random.seed(seed)
    _w = jnp.asarray

    def _rec_inputs():
        import jax
        import jax.numpy as jnp
        _gk = jax.random.key(seed)
        x = -0.0009044 + 1 * jax.random.normal(jax.random.fold_in(_gk, 1), (3125, 160), jnp.float32)
        src = jax.random.randint(jax.random.fold_in(_gk, 2), (100000,), 0, 3125, jnp.int32)
        dst = jnp.minimum((3125 * jax.random.uniform(jax.random.fold_in(_gk, 3), (100000,)) ** 2.0).astype(jnp.int32), 99999)
        _o = jnp.argsort(dst, stable=True)
        src = src[_o]
        dst = dst[_o]
        edge_attr_10 = jax.random.uniform(jax.random.fold_in(_gk, 12), (100000, 10), jnp.float32, 0.0, 1)
        edge_attr_3 = 0.00047201 + 1.00023 * jax.random.normal(jax.random.fold_in(_gk, 13), (100000, 3), jnp.float32)
        edge_attr_4 = -0.000107899 + 1.00008 * jax.random.normal(jax.random.fold_in(_gk, 14), (100000, 4), jnp.float32)
        edge_attr_64 = 0.000279952 + 1.00013 * jax.random.normal(jax.random.fold_in(_gk, 15), (100000, 64), jnp.float32)
        edge_attr_8 = jax.random.uniform(jax.random.fold_in(_gk, 16), (100000, 8), jnp.float32, 0.0, 1)
        node_vec1 = jax.random.uniform(jax.random.fold_in(_gk, 18), (3125, 1), jnp.float32, 0.0, 1)
        return (x, src, dst, edge_attr_10, edge_attr_3, edge_attr_4, edge_attr_64, edge_attr_8, node_vec1)
    x, src, dst, edge_attr_10, edge_attr_3, edge_attr_4, edge_attr_64, edge_attr_8, node_vec1 = _rec_inputs()

    def _L0_gnn_setup():
        import jax, jax.numpy as jnp
        import numpy as np
        N_NODES = 10000
        N_EDGES = 10000
        MUL0, MUL1 = (64, 32)
        EDGE_DIM = 64
        W_NUMEL = 224
        DENOM = 32.0
        SQRT3 = 3.0 ** 0.5
        INV_SQRT3 = 1.0 / SQRT3
        INV_SQRT2 = 2.0 ** (-0.5)

        def _forward(node_feature, edge_attr, edge_feature, W_skip0, W_skip1, W_nl0, W_nl1, W_fc1, W_fc2, W_out_s, W_out_v, edge_index):
            N = node_feature.shape[0]
            E = edge_attr.shape[0]
            s = node_feature[:, :MUL0]
            v = node_feature[:, MUL0:].reshape(N, MUL1, 3)
            skip_s = s @ W_skip0
            skip_v = jnp.einsum('nmi,mk->nki', v, W_skip1)
            s = s @ W_nl0
            v = jnp.einsum('nmi,mk->nki', v, W_nl1)
            rhat = edge_attr / jnp.linalg.norm(edge_attr, axis=-1, keepdims=True)
            sh1 = SQRT3 * rhat
            w = jax.nn.relu(edge_feature @ W_fc1) @ W_fc2
            w0, w1, w2, w3, w4 = jnp.split(w, [64, 128, 160, 192], axis=-1)
            src, dst = (edge_index[0], edge_index[1])
            xs = s[dst]
            xv = v[dst]
            out0a = w0 * xs
            out0b = w3 * (jnp.einsum('emi,ei->em', xv, sh1) * INV_SQRT3)
            out1a = (w1 * xs)[:, :, None] * sh1[:, None, :]
            out1b = w2[:, :, None] * xv
            out1c = w4[:, :, None] * (jnp.cross(xv, sh1[:, None, :]) * INV_SQRT2)
            tp = jnp.concatenate([out0a, out0b, out1a.reshape(E, -1), out1b.reshape(E, -1), out1c.reshape(E, -1)], axis=-1)
            agg = jax.ops.segment_sum(tp, src, num_segments=N) / DENOM
            agg_s = agg[:, :96]
            agg_v = agg[:, 96:].reshape(N, 128, 3)
            out_s = agg_s @ W_out_s + skip_s
            out_v = jnp.einsum('nmi,mk->nki', agg_v, W_out_v) + skip_v
            fs = jax.nn.silu(out_s[:, :MUL0])
            gate = jax.nn.sigmoid(out_s[:, MUL0:MUL0 + 32])
            gv = gate[:, :, None] * out_v
            return jnp.concatenate([fs, gv.reshape(N, -1)], axis=-1)
        key = jax.random.key(seed)
        ks = jax.random.split(key, 12)

        def lin(k, fi, fo):
            return jax.random.normal(k, (fi, fo), jnp.float32) / np.float32(np.sqrt(fi))
        return {'node_feature': jax.random.normal(ks[0], (N_NODES, MUL0 + 3 * MUL1), jnp.float32), 'edge_attr': jax.random.normal(ks[1], (N_EDGES, 3), jnp.float32), 'edge_feature': jax.random.normal(ks[2], (N_EDGES, EDGE_DIM), jnp.float32), 'W_skip0': lin(ks[3], MUL0, 96), 'W_skip1': lin(ks[4], MUL1, 32), 'W_nl0': lin(ks[5], MUL0, MUL0), 'W_nl1': lin(ks[6], MUL1, MUL1), 'W_fc1': lin(ks[7], EDGE_DIM, 64), 'W_fc2': lin(ks[8], 64, W_NUMEL), 'W_out_s': lin(ks[9], 96, 96), 'W_out_v': lin(ks[10], 128, 32), 'edge_index': jax.random.randint(ks[11], (2, N_EDGES), 0, N_NODES)}
    _L0_gnn_all = _L0_gnn_setup()
    _L0_gnn_in = {k: v for k, v in _L0_gnn_all.items() if k in ('W_skip0', 'W_skip1', 'W_nl0', 'W_nl1', 'W_fc1', 'W_fc2', 'W_out_s', 'W_out_v')}
    del _L0_gnn_all

    def _L1_gnn_setup():
        import jax, jax.numpy as jnp
        import numpy as np
        N_NODES = 50000
        N_EDGES = 25000
        MUL0, MUL1 = (64, 32)
        N_BASIS, N_RADIAL = (10, 100)
        W_NUMEL = 192
        NUM_NEIGHBORS = 16.0
        INV_SQRT3 = np.float32(1.0 / np.sqrt(3.0))
        RELU_GAIN = np.float32(np.sqrt(2.0))
        FAN_L2 = np.float32(np.sqrt(MUL0 + MUL1))

        def _fctp_scalar_attr(x0, x1, a, W0, W1):
            o0 = x0 @ W0 * a * (1.0 / np.sqrt(W0.shape[0]))
            o1 = jnp.einsum('nud,uw->nwd', x1, W1) * a[..., None] * (1.0 / np.sqrt(W1.shape[0]))
            return (o0, o1)
        key = jax.random.key(seed)
        ks = jax.random.split(key, 16)
        return {'node_input': jax.random.normal(ks[0], (N_NODES, MUL0 + 3 * MUL1), jnp.float32), 'node_attr': jnp.ones((N_NODES, 1), jnp.float32), 'edge_attr': jax.random.normal(ks[1], (N_EDGES, 4), jnp.float32), 'edge_length_embedded': jax.random.uniform(ks[2], (N_EDGES, N_BASIS), dtype=jnp.float32), 'W_si0': jax.random.normal(ks[3], (MUL0, MUL0), jnp.float32), 'W_si1': jax.random.normal(ks[4], (MUL1, MUL1), jnp.float32), 'W_l1_0': jax.random.normal(ks[5], (MUL0, MUL0), jnp.float32), 'W_l1_1': jax.random.normal(ks[6], (MUL1, MUL1), jnp.float32), 'W_l2_00': jax.random.normal(ks[7], (MUL0, MUL0), jnp.float32), 'W_l2_10': jax.random.normal(ks[8], (MUL1, MUL0), jnp.float32), 'W_l2_01': jax.random.normal(ks[9], (MUL0, MUL1), jnp.float32), 'W_l2_11': jax.random.normal(ks[10], (MUL1, MUL1), jnp.float32), 'W_fc1': jax.random.normal(ks[11], (N_BASIS, N_RADIAL), jnp.float32), 'W_fc2': jax.random.normal(ks[12], (N_RADIAL, W_NUMEL), jnp.float32), 'edge_src': jax.random.randint(ks[13], (N_EDGES,), 0, N_NODES), 'edge_dst': jax.random.randint(ks[14], (N_EDGES,), 0, N_NODES)}
    _L1_gnn_all = _L1_gnn_setup()
    _L1_gnn_in = {k: v for k, v in _L1_gnn_all.items() if k in ('W_si0', 'W_si1', 'W_l1_0', 'W_l1_1', 'W_l2_00', 'W_l2_10', 'W_l2_01', 'W_l2_11', 'W_fc1', 'W_fc2')}
    del _L1_gnn_all

    def _L2_gnn_setup():
        import jax, jax.numpy as jnp
        import numpy as np
        N, E = (50000, 25000)
        MUL0, MUL1 = (64, 32)
        D = MUL0 + 3 * MUL1
        INV3 = float(1.0 / np.sqrt(3.0))
        INV6 = float(1.0 / np.sqrt(6.0))
        C0 = float(1.0 / np.sqrt(MUL0 + MUL1))
        C1 = float(np.sqrt(3.0 / (MUL0 + 2 * MUL1)))
        LIN_S = float(1.0 / np.sqrt(MUL0))
        LIN_V = float(1.0 / np.sqrt(MUL1))
        key = jax.random.key(seed)
        ks = jax.random.split(key, 10)
        x = jax.random.normal(ks[0], (N, D), dtype=jnp.float32)
        sh = jax.random.normal(ks[1], (E, 4), dtype=jnp.float32)
        edge_index = jax.random.randint(ks[2], (2, E), 0, N, dtype=jnp.int64)
        W1 = jax.random.normal(ks[3], (MUL0, MUL0), dtype=jnp.float32)
        W2 = jax.random.normal(ks[4], (MUL1, MUL0), dtype=jnp.float32)
        W3 = jax.random.normal(ks[5], (MUL0, MUL1), dtype=jnp.float32)
        W4 = jax.random.normal(ks[6], (MUL1, MUL1), dtype=jnp.float32)
        W5 = jax.random.normal(ks[7], (MUL1, MUL1), dtype=jnp.float32)
        Ws = jax.random.normal(ks[8], (MUL0, MUL0), dtype=jnp.float32)
        Wv = jax.random.normal(ks[9], (MUL1, MUL1), dtype=jnp.float32)
        return {'x': x, 'sh': sh, 'W1': W1, 'W2': W2, 'W3': W3, 'W4': W4, 'W5': W5, 'Ws': Ws, 'Wv': Wv, 'edge_index': edge_index}
    _L2_gnn_all = _L2_gnn_setup()
    _L2_gnn_in = {k: v for k, v in _L2_gnn_all.items() if k in ('W1', 'W2', 'W3', 'W4', 'W5', 'Ws', 'Wv')}
    del _L2_gnn_all

    def _L3_gnn_setup():
        import jax, jax.numpy as jnp
        import numpy as np
        N = 1250
        E = 12500
        MUL0, MUL1 = (64, 32)
        RAD, HID = (8, 64)
        WNUM = 192
        NUM_NEIGHBORS = 10.0
        INV3 = 1.0 / np.sqrt(3.0)

        def _lin(s, v, Ws, Wv, attr):
            out_s = s @ Ws * attr * (1.0 / np.sqrt(Ws.shape[0]))
            out_v = jnp.einsum('nud,uv->nvd', v, Wv) * attr[..., None] * (1.0 / np.sqrt(Wv.shape[0]))
            return (out_s, out_v)
        key = jax.random.key(seed)
        ks = jax.random.split(key, 16)
        return {'node_input': jax.random.normal(ks[0], (N, MUL0 + 3 * MUL1), jnp.float32), 'node_attr': jnp.ones((N, 1), jnp.float32), 'edge_attr': jax.random.normal(ks[1], (E, 4), jnp.float32), 'edge_scalars': jax.random.uniform(ks[2], (E, RAD), jnp.float32), 'W_sc_s': jax.random.normal(ks[3], (MUL0, MUL0), jnp.float32), 'W_sc_v': jax.random.normal(ks[4], (MUL1, MUL1), jnp.float32), 'W1_s': jax.random.normal(ks[5], (MUL0, MUL0), jnp.float32), 'W1_v': jax.random.normal(ks[6], (MUL1, MUL1), jnp.float32), 'W2_s': jax.random.normal(ks[7], (MUL0 + MUL1, MUL0), jnp.float32), 'W2_v': jax.random.normal(ks[8], (MUL0 + MUL1, MUL1), jnp.float32), 'W3': jax.random.normal(ks[9], (MUL0 + MUL1, 1), jnp.float32), 'fcW1': jax.random.normal(ks[10], (RAD, HID), jnp.float32), 'fcW2': jax.random.normal(ks[11], (HID, WNUM), jnp.float32), 'edge_src': jax.random.randint(ks[12], (E,), 0, N, jnp.int32), 'edge_dst': jax.random.randint(ks[13], (E,), 0, N, jnp.int32)}
    _L3_gnn_all = _L3_gnn_setup()
    _L3_gnn_in = {k: v for k, v in _L3_gnn_all.items() if k in ('W_sc_s', 'W_sc_v', 'W1_s', 'W1_v', 'W2_s', 'W2_v', 'W3', 'fcW1', 'fcW2')}
    del _L3_gnn_all
    return {'x': x, 'src': src, 'dst': dst, 'edge_attr_10': edge_attr_10, 'edge_attr_3': edge_attr_3, 'edge_attr_4': edge_attr_4, 'edge_attr_64': edge_attr_64, 'edge_attr_8': edge_attr_8, 'node_vec1': node_vec1, 'L0_gnn_W_skip0': _L0_gnn_in['W_skip0'], 'L0_gnn_W_skip1': _L0_gnn_in['W_skip1'], 'L0_gnn_W_nl0': _L0_gnn_in['W_nl0'], 'L0_gnn_W_nl1': _L0_gnn_in['W_nl1'], 'L0_gnn_W_fc1': _L0_gnn_in['W_fc1'], 'L0_gnn_W_fc2': _L0_gnn_in['W_fc2'], 'L0_gnn_W_out_s': _L0_gnn_in['W_out_s'], 'L0_gnn_W_out_v': _L0_gnn_in['W_out_v'], 'L1_gnn_W_si0': _L1_gnn_in['W_si0'], 'L1_gnn_W_si1': _L1_gnn_in['W_si1'], 'L1_gnn_W_l1_0': _L1_gnn_in['W_l1_0'], 'L1_gnn_W_l1_1': _L1_gnn_in['W_l1_1'], 'L1_gnn_W_l2_00': _L1_gnn_in['W_l2_00'], 'L1_gnn_W_l2_10': _L1_gnn_in['W_l2_10'], 'L1_gnn_W_l2_01': _L1_gnn_in['W_l2_01'], 'L1_gnn_W_l2_11': _L1_gnn_in['W_l2_11'], 'L1_gnn_W_fc1': _L1_gnn_in['W_fc1'], 'L1_gnn_W_fc2': _L1_gnn_in['W_fc2'], 'L2_gnn_W1': _L2_gnn_in['W1'], 'L2_gnn_W2': _L2_gnn_in['W2'], 'L2_gnn_W3': _L2_gnn_in['W3'], 'L2_gnn_W4': _L2_gnn_in['W4'], 'L2_gnn_W5': _L2_gnn_in['W5'], 'L2_gnn_Ws': _L2_gnn_in['Ws'], 'L2_gnn_Wv': _L2_gnn_in['Wv'], 'L3_gnn_W_sc_s': _L3_gnn_in['W_sc_s'], 'L3_gnn_W_sc_v': _L3_gnn_in['W_sc_v'], 'L3_gnn_W1_s': _L3_gnn_in['W1_s'], 'L3_gnn_W1_v': _L3_gnn_in['W1_v'], 'L3_gnn_W2_s': _L3_gnn_in['W2_s'], 'L3_gnn_W2_v': _L3_gnn_in['W2_v'], 'L3_gnn_W3': _L3_gnn_in['W3'], 'L3_gnn_fcW1': _L3_gnn_in['fcW1'], 'L3_gnn_fcW2': _L3_gnn_in['fcW2']}

def reference(x, src, dst, edge_attr_10, edge_attr_3, edge_attr_4, edge_attr_64, edge_attr_8, node_vec1, L0_gnn_W_skip0, L0_gnn_W_skip1, L0_gnn_W_nl0, L0_gnn_W_nl1, L0_gnn_W_fc1, L0_gnn_W_fc2, L0_gnn_W_out_s, L0_gnn_W_out_v, L1_gnn_W_si0, L1_gnn_W_si1, L1_gnn_W_l1_0, L1_gnn_W_l1_1, L1_gnn_W_l2_00, L1_gnn_W_l2_10, L1_gnn_W_l2_01, L1_gnn_W_l2_11, L1_gnn_W_fc1, L1_gnn_W_fc2, L2_gnn_W1, L2_gnn_W2, L2_gnn_W3, L2_gnn_W4, L2_gnn_W5, L2_gnn_Ws, L2_gnn_Wv, L3_gnn_W_sc_s, L3_gnn_W_sc_v, L3_gnn_W1_s, L3_gnn_W1_v, L3_gnn_W2_s, L3_gnn_W2_v, L3_gnn_W3, L3_gnn_fcW1, L3_gnn_fcW2):
    import jax
    import jax.numpy as jnp

    def _L0_gnn_ref(node_feature, edge_attr, edge_feature, W_skip0, W_skip1, W_nl0, W_nl1, W_fc1, W_fc2, W_out_s, W_out_v, edge_index):
        import jax, jax.numpy as jnp
        import numpy as np
        N_NODES = 10000
        N_EDGES = 10000
        MUL0, MUL1 = (64, 32)
        EDGE_DIM = 64
        W_NUMEL = 224
        DENOM = 32.0
        SQRT3 = 3.0 ** 0.5
        INV_SQRT3 = 1.0 / SQRT3
        INV_SQRT2 = 2.0 ** (-0.5)

        def _forward(node_feature, edge_attr, edge_feature, W_skip0, W_skip1, W_nl0, W_nl1, W_fc1, W_fc2, W_out_s, W_out_v, edge_index):
            N = node_feature.shape[0]
            E = edge_attr.shape[0]
            s = node_feature[:, :MUL0]
            v = node_feature[:, MUL0:].reshape(N, MUL1, 3)
            skip_s = s @ W_skip0
            skip_v = jnp.einsum('nmi,mk->nki', v, W_skip1)
            s = s @ W_nl0
            v = jnp.einsum('nmi,mk->nki', v, W_nl1)
            rhat = edge_attr / jnp.linalg.norm(edge_attr, axis=-1, keepdims=True)
            sh1 = SQRT3 * rhat
            w = jax.nn.relu(edge_feature @ W_fc1) @ W_fc2
            w0, w1, w2, w3, w4 = jnp.split(w, [64, 128, 160, 192], axis=-1)
            src, dst = (edge_index[0], edge_index[1])
            xs = s[dst]
            xv = v[dst]
            out0a = w0 * xs
            out0b = w3 * (jnp.einsum('emi,ei->em', xv, sh1) * INV_SQRT3)
            out1a = (w1 * xs)[:, :, None] * sh1[:, None, :]
            out1b = w2[:, :, None] * xv
            out1c = w4[:, :, None] * (jnp.cross(xv, sh1[:, None, :]) * INV_SQRT2)
            tp = jnp.concatenate([out0a, out0b, out1a.reshape(E, -1), out1b.reshape(E, -1), out1c.reshape(E, -1)], axis=-1)
            agg = jax.ops.segment_sum(tp, src, num_segments=N) / DENOM
            agg_s = agg[:, :96]
            agg_v = agg[:, 96:].reshape(N, 128, 3)
            out_s = agg_s @ W_out_s + skip_s
            out_v = jnp.einsum('nmi,mk->nki', agg_v, W_out_v) + skip_v
            fs = jax.nn.silu(out_s[:, :MUL0])
            gate = jax.nn.sigmoid(out_s[:, MUL0:MUL0 + 32])
            gv = gate[:, :, None] * out_v
            return jnp.concatenate([fs, gv.reshape(N, -1)], axis=-1)
        return _forward(node_feature, edge_attr, edge_feature, W_skip0, W_skip1, W_nl0, W_nl1, W_fc1, W_fc2, W_out_s, W_out_v, edge_index)

    def _L1_gnn_ref(node_input, node_attr, edge_src, edge_dst, edge_attr, edge_length_embedded, W_si0, W_si1, W_l1_0, W_l1_1, W_l2_00, W_l2_10, W_l2_01, W_l2_11, W_fc1, W_fc2):
        import jax, jax.numpy as jnp
        import numpy as np
        N_NODES = 50000
        N_EDGES = 25000
        MUL0, MUL1 = (64, 32)
        N_BASIS, N_RADIAL = (10, 100)
        W_NUMEL = 192
        NUM_NEIGHBORS = 16.0
        INV_SQRT3 = np.float32(1.0 / np.sqrt(3.0))
        RELU_GAIN = np.float32(np.sqrt(2.0))
        FAN_L2 = np.float32(np.sqrt(MUL0 + MUL1))

        def _fctp_scalar_attr(x0, x1, a, W0, W1):
            o0 = x0 @ W0 * a * (1.0 / np.sqrt(W0.shape[0]))
            o1 = jnp.einsum('nud,uw->nwd', x1, W1) * a[..., None] * (1.0 / np.sqrt(W1.shape[0]))
            return (o0, o1)
        N = node_input.shape[0]
        x0 = node_input[:, :MUL0]
        x1 = node_input[:, MUL0:].reshape(N, MUL1, 3)
        a = node_attr
        h = jax.nn.relu(edge_length_embedded @ W_fc1 * (1.0 / np.sqrt(N_BASIS))) * RELU_GAIN
        w = h @ W_fc2 * (1.0 / np.sqrt(N_RADIAL))
        w0, w1, w2, w3 = (w[:, :64], w[:, 64:128], w[:, 128:160], w[:, 160:192])
        si0, si1 = _fctp_scalar_attr(x0, x1, a, W_si0, W_si1)
        l0, l1 = _fctp_scalar_attr(x0, x1, a, W_l1_0, W_l1_1)
        y0 = l0[edge_src]
        y1 = l1[edge_src]
        e0 = edge_attr[:, :1]
        e1 = edge_attr[:, 1:4]
        m0 = w0 * y0 * e0
        m1 = (w1 * y0)[:, :, None] * e1[:, None, :]
        m2 = (w2 * e0)[:, :, None] * y1
        m3 = w3 * jnp.einsum('eud,ed->eu', y1, e1) * INV_SQRT3
        inv = np.float32(1.0 / np.sqrt(NUM_NEIGHBORS))
        s0 = jax.ops.segment_sum(m0, edge_dst, num_segments=N) * inv
        s1 = jax.ops.segment_sum(m1, edge_dst, num_segments=N) * inv
        s2 = jax.ops.segment_sum(m2, edge_dst, num_segments=N) * inv
        s3 = jax.ops.segment_sum(m3, edge_dst, num_segments=N) * inv
        o0 = (s0 @ W_l2_00 + s3 @ W_l2_10) * a / FAN_L2
        o1 = (jnp.einsum('nud,uw->nwd', s1, W_l2_01) + jnp.einsum('nud,uw->nwd', s2, W_l2_11)) * a[..., None] / FAN_L2
        out0 = si0 + 0.5 * o0
        out1 = si1 + 0.5 * o1
        return jnp.concatenate([out0, out1.reshape(N, 3 * MUL1)], axis=1)

    def _L2_gnn_ref(x, sh, W1, W2, W3, W4, W5, Ws, Wv, edge_index):
        import jax, jax.numpy as jnp
        import numpy as np
        N, E = (50000, 25000)
        MUL0, MUL1 = (64, 32)
        D = MUL0 + 3 * MUL1
        INV3 = float(1.0 / np.sqrt(3.0))
        INV6 = float(1.0 / np.sqrt(6.0))
        C0 = float(1.0 / np.sqrt(MUL0 + MUL1))
        C1 = float(np.sqrt(3.0 / (MUL0 + 2 * MUL1)))
        LIN_S = float(1.0 / np.sqrt(MUL0))
        LIN_V = float(1.0 / np.sqrt(MUL1))
        n = x.shape[0]
        src, dst = (edge_index[0], edge_index[1])
        s = x[:, :MUL0]
        v = x[:, MUL0:].reshape(n, MUL1, 3)
        ss, vv = (s[src], v[src])
        e0 = sh[:, 0:1]
        e1 = sh[:, 1:4]
        dot = jnp.einsum('eui,ei->eu', vv, e1)
        out0 = C0 * (ss * e0 @ W1 + dot * INV3 @ W2)
        p3 = (ss @ W3)[:, :, None] * e1[:, None, :] * INV3
        p4 = jnp.einsum('eui,uw->ewi', vv * e0[:, :, None], W4) * INV3
        p5 = jnp.einsum('eui,uw->ewi', jnp.cross(vv, e1[:, None, :]), W5) * INV6
        out1 = C1 * (p3 + p4 + p5)
        m = jnp.concatenate([out0, out1.reshape(-1, 3 * MUL1)], axis=1)
        m_agg = jax.ops.segment_sum(m, dst, num_segments=n)
        hs = m_agg[:, :MUL0] @ Ws * LIN_S
        hv = jnp.einsum('nui,uw->nwi', m_agg[:, MUL0:].reshape(n, MUL1, 3), Wv) * LIN_V
        h = jnp.concatenate([hs, hv.reshape(n, 3 * MUL1)], axis=1)
        return x + jax.nn.relu(h)

    def _L3_gnn_ref(node_input, node_attr, edge_attr, edge_scalars, W_sc_s, W_sc_v, W1_s, W1_v, W2_s, W2_v, W3, fcW1, fcW2, edge_src, edge_dst):
        import jax, jax.numpy as jnp
        import numpy as np
        N = 1250
        E = 12500
        MUL0, MUL1 = (64, 32)
        RAD, HID = (8, 64)
        WNUM = 192
        NUM_NEIGHBORS = 10.0
        INV3 = 1.0 / np.sqrt(3.0)

        def _lin(s, v, Ws, Wv, attr):
            out_s = s @ Ws * attr * (1.0 / np.sqrt(Ws.shape[0]))
            out_v = jnp.einsum('nud,uv->nvd', v, Wv) * attr[..., None] * (1.0 / np.sqrt(Wv.shape[0]))
            return (out_s, out_v)
        n = node_input.shape[0]
        s_in = node_input[:, :MUL0]
        v_in = node_input[:, MUL0:].reshape(n, MUL1, 3)
        sc_s, sc_v = _lin(s_in, v_in, W_sc_s, W_sc_v, node_attr)
        f_s, f_v = _lin(s_in, v_in, W1_s, W1_v, node_attr)
        h = jax.nn.silu(edge_scalars @ fcW1 * (1.0 / np.sqrt(RAD)))
        w = h @ fcW2 * (1.0 / np.sqrt(HID))
        wA, wB, wC, wD = (w[:, :64], w[:, 64:128], w[:, 128:160], w[:, 160:192])
        xs = f_s[edge_src]
        xv = f_v[edge_src]
        y0 = edge_attr[:, :1]
        y1 = edge_attr[:, 1:4]
        outA = wA * xs * y0
        outD = wD * jnp.einsum('eud,ed->eu', xv, y1) * INV3
        outB = wB[:, :, None] * xs[:, :, None] * y1[:, None, :]
        outC = wC[:, :, None] * xv * y0[:, :, None]
        edge_feat = jnp.concatenate([outA, outD, outB.reshape(-1, MUL0 * 3), outC.reshape(-1, MUL1 * 3)], axis=1)
        agg = jax.ops.segment_sum(edge_feat, edge_dst, num_segments=n)
        agg = agg * (1.0 / np.sqrt(NUM_NEIGHBORS))
        ms = agg[:, :MUL0 + MUL1]
        mv = agg[:, MUL0 + MUL1:].reshape(n, MUL0 + MUL1, 3)
        c_s, c_v = _lin(ms, mv, W2_s, W2_v, node_attr)
        conv = jnp.concatenate([c_s, c_v.reshape(n, -1)], axis=1)
        sc = jnp.concatenate([sc_s, sc_v.reshape(n, -1)], axis=1)
        angle = 0.1 * (ms @ W3) * node_attr * (1.0 / np.sqrt(MUL0 + MUL1))
        cos, sin = (jnp.cos(angle), jnp.sin(angle))
        return cos * sc + sin * conv
    edge_index = jnp.stack([src, dst])
    h = jnp.maximum(_layernorm(x, axis=-1), 0.0)
    x = x + _L0_gnn_ref(h, edge_attr_3, edge_attr_64, L0_gnn_W_skip0, L0_gnn_W_skip1, L0_gnn_W_nl0, L0_gnn_W_nl1, L0_gnn_W_fc1, L0_gnn_W_fc2, L0_gnn_W_out_s, L0_gnn_W_out_v, edge_index)
    h = jnp.maximum(_layernorm(x, axis=-1), 0.0)
    x = x + _L1_gnn_ref(h, node_vec1, src, dst, edge_attr_4, edge_attr_10, L1_gnn_W_si0, L1_gnn_W_si1, L1_gnn_W_l1_0, L1_gnn_W_l1_1, L1_gnn_W_l2_00, L1_gnn_W_l2_10, L1_gnn_W_l2_01, L1_gnn_W_l2_11, L1_gnn_W_fc1, L1_gnn_W_fc2)
    h = jnp.maximum(_layernorm(x, axis=-1), 0.0)
    x = x + _L2_gnn_ref(h, edge_attr_4, L2_gnn_W1, L2_gnn_W2, L2_gnn_W3, L2_gnn_W4, L2_gnn_W5, L2_gnn_Ws, L2_gnn_Wv, edge_index)
    h = jnp.maximum(_layernorm(x, axis=-1), 0.0)
    x = x + _L3_gnn_ref(h, node_vec1, edge_attr_4, edge_attr_8, L3_gnn_W_sc_s, L3_gnn_W_sc_v, L3_gnn_W1_s, L3_gnn_W1_v, L3_gnn_W2_s, L3_gnn_W2_v, L3_gnn_W3, L3_gnn_fcW1, L3_gnn_fcW2, src, dst)
    return x

_drawn_inputs = setup_inputs


def setup_inputs(seed=0):
    import zlib

    import numpy as np

    out = dict(_drawn_inputs(seed))
    spreads = {}
    factors = {}
    for name, (base, spread) in spreads.items():
        noise = np.random.default_rng([zlib.crc32(name.encode()), seed]).standard_normal(out[name].shape)
        drawn = base * np.exp(spread * noise) if base else spread * noise
        out[name] = jnp.asarray(drawn.astype(out[name].dtype))
    for name, factor in factors.items():
        out[name] = (out[name] * factor).astype(out[name].dtype)
    return out
```

```python
import math
from contextlib import ExitStack

import concourse.bass as bass
from concourse import mybir

F32 = mybir.dt.float32
I32 = mybir.dt.int32
I16 = mybir.dt.int16
BF16 = mybir.dt.bfloat16
ALU = mybir.AluOpType
ACT = mybir.ActivationFunctionType
AX_X = mybir.AxisListType.X
DVE = mybir.EngineType.DVE

P = 128
NODES, EDGES = 3125, 100000
S0, V1 = 64, 32
NF = S0 + 3 * V1
BLOCKS = -(-NODES // P)
NPAD = BLOCKS * P
BIN = 32
BINS = NPAD // BIN
PAD_NODE = -(-NODES // BIN) * BIN
COLS = -(-EDGES // P)
GT = 8
FULL_BINS = PAD_NODE // BIN
MAX_TILES = (EDGES + FULL_BINS * (P - 1)) // P + 1
GROUPS = -(-MAX_TILES // GT)
TILES = GROUPS * GT
SLOTS = TILES * P
CHUNK = 23
CHUNKS = COLS // CHUNK
TCOLS = -(-TILES // P)
LAG_SC, LAG_FL = 2, 4
RING = 4

A_EF, A_SH, A_IDX, A_KEY, A_W = 0, 64, 67, 68, 69
B_10, B_8, B_4, B_IDX, B_KEY, B_W = 0, 10, 18, 22, 23, 32

N_SCALED = 10 + 3
EPS = 1e-5
R2, R3 = math.sqrt(2.0), math.sqrt(3.0)
assert COLS % CHUNK == 0 and CHUNKS % 2 == 0 and GROUPS % 2 == 0


def is_static(v):
    return isinstance(v, int)


def within(v, n):
    return not is_static(v) or 0 <= v < n


class Signal:

    def __init__(self, sem, base):
        self.sem, self.base = sem, base


def wait(eng, signal, value):
    if is_static(value) and value <= 0:
        return
    if isinstance(signal, Signal):
        eng.wait_ge(signal.sem, value + signal.base)
    else:
        eng.wait_ge(signal, value)


def pipeline(eng, n, first, last, extra, body):
    for s in range(first):
        body(s, s // 2, s % 2)
    assert (n - first - last) % 2 == 0
    with eng.Fori(0, (n - first - last) // 2) as i:
        for u in range(first, first + 2):
            body(i * 2 + u, i + u // 2, u % 2)
    for s in range(n - last, n + extra):
        body(s, s // 2, s % 2)


class Layer:

    def __init__(self, n):
        self.n = n
        self.rowsA = n == 0
        self.mlp = n != 2
        self.width = 256 if n == 0 else 160
        self.wcols = 224 if n == 0 else 192
        self.chunks = [(0, 128), (128, 256)] if n == 0 else [(0, 64), (64, 160)]
        self.out = {0: 192, 1: 160, 2: 160, 3: 161}[n]
        self.tab_side = 96 if n == 0 else 64


LAYERS = [Layer(n) for n in range(4)]


def sum_weights(n):
    put = []
    if n == 0:
        put.append(("L0_gnn_W_out_s", 0, 64, 0, 0, 0, 0, 1.0))
        for i in range(3):
            put.append(("L0_gnn_W_out_v", 64, 96, 0 if i < 2 else 1, 0, (64, 96, 0)[i], 96 + 32 * i, 1.0))
            put.append(("L0_gnn_W_out_s", 64, 96, 0, 1 + i, 32 * i, 0, 1.0))
            put.append(("L0_gnn_W_out_v", 0, 64, 1, 1 + i, 64, 96 + 32 * i, 1.0))
            for j in range(3):
                if j != i:
                    sign = 1.0 if i == (j + 1) % 3 else -1.0
                    put.append(("L0_gnn_W_out_v", 96, 128, 0 if j == 0 else 1, 1 + i, (96, 0, 32)[j],
                                96 + 32 * (3 - i - j), sign))
        return put
    if n == 2:
        put.append(("L2_gnn_W1", 0, 64, 0, 0, 0, 0, 1.0))
        for i in range(3):
            put.append(("L2_gnn_W4", 0, 32, 1, 0, 32 * i, 64 + 32 * i, 1.0))
            put.append(("L2_gnn_W3", 0, 64, 0, 1 + i, 0, 64 + 32 * i, 1.0))
            put.append(("L2_gnn_W2", 0, 32, 1, 1 + i, 32 * i, 0, 1.0 / R3))
            for j in range(3):
                if j != i:
                    sign = 1.0 if i == (j + 1) % 3 else -1.0
                    put.append(("L2_gnn_W5", 0, 32, 1, 1 + i, 32 * j, 64 + 32 * (3 - i - j), sign / R2))
        return put
    if n == 1:
        ws, wv, o = (("L1_gnn_W_l2_00", 0), ("L1_gnn_W_l2_10", 0)), (("L1_gnn_W_l2_01", 0), ("L1_gnn_W_l2_11", 0)), 0
    else:
        ws, wv, o = (("L3_gnn_W2_s", 0), ("L3_gnn_W2_s", 64)), (("L3_gnn_W2_v", 0), ("L3_gnn_W2_v", 64)), 1
        put.append(("L3_gnn_W3", 0, 64, 0, 0, 0, 0, 1.0))
    put.append((ws[0][0], 0, 64, 0, 0, 0, o, 1.0))
    for i in range(3):
        put.append((wv[1][0], wv[1][1], wv[1][1] + 32, 1, 0, 32 * i, o + 64 + 32 * i, 1.0))
        put.append((wv[0][0], 0, 64, 0, 1 + i, 0, o + 64 + 32 * i, 1.0))
        put.append((ws[1][0], ws[1][1], ws[1][1] + 32, 1, 1 + i, 32 * i, o, 1.0))
        if n == 3:
            put.append(("L3_gnn_W3", 64, 96, 1, 1 + i, 32 * i, 0, 1.0))
    return put


def sum_products(n):
    if n == 0:
        return ([(0, 0, 128, 0, 192), (1, 0, 32, 160, 192)] + [(0, k, 128, 0, 192) for k in (1, 2, 3)]
                + [(1, k, 128, 96, 192) for k in (1, 2, 3)])
    o = 1 if n == 3 else 0
    return ([(0, 0, 64, 0, o + 64)] + [(0, k, 64, o + 32 + 32 * k, o + 64 + 32 * k) for k in (1, 2, 3)]
            + [(1, 0, 96, o + 64, o + 160)] + [(1, k, 96, 0, o + 64) for k in (1, 2, 3)])


def gnn_program(nc, t):
    ctx = ExitStack()
    with ctx:
        def sb(name, shape, dt=F32):
            return ctx.enter_context(nc.sbuf_tensor(name, shape, dt))

        def sem(name):
            return ctx.enter_context(nc.semaphore(name))

        rows_dram = [nc.dram_tensor("rows_a", (SLOTS, A_W), F32).ap(), nc.dram_tensor("rows_b", (SLOTS, B_W), F32).ap()]
        table_dram = [nc.dram_tensor(f"table_{n}", (NPAD, NF), F32).ap() for n in range(4)]
        bins_dram = [nc.dram_tensor(f"tile_bins_{o}", (TCOLS * P,), I32).ap() for o in range(2)]

        x = sb("x", [P, BLOCKS * NF])
        attr = sb("attr", [P, BLOCKS])
        side = sb("side", [P, BLOCKS * 192])
        acc = sb("acc", [P, BINS * 256])
        ident = sb("ident", [P, P])
        iota_bin = sb("iota_bin", [P, BIN])
        iota_bins = sb("iota_bins", [P, BINS])
        tile_bins = sb("tile_bins_row", [1, RING + TCOLS * P], I32)
        w1 = {0: sb("w1_0", [P, P]), 1: sb("w1_1", [P, 4, 100]), 3: sb("w1_3", [P, 2, P])}
        w2 = {0: sb("w2_0", [P, 2, 224]), 1: sb("w2_1", [P, 192]), 3: sb("w2_3", [P, 2, 192])}
        wsum = {0: sb("wsum_0", [P, 2, 4, LAYERS[0].out])}
        tail = BINS * 256
        for n in (1, 2, 3):
            tail -= 8 * LAYERS[n].out
            wsum[n] = acc[:, tail:tail + 8 * LAYERS[n].out].rearrange("p (c k o) -> p c k o", c=2, k=4)
        assert tail >= BINS * LAYERS[1].width
        wps = {n: sb(f"wps_{n}", [S0, 2 * S0 if n else S0 + 96]) for n in (0, 1, 3)}
        wpv = {n: sb(f"wpv_{n}", [96, 192]) for n in (0, 1, 3)}
        w2s, w2v = sb("w2s", [S0, S0]), sb("w2v", [96, 96])
        rows = [sb(f"rows_{q}", [P, GT, A_W]) for q in range(2)]
        gath = [sb(f"gath_{q}", [P, GT, NF]) for q in range(2)]
        sel = [sb(f"sel_{q}", [P, GT, 224]) for q in range(2)]
        onehot = sb("onehot", [P, GT, BIN])
        prod = sb("prod", [P, 3 * 416 + 704])
        attrT = sb("attrT", [P, 512])
        hidT = [sb(f"hidT_{q}", [P, 1024]) for q in range(2)]
        stg = [sel[q][:, :, :].rearrange("p t c -> p (t c)")[:, 0:4 * 256] for q in range(2)]
        sumT = [gath[q][:, :, :].rearrange("p t c -> p (t c)")[:, 0:1024].rearrange("p (c m) -> p c m", c=2) for q in range(2)]
        tmp, hbuf, trow, hT = ([prod[:, 768 * q + a:768 * q + b] for q in range(2)]
                               for a, b in ((0, 192), (192, 352), (352, 512), (512, 768)))
        stats = sb("stats", [P, BLOCKS, 6])
        small = sb("small", [P, 12, BLOCKS])

        pb = [ctx.enter_context(nc.psum_tensor(f"bank_{i}", [P, 512], F32)) for i in range(6)]
        wide = ctx.enter_context(nc.psum_tensor("bank_67", [P, 1024], F32))
        pb += [wide[:, 0:512], wide[:, 512:1024]]

        def bank(i, p, a, b):
            return pb[i][0:p, a:b]

        used = [0]

        def carve(words):
            a = used[0]
            used[0] += words
            assert used[0] <= BINS * 256
            return acc[:, a:a + words]

        even = COLS + COLS % 2
        key_i = [carve(COLS).bitcast(I32) for _ in range(2)]
        key_f = [carve(COLS) for _ in range(2)]
        pos_f = carve(COLS)
        pos_i = [carve(COLS).bitcast(I32) for _ in range(2)]
        int_a, int_b = carve(COLS).bitcast(I32), carve(COLS).bitcast(I32)
        bin_h = carve(even // 2).bitcast(BF16)[:, 0:COLS]
        eq = carve(even // 2).bitcast(I16)[:, 0:COLS]
        zero_h = carve(even // 2).bitcast(I16)[:, 0:COLS]
        sh = carve(3 * COLS)
        sh2 = carve(3 * COLS)
        norm = carve(COLS)
        tri, ones = carve(P), carve(P)
        count, base, ntile, first_tile, bins_f, bins_z = (carve(BINS) for _ in range(6))
        bins_i = carve(BINS).bitcast(I32)
        tile_id, tile_bin = carve(TCOLS), carve(TCOLS)
        tile_bin_i = carve(TCOLS).bitcast(I32)
        stage = [[carve(CHUNK * w) for _ in range(2)] for w in (A_W, B_W)]
        pos_r = [carve(CHUNK).bitcast(I32) for _ in range(2)]
        blank = [carve(GT * w) for w in (A_W, B_W)]

        s_in = sem("s_in")
        s_nodes = sem("s_nodes")
        s_wz = sem("s_wz")
        s_w = sem("s_w")
        s_wf = sem("s_wf")
        s_const = sem("s_const")
        s_cz = sem("s_cz")
        s_blank = sem("s_blank")
        s_init = sem("s_init")
        s_lz = sem("s_lz")
        s_lw = sem("s_lw")
        s_lf = sem("s_lf")
        s_bz = sem("s_bz")
        s_chain = sem("s_chain")
        s_sq = sem("s_sq")
        s_rt = sem("s_rt")
        s_cnt = [sem(f"s_cnt{o}") for o in range(2)]
        s_cum = [sem(f"s_cum{o}") for o in range(2)]
        s_eq = [sem(f"s_eq{o}") for o in range(2)]
        s_scan = [sem(f"s_scan{o}") for o in range(2)]
        s_pick = [sem(f"s_pick{o}") for o in range(2)]
        s_tb = [sem(f"s_tb{o}") for o in range(2)]
        s_tbd = [sem(f"s_tbd{o}") for o in range(2)]
        s_tbs = [sem(f"s_tbs{o}") for o in range(2)]
        s_pos = [sem(f"s_pos{o}") for o in range(2)]
        s_stage = [[sem(f"s_stage{o}{q}") for q in range(2)] for o in range(2)]
        s_fill = [sem(f"s_fill{o}") for o in range(2)]
        s_scat = [[sem(f"s_scat{o}{q}") for q in range(2)] for o in range(2)]

        def signals(names, n):
            return {k: Signal(sem(f"s_{k}_{n}"), 0) for k in names.split()}

        s_p = [signals("stat var root rstd h side td0 td1" + (" ht hts htv m tab" if n != 2 else ""), n)
               for n in range(4)]
        s_e = [signals("rows0 rows1 ga0 ga1 zero" + (" tr tc m1 hid w prod" if n != 2 else ""), n) for n in range(4)]
        s_c = [signals({0: "t1 sig t2", 2: "ms mv fin"}.get(n, ""), n) for n in range(4)]
        for names, where, each in (("oh sel", s_e, GROUPS), ("sc fl", s_e, TILES), ("stg trn ca cd big ev", s_c, BLOCKS)):
            for k in names.split():
                shared = sem(f"s_{k}")
                for n in range(4):
                    where[n][k] = Signal(shared, each * n)
        s_apart = {e: sem(f"s_apart_{e}") for e in ("pool", "pe", "dve", "sp")}
        s_fin = sem("s_fin")
        s_trig = sem("s_trig")
        s_out = sem("s_out")

        loads = []
        for half in range(2):
            loads.append((w1[0][64 * half:64 * half + 64, 64 * half:64 * half + 64], t["L0_gnn_W_fc1"]))
            loads.append((w2[0][64 * half:64 * half + 64, half, :], t["L0_gnn_W_fc2"]))
            loads.append((w2[3][64 * half:64 * half + 64, half, :], t["L3_gnn_fcW2"]))
        for i in range(4):
            loads.append((w1[1][32 * i + B_10:32 * i + B_10 + 10, i, :], t["L1_gnn_W_fc1"]))
            loads.append((w1[3][32 * i + B_8:32 * i + B_8 + 8, i // 2, 64 * (i % 2):64 * (i % 2) + 64], t["L3_gnn_fcW1"]))
        loads.append((w2[1][0:100, :], t["L1_gnn_W_fc2"]))
        late = []
        for n in range(4):
            for name, a, b, c, k, r, col, _factor in sum_weights(n):
                (late if n else loads).append((wsum[n][r:r + b - a, c, k, col:col + t[name].shape[1]], t[name][a:b, :]))
        for n, (ts, tv, ks, kv) in {0: ("L0_gnn_W_nl0", "L0_gnn_W_nl1", "L0_gnn_W_skip0", "L0_gnn_W_skip1"),
                                    1: ("L1_gnn_W_l1_0", "L1_gnn_W_l1_1", "L1_gnn_W_si0", "L1_gnn_W_si1"),
                                    3: ("L3_gnn_W1_s", "L3_gnn_W1_v", "L3_gnn_W_sc_s", "L3_gnn_W_sc_v")}.items():
            loads.append((wps[n][:, 0:64], t[ts]))
            loads.append((wps[n][:, 64:64 + LAYERS[n].tab_side], t[ks]))
            for i in range(3):
                loads.append((wpv[n][32 * i:32 * i + 32, 32 * i:32 * i + 32], t[tv]))
                loads.append((wpv[n][32 * i:32 * i + 32, 96 + 32 * i:128 + 32 * i], t[kv]))
        loads.append((w2s[:, :], t["L2_gnn_Ws"]))
        for i in range(3):
            loads.append((w2v[32 * i:32 * i + 32, 32 * i:32 * i + 32], t["L2_gnn_Wv"]))

        def sum_factors(n):
            return [(wsum[n][r:r + b - a, c, k, col:col + t[name].shape[1]], f)
                    for name, a, b, c, k, r, col, f in sum_weights(n) if f != 1.0]

        def by_bin(a):
            return a.rearrange("p (b k m) -> p k b m", b=4, k=4)

        def by_kind(a):
            return a.rearrange("p (k b m) -> p k b m", b=4, k=4)

        def rows_a(q):
            flat = rows[q][:, :, :].rearrange("p t c -> p (t c)")
            return flat[:, 0:GT * 64], flat[:, GT * 64:GT * A_W].rearrange("p (t c) -> p t c", t=GT)

        def rows_b(q):
            return rows[q][:, :, :].rearrange("p t c -> p (t c)")[:, 0:GT * B_W]

        def scratch(i):
            return small[:, i, :]

        RSTD, NMR = 0, 1

        def xj(j, n=1):
            return x[:, bass.ds(j * NF, n * NF)]

        def sj(j):
            return side[:, bass.ds(j * 192, 192)]

        block = ctx.enter_context(nc.Block())

        @block.sync
        def _(sp):
            sp.dma_start(key_i[0], t["skey"]).then_inc(s_in, 16)
            sp.dma_start(key_i[1], t["dkey"]).then_inc(s_in, 16)
            sp.dma_start(sh, t["edge_attr_3"]).then_inc(s_in, 16)
            sp.dma_start(x[:, :].rearrange("p (j c) -> p j c", j=BLOCKS),
                         t["x"].rearrange("(j p) c -> p j c", p=P)).then_inc(s_nodes, 16)
            with nc.allow_non_contiguous_dma(reason="one word per node"):
                sp.dma_start(attr[:, :], t["node_vec1"].rearrange("(j p) c -> p (j c)", p=P)).then_inc(s_nodes, 16)
            sp.wait_ge(s_blank, 4)
            for o, w in enumerate((A_W, B_W)):
                sp.dma_start(rows_dram[o].rearrange("(g p t) c -> p g (t c)", p=P, t=GT),
                             blank[o].unsqueeze(1).to_broadcast([P, GROUPS, GT * w])).then_inc(s_init, 16)
            sp.wait_ge(s_wz, 1)
            for dst, src in loads:
                sp.dma_start(dst, src).then_inc(s_w, 16)

            def tables(n):
                S = s_p[n]

                def body(j, half, q):
                    if n == 2:
                        wait(sp, S["h"], j + 1)
                    else:
                        wait(sp, S["tab"], j + 1)
                    sp.sem_inc(s_apart["sp"], 1)
                    src = hbuf[q] if n == 2 else trow[q]
                    sp.dma_start(table_dram[n].rearrange("(j p) c -> p j c", p=P)[:, bass.ds(j, 1), :],
                                 src[:, :].unsqueeze(1)).then_inc(S[f"td{q}"].sem, 16)
                pipeline(sp, BLOCKS, 3, 0, 0, body)

            def bins_out(o):
                sp.wait_ge(s_tb[o], 1)
                with nc.allow_non_contiguous_dma(reason="one word per tile"):
                    sp.dma_start(bins_dram[o].rearrange("(c p) -> p c", p=P), tile_bin_i).then_inc(s_tbd[o], 16)
                sp.wait_ge(s_tbd[o], 16)

            def bins_in(o):
                if o:
                    wait(sp, s_e[0]["fl"], TILES)
                sp.wait_ge(s_bz, 1)
                sp.dma_start(tile_bins[0:1, RING:], bins_dram[o].rearrange("(a c) -> a c", a=1)).then_inc(s_tbs[o], 16)

            def stage_rows(o):
                w = (A_W, B_W)[o]
                src = t[("rows_a", "rows_b")[o]]

                def body(c, half, q):
                    wait(sp, s_scat[o][q], half * (16 * CHUNK))
                    sp.sem_inc(s_apart["sp"], 1)
                    sp.dma_start(stage[o][q], src[:, bass.ds(c * (CHUNK * w), CHUNK * w)]).then_inc(s_stage[o][q], 16)
                pipeline(sp, CHUNKS, 2, 0, 0, body)

            def edge_rows(n):
                S, L = s_e[n], LAYERS[n]
                o, w = (0, A_W) if L.rowsA else (1, B_W)
                if n == 0:
                    for o_ in range(2):
                        for q in range(2):
                            sp.wait_ge(s_scat[o_][q], 16 * CHUNK * (CHUNKS // 2))
                src = rows_dram[o].rearrange("(g p t) c -> p g (t c)", p=P, t=GT)

                def body(g, half, q):
                    wait(sp, S[f"ga{q}"], half * (16 * GT))
                    sp.sem_inc(s_apart["sp"], 1)
                    wait(sp, S["sel"], g - 1)
                    sp.sem_inc(s_apart["sp"], 1)
                    if L.mlp:
                        wait(sp, S["tr"], g - 1)
                    sp.sem_inc(s_apart["sp"], 1)
                    if L.rowsA:
                        one = src[:, bass.ds(g, 1), :].rearrange("p g (t c) -> p (g t) c", t=GT)
                        ef, rest = rows_a(q)
                        sp.dma_start(ef.rearrange("p (t c) -> p t c", t=GT), one[:, :, 0:A_SH]).then_inc(S[f"rows{q}"].sem, 16)
                        sp.dma_start(rest, one[:, :, A_SH:A_W]).then_inc(S[f"rows{q}"].sem, 16)
                    else:
                        sp.dma_start(rows_b(q).unsqueeze(1), src[:, bass.ds(g, 1), :]).then_inc(S[f"rows{q}"].sem, 16)
                if n:
                    wait(sp, s_e[n - 1]["sel"], GROUPS)
                    wait(sp, s_e[n - 1]["ga0"], 16 * GT * (GROUPS // 2))
                    wait(sp, s_e[n - 1]["ga1"], 16 * GT * (GROUPS // 2))
                    if LAYERS[n - 1].mlp:
                        wait(sp, s_e[n - 1]["tr"], GROUPS)
                pipeline(sp, GROUPS, 2, 0, 0, body)

            tables(0)
            bins_out(0)
            stage_rows(0)
            bins_out(1)
            stage_rows(1)
            bins_in(0)
            edge_rows(0)
            bins_in(1)
            sp.wait_ge(s_lz, 1)
            for dst, src in late:
                sp.dma_start(dst, src).then_inc(s_lw, 16)
            for n in range(1, 4):
                tables(n)
                edge_rows(n)
            sp.wait_ge(s_fin, 1)
            sp.dma_start(t["out"].rearrange("(j p) c -> p j c", p=P),
                         x[:, :].rearrange("p (j c) -> p j c", j=BLOCKS)).then_inc(s_out, 16)
            sp.wait_ge(s_out, 16)
            for n in range(4):
                for q in range(2):
                    wait(sp, s_p[n][f"td{q}"], 16 * ((BLOCKS + 1 - q) // 2))

        @block.gpsimd
        def _(pool):
            for o, w in enumerate((A_W, B_W)):
                pool.memset(blank[o], 0.0).then_inc(s_blank, 1)
            pool.wait_ge(s_blank, 2)
            for o, (w, k) in enumerate(((A_W, A_KEY), (B_W, B_KEY))):
                pool.memset(blank[o].rearrange("p (t c) -> p t c", t=GT)[:, :, k:k + 1], -1.0).then_inc(s_blank, 1)
            pool.memset(ident[:, :], 0.0).then_inc(s_cz, 1)
            pool.memset(tri, 1.0).then_inc(s_cz, 1)
            pool.memset(ones, 1.0)
            pool.memset(bins_z, 0.0)
            pool.memset(zero_h, 0)
            pool.iota(iota_bin[:, :], pattern=[[1, BIN]], base=0, channel_multiplier=0,
                      allow_small_or_imprecise_dtypes=True)
            pool.iota(iota_bins[:, :], pattern=[[1, BINS]], base=0, channel_multiplier=0,
                      allow_small_or_imprecise_dtypes=True)
            pool.iota(tile_id, pattern=[[P, TCOLS]], base=0, channel_multiplier=1,
                      allow_small_or_imprecise_dtypes=True)
            pool.wait_ge(s_cz, 2)
            pool.affine_select(out=ident[:, :], in_=ident[:, :], compare_op=ALU.not_equal, fill=1.0, base=0,
                               pattern=[[-1, P]], channel_multiplier=1)
            pool.affine_select(out=tri, in_=tri, compare_op=ALU.is_gt, fill=0.0, base=0,
                               pattern=[[1, P]], channel_multiplier=-1).then_inc(s_const, 1)
            pool.memset(tile_bins[:, :], 0).then_inc(s_bz, 1)
            for ws in (w1, w2, wps, wpv):
                for m in ws.values():
                    pool.memset(m[...], 0.0)
            pool.memset(wsum[0][...], 0.0)
            pool.memset(w2v[:, :], 0.0).then_inc(s_wz, 1)
            pool.wait_ge(s_w, 16 * len(loads))
            fac = [(w2[0][:, :, 64:128], R3), (w2[0][:, :, 192:224], R3 / R2),
                   (w2[1][:, 0:160], 0.1), (w2[1][:, 160:192], 0.1 / R3),
                   (w2[3][:, :, 0:160], 1 / 8), (w2[3][:, :, 160:192], 1 / 8 / R3),
                   (wps[1][:, :], 1 / 8), (wps[3][:, :], 1 / 8),
                   (wpv[1][:, :], 1 / math.sqrt(32)), (wpv[3][:, :], 1 / math.sqrt(32))]
            assert len(fac) + len(sum_factors(0)) == N_SCALED
            for i, (m, f) in enumerate(fac + sum_factors(0)):
                wait(pool, s_wf, i)
                pool.tensor_scalar(m, m, f, None, ALU.mult).then_inc(s_wf, 1)

            pool.wait_ge(s_init, 32)
            for o, w in enumerate((A_W, B_W)):
                def body(c, half, q, o=o, w=w):
                    pool.wait_ge(s_fill[o], c * (4 if o == 0 else 3) + (4 if o == 0 else 3))
                    pool.sem_inc(s_apart["pool"], 1)
                    for u in range(CHUNK):
                        pool.indirect_dma_start(
                            rows_dram[o][:, :], bass.IndirectOffsetOnAxis(ap=pos_r[q][:, u:u + 1], axis=0),
                            stage[o][q][:, u * w:(u + 1) * w], None).then_inc(s_scat[o][q], 16)
                pipeline(pool, CHUNKS, 2, 0, 0, body)
            for o in range(2):
                for q in range(2):
                    pool.wait_ge(s_scat[o][q], 16 * CHUNK * (CHUNKS // 2))

            for n in range(4):
                L, S = LAYERS[n], s_e[n]
                if n:
                    wait(pool, s_c[n - 1]["stg"], BLOCKS)
                else:
                    pool.wait_ge(s_tbd[0], 16)
                    pool.wait_ge(s_tbd[1], 16)
                pool.memset(acc[:, 0:BINS * L.width], 0.0).then_inc(S["zero"].sem, 1)
                if n == 1:
                    pool.memset(acc[:, tail:], 0.0).then_inc(s_lz, 1)
                for q in range(2):
                    wait(pool, s_p[n][f"td{q}"], 16 * ((BLOCKS + 1 - q) // 2))
                if n:
                    wait(pool, s_e[n - 1]["sc"], TILES)

                def body(g, half, q, n=n, L=L, S=S):
                    wait(pool, S[f"rows{q}"], (half + 1) * (32 if n == 0 else 16))
                    wait(pool, S["prod"] if L.mlp else S["sc"], (g - 1) * GT)
                    pool.sem_inc(s_apart["pool"], 1)
                    first, w = (GT * 64 + A_IDX - A_SH, A_W - A_SH) if L.rowsA else (B_IDX, B_W)
                    flat = rows[q][:, :, :].rearrange("p t c -> p (t c)")
                    for u in range(GT):
                        pool.indirect_dma_start(
                            gath[q][:, u, :], None, table_dram[n][:, :],
                            bass.IndirectOffsetOnAxis(ap=flat[:, u * w + first:u * w + first + 1].bitcast(I32), axis=0)).then_inc(S[f"ga{q}"].sem, 16)
                pipeline(pool, GROUPS, 2, 0, 0, body)

                C = s_c[n]
                wait(pool, S["fl"], TILES)
                w4 = 4 * L.width

                def stage_sums(j, half, q, C=C, w4=w4):
                    wait(pool, C["trn"], j - 1)
                    pool.sem_inc(s_apart["pool"], 1)
                    pool.tensor_copy(stg[q][:, 0:w4], acc[:, bass.ds(j * w4, w4)]).then_inc(C["stg"].sem, 1)
                pipeline(pool, BLOCKS, 3, 2, 0, stage_sums)

        @block.scalar
        def _(act):
            act.wait_ge(s_sq, 1)
            act.activation(norm, norm, ACT.Sqrt).then_inc(s_rt, 1)
            act.wait_ge(s_nodes, 32)

            def prep(n):
                S = s_p[n]
                wait(act, S["var"], 1)
                act.activation(scratch(4), scratch(4), ACT.Sqrt).then_inc(S["root"].sem, 1)
                wait(act, S["rstd"], 1)

                def body(j, half, q):
                    if within(j, BLOCKS):
                        if n == 2:
                            wait(act, S[f"td{q}"], half * 16)
                            wait(act, S["side"], j - 1)
                        else:
                            wait(act, S["ht"], j - 1)
                        act.activation(hbuf[q][:, :], xj(j), ACT.Relu, bias=small[:, NMR, bass.ds(j, 1)],
                                       scale=small[:, RSTD, bass.ds(j, 1)]).then_inc(S["h"].sem, 1)
                    if n != 2 and within(j - 1, BLOCKS):
                        wait(act, S["ht"], j)
                        act.activation(hT[1 - q][0:96, 128:256], bank(5 - q, 96, 0, 128), ACT.Copy).then_inc(S["htv"].sem, 1)
                    if n != 2 and within(j - 2, BLOCKS):
                        wait(act, S["m"], j - 1)
                        wait(act, S[f"td{q}"], half * 16 - 16)
                        act.activation(trow[q][:, :], bank(6 + q, P, 0, NF), ACT.Copy,
                                       scale=1.0 if n == 0 else attr[:, bass.ds(j - 2, 1)]).then_inc(S["tab"].sem, 1)
                pipeline(act, BLOCKS, 3, 2, 2, body)

            prep(0)

            for o, w in enumerate((A_W, B_W)):
                idx, key = ((A_IDX, A_KEY), (B_IDX, B_KEY))[o]
                act.wait_ge(s_pos[o], 1)

                def body(c, half, q, o=o, w=w, idx=idx, key=key):
                    wait(act, s_stage[o][q], half * 16 + 16)
                    st = stage[o][q].rearrange("p (u c) -> p u c", c=w)
                    at = bass.ds(c * CHUNK, CHUNK)
                    if o == 0:
                        act.activation(st[:, :, A_SH:A_SH + 3],
                                       sh[:, bass.ds(c * (3 * CHUNK), 3 * CHUNK)].rearrange("p (u c) -> p u c", c=3),
                                       ACT.Copy).then_inc(s_fill[o], 1)
                    act.activation(st[:, :, idx:idx + 1].bitcast(I32), key_i[1 - o][:, at].unsqueeze(2),
                                   ACT.Copy).then_inc(s_fill[o], 1)
                    act.activation(st[:, :, key:key + 1], key_f[o][:, at].unsqueeze(2), ACT.Copy).then_inc(s_fill[o], 1)
                    if o == 1 and is_static(c) and c < 2:
                        act.wait_ge(s_scat[0][q], 16 * CHUNK * (CHUNKS // 2))
                    act.activation(pos_r[q], pos_i[o][:, at], ACT.Copy).then_inc(s_fill[o], 1)
                pipeline(act, CHUNKS, 2, 0, 0, body)

            for n in range(4):
                L, S, C = LAYERS[n], s_e[n], s_c[n]
                if L.mlp:
                    tcols = 512 if n == 0 else 256
                    hrows = 100 if n == 1 else P

                    def body(g, half, q, n=n, S=S, tcols=tcols, hrows=hrows):
                        wait(act, S["tr"], g + 1)
                        act.activation(attrT[:, 0:tcols], bank(0, P, 0, tcols), ACT.Copy).then_inc(S["tc"].sem, 1)
                        wait(act, S["m1"], g + 1)
                        for b in range(2 if n == 1 else 1):
                            i = act.activation(hidT[q][0:hrows, 512 * b:512 * b + 512], bank(2 + b, hrows, 0, 512),
                                               ACT.Silu if n == 3 else ACT.Relu,
                                               scale={0: 1.0, 1: R2 / math.sqrt(10.0), 3: 1 / math.sqrt(8.0)}[n])
                        i.then_inc(S["hid"].sem, 1)
                    pipeline(act, GROUPS, 2, 2, 0, body)

                (a0, a1) = L.chunks[0]

                def combine(j, half, q, n=n, C=C, a0=a0, a1=a1):
                    if within(j, BLOCKS):
                        wait(act, C["trn"], j + 1)
                        act.activation(by_kind(sumT[q][0:a1 - a0, 0, :]), by_bin(bank(0, a1 - a0, 0, 512)), ACT.Copy).then_inc(C["ca"].sem, 1)
                    if within(j - 1, BLOCKS):
                        if n == 0:
                            wait(act, C["t1"], j)
                            act.activation(hbuf[1 - q][:, 0:96], tmp[1 - q][:, 0:96], ACT.Sigmoid).then_inc(C["sig"].sem, 1)
                        if n == 2:
                            wait(act, C["big"], j)
                            act.activation(hT[1 - q][0:64, 0:128], bank(3 - q, 64, 0, 128), ACT.Copy,
                                           scale=1 / math.sqrt(96.0) / 8).then_inc(C["ms"].sem, 1)
                pipeline(act, BLOCKS, 3, 2, 1, combine)
                if n < 3:
                    prep(n + 1)
            act.wait_ge(s_trig, 1)
            act.activation(scratch(4), scratch(2), ACT.Sin)
            act.activation(scratch(5), scratch(3), ACT.Sin).then_inc(s_trig, 1)

        @block.vector
        def _(dve):
            links = [0]

            def link(ins):
                links[0] += 1
                ins.then_inc(s_chain, 1)
                dve.wait_ge(s_chain, links[0])

            dve.wait_ge(s_in, 48)
            sh3 = sh.rearrange("p (e c) -> p e c", c=3)
            link(dve.tensor_tensor(sh2, sh, sh, ALU.mult))
            dve.tensor_reduce(norm, sh2.rearrange("p (e c) -> p e c", c=3), AX_X, ALU.add).then_inc(s_sq, 1)
            dve.wait_ge(s_rt, 1)
            link(dve.reciprocal(norm, norm))
            link(dve.tensor_tensor(sh3, sh3, norm.unsqueeze(2).to_broadcast([P, COLS, 3]), ALU.mult))

            def statistics(n):
                S = s_p[n]
                with dve.Fori(0, BLOCKS) as j:
                    dve.bn_stats(stats[:, bass.ds(j, 1), :].rearrange("p j c -> p (j c)"), xj(j)).then_inc(S["stat"].sem, 1)
                wait(dve, S["stat"], BLOCKS)
                me, ve, mo, vo = (stats[:, :, i] for i in (1, 2, 4, 5))
                link(dve.tensor_tensor(scratch(2), me, mo, ALU.add))
                link(dve.tensor_tensor(scratch(3), me, mo, ALU.subtract))
                link(dve.tensor_tensor(scratch(4), ve, vo, ALU.add))
                link(dve.tensor_tensor(scratch(3), scratch(3), scratch(3), ALU.mult))
                link(dve.tensor_scalar(scratch(4), scratch(4), 1 / NF, EPS, ALU.mult, ALU.add))
                dve.scalar_tensor_tensor(out=scratch(4), in0=scratch(3), scalar=0.25, in1=scratch(4),
                                         op0=ALU.mult, op1=ALU.add).then_inc(S["var"].sem, 1)
                wait(dve, S["root"], 1)
                link(dve.reciprocal(scratch(RSTD), scratch(4)))
                dve.scalar_tensor_tensor(out=scratch(NMR), in0=scratch(2), scalar=-0.5, in1=scratch(RSTD),
                                         op0=ALU.mult, op1=ALU.mult).then_inc(S["rstd"].sem, 1)

            def prep(n):
                S = s_p[n]

                def body(j, half, q):
                    if n == 2:
                        if within(j, BLOCKS):
                            wait(dve, S["h"], j + 1)
                            dve.tensor_tensor(xj(j), xj(j), hbuf[q][:, :], ALU.add).then_inc(S["side"].sem, 1)
                        return
                    if within(j - 1, BLOCKS):
                        wait(dve, S["ht"], j)
                        dve.tensor_copy(hT[1 - q][0:64, 0:128], bank(3 - q, 64, 0, 128)).then_inc(S["hts"].sem, 1)
                    if within(j - 2, BLOCKS):
                        wait(dve, S["m"], j - 1)
                        if n == 0:
                            dve.tensor_copy(sj(j - 2), bank(q, P, 0, 192)).then_inc(S["side"].sem, 1)
                        elif n == 1:
                            dve.scalar_tensor_tensor(out=xj(j - 2), in0=bank(q, P, 0, NF),
                                                     scalar=attr[:, bass.ds(j - 2, 1)], in1=xj(j - 2),
                                                     op0=ALU.mult, op1=ALU.add).then_inc(S["side"].sem, 1)
                        else:
                            dve.tensor_scalar(side[:, bass.ds((j - 2) * 192, NF)], bank(q, P, 0, NF),
                                              attr[:, bass.ds(j - 2, 1)], None, ALU.mult).then_inc(S["side"].sem, 1)
                pipeline(dve, BLOCKS, 3, 2, 2, body)

            def binning(o):
                link(dve.tensor_scalar(int_a, key_i[o], 5, None, ALU.arith_shift_right))
                link(dve.tensor_scalar(int_b, key_i[o], BIN - 1, None, ALU.bitwise_and))
                link(dve.tensor_copy(bin_h, int_a))
                link(dve.tensor_copy(key_f[o], int_b))
                with dve.Fori(0, BINS) as b:
                    dve.tensor_scalar(eq, bin_h, iota_bins[:, bass.ds(b, 1)], 0.0, ALU.is_equal, ALU.add,
                                      accum_out=count[:, bass.ds(b, 1)]).then_inc(s_cnt[o], 1)
                    dve.wait_ge(s_cnt[o], b + 1)
                dve.wait_ge(s_cum[o], 1)
                link(dve.tensor_scalar(bins_i, bank(0, P, 128, 128 + BINS), float(P - 1), None, ALU.add))
                link(dve.tensor_scalar(bins_i, bins_i, 7, None, ALU.arith_shift_right))
                link(dve.tensor_copy(ntile, bins_i))
                link(dve.tensor_tensor_scan(first_tile, ntile, bins_z, 0.0, ALU.add, ALU.add))
                link(dve.tensor_tensor(first_tile, first_tile, ntile, ALU.subtract))
                link(dve.tensor_scalar(bins_f, first_tile, float(P), -1.0, ALU.mult, ALU.add))
                link(dve.tensor_tensor(base, bins_f, bank(0, P, 0, BINS), ALU.add))
                for c in range(TCOLS):
                    link(dve.tensor_scalar(bins_f, first_tile, tile_id[:, c:c + 1], 0.0, ALU.is_le, ALU.add,
                                           accum_out=tile_bin[:, c:c + 1]))
                if o:
                    dve.wait_ge(s_tbd[0], 16)
                dve.tensor_scalar(tile_bin_i, tile_bin, -1.0, None, ALU.add).then_inc(s_tb[o], 1)
                link(dve.memset(pos_f, 0.0))
                with dve.Fori(0, BINS) as b:
                    dve.tensor_scalar(eq, bin_h, iota_bins[:, bass.ds(b, 1)], None, ALU.is_equal).then_inc(s_eq[o], 1)
                    dve.wait_ge(s_eq[o], b + 1)
                    dve.tensor_tensor_scan(wide[:, 0:COLS], eq, zero_h, base[:, bass.ds(b, 1)],
                                           ALU.add, ALU.add).then_inc(s_scan[o], 1)
                    dve.wait_ge(s_scan[o], b + 1)
                    dve.sem_inc(s_apart["dve"], 1)
                    dve.copy_predicated(pos_f, eq, wide[:, 0:COLS]).then_inc(s_pick[o], 1)
                    dve.wait_ge(s_pick[o], b + 1)
                link(dve.tensor_copy(int_a, pos_f))
                link(dve.tensor_scalar(pos_i[o], int_a, 10, 10, ALU.arith_shift_right, ALU.logical_shift_left))
                link(dve.tensor_scalar(int_b, int_a, P - 1, 3, ALU.bitwise_and, ALU.logical_shift_left))
                link(dve.tensor_tensor(pos_i[o], pos_i[o], int_b, ALU.bitwise_or))
                link(dve.tensor_scalar(int_b, int_a, 7, GT - 1, ALU.arith_shift_right, ALU.bitwise_and))
                dve.tensor_tensor(pos_i[o], pos_i[o], int_b, ALU.bitwise_or).then_inc(s_pos[o], 1)

            dve.wait_ge(s_nodes, 32)
            statistics(0)
            prep(0)
            wait(dve, s_p[0]["tab"], BLOCKS)
            dve.wait_ge(s_const, 1)
            binning(0)
            dve.wait_ge(s_pos[0], 1)
            binning(1)

            for n in range(4):
                L, S, C = LAYERS[n], s_e[n], s_c[n]
                o = 0 if L.rowsA else 1
                wait(dve, S["zero"], 1)
                if n != 2:
                    for q in range(2):
                        link(dve.memset(sel[q][:, :, 32:128], 0.0))
                dve.wait_ge(s_tbs[o], 16)

                def select(g, half, q, n=n, L=L, S=S):
                    wait(dve, S[f"rows{q}"], (half + 1) * (32 if n == 0 else 16))
                    if L.rowsA:
                        r = rows_a(q)[1]
                        key, e0, e1 = r[:, :, A_KEY - A_SH], None, r[:, :, 0:3]
                    else:
                        r = rows_b(q).rearrange("p (t c) -> p t c", c=B_W)
                        key, e0, e1 = r[:, :, B_KEY], r[:, :, B_4], r[:, :, B_4 + 1:B_4 + 4]
                    nodes = iota_bin[:, :].unsqueeze(1).to_broadcast([P, GT, BIN])
                    hot = sel[q][:, :, 0:BIN] if n == 0 else onehot[:, :, :]
                    dve.tensor_tensor(hot, nodes, key.unsqueeze(2).to_broadcast([P, GT, BIN]),
                                      ALU.is_equal).then_inc(S["oh"].sem, 1)
                    wait(dve, S["oh"], g + 1)
                    if n == 2:
                        dve.tensor_tensor(sel[q][:, :, 0:128].rearrange("p t (k b) -> p t k b", k=4),
                                          hot.unsqueeze(2).to_broadcast([P, GT, 4, BIN]),
                                          r[:, :, B_4:B_4 + 4].unsqueeze(3).to_broadcast([P, GT, 4, BIN]),
                                          ALU.mult).then_inc(S["sel"].sem, 1)
                        return
                    if n:
                        dve.tensor_tensor(sel[q][:, :, 0:BIN], hot, e0.unsqueeze(2).to_broadcast([P, GT, BIN]), ALU.mult)
                    dve.tensor_tensor(sel[q][:, :, 128:224].rearrange("p t (k b) -> p t k b", k=3),
                                      hot.unsqueeze(2).to_broadcast([P, GT, 3, BIN]),
                                      e1.unsqueeze(3).to_broadcast([P, GT, 3, BIN]), ALU.mult).then_inc(S["sel"].sem, 1)

                def edges(g, half, q, n=n, L=L, S=S, o=o, select=select):
                    _, at = nc.values_load_multi_w_load_instructions(
                        tile_bins[0:1, bass.ds(g * GT, GT)], engines=(DVE,), min_val=0, max_val=BINS - 1,
                        skip_runtime_bounds_check_because="counts of at most BINS bins, less one")
                    for u in range(0, GT, 2):
                        m = g * GT + u
                        b = u // 2 % 2
                        if within(m - LAG_FL, TILES):
                            wait(dve, S["sc"], m - LAG_FL + 2)
                            for h in range(2):
                                wait(dve, S["fl"], m - LAG_FL + h)
                                sums = acc[:, bass.ds(at[u + h] * L.width, L.width)]
                                dve.tensor_tensor(sums, sums, bank(6 + b, P, 256 * h, 256 * h + L.width),
                                                  ALU.add).then_inc(S["fl"].sem, 1)
                        if L.mlp and within(m, TILES):
                            if u == 0:
                                wait(dve, S[f"ga{q}"], half * (16 * GT) + 16 * GT)
                            wait(dve, S["w"], m + 2)
                            for h in range(2):
                                wt = bank(4 + b, P, 224 * h, 224 * h + L.wcols)
                                xs = gath[q][:, u + h, 0:S0]
                                xv = gath[q][:, u + h, S0:NF].rearrange("p (c m) -> p c m", c=3)
                                nv = (L.wcols - 128) // V1
                                a = (2 * b + h) * (416 if n == 0 else 320)
                                if n == 0:
                                    ps = prod[:, a:a + 704].rearrange("p (a c) -> p a c", a=2)[:, :, 0:S0]
                                    pv = prod[:, a + S0:a + S0 + 288].rearrange("p (w c m) -> p w c m", w=3, c=3)
                                else:
                                    both = prod[:, a:a + 320].rearrange("p (w c) -> p w c", w=2)
                                    ps, pv = both[:, :, 0:S0], both[:, :, S0:NF].rearrange("p w (c m) -> p w c m", c=3)
                                dve.tensor_tensor(ps, wt[:, 0:128].rearrange("p (w c) -> p w c", w=2),
                                                  xs.unsqueeze(1).to_broadcast([P, 2, S0]), ALU.mult)
                                ins = dve.tensor_tensor(pv, wt[:, 128:L.wcols].rearrange("p (w m) -> p w m", w=nv)
                                                        .unsqueeze(2).to_broadcast([P, nv, 3, V1]),
                                                        xv.unsqueeze(1).to_broadcast([P, nv, 3, V1]), ALU.mult)
                                ins.then_inc(S["prod"].sem, 1)
                        if u == LAG_FL and within(g + 1, GROUPS):
                            select(g + 1, half + q, 1 - q)
                        if is_static(g) and g == GROUPS and u == LAG_FL - 2:
                            break
                select(0, 0, 0)
                pipeline(dve, GROUPS, 2, 2, 1, edges)

                (b0, b1) = L.chunks[1]

                def combine(j, half, q, n=n, L=L, C=C, b0=b0, b1=b1):
                    if within(j, BLOCKS):
                        wait(dve, C["trn"], j + 1)
                        dve.tensor_copy(by_kind(sumT[q][0:b1 - b0, 1, :]), by_bin(bank(1, b1 - b0, 0, 512))).then_inc(C["cd"].sem, 1)
                    if within(j - 1, BLOCKS):
                        k, r = j - 1, 1 - q
                        po = pb[2 + r]
                        wait(dve, C["big"], j)
                        if n == 0:
                            dve.scalar_tensor_tensor(out=tmp[r][:, :], in0=po[:, 0:192], scalar=1 / 32.0, in1=sj(k),
                                                     op0=ALU.mult, op1=ALU.add).then_inc(C["t1"].sem, 1)
                            wait(dve, C["sig"], j)
                            dve.tensor_tensor(trow[r][:, 0:64], tmp[r][:, 0:64], hbuf[r][:, 0:64], ALU.mult)
                            dve.tensor_tensor(trow[r][:, 64:NF].rearrange("p (c m) -> p c m", c=3),
                                              tmp[r][:, 96:192].rearrange("p (c m) -> p c m", c=3),
                                              hbuf[r][:, 64:96].unsqueeze(1).to_broadcast([P, 3, V1]),
                                              ALU.mult).then_inc(C["t2"].sem, 1)
                            wait(dve, C["t2"], j)
                            dve.tensor_tensor(xj(k), xj(k), trow[r][:, :], ALU.add).then_inc(C["ev"].sem, 1)
                        elif n == 1:
                            dve.scalar_tensor_tensor(out=xj(k), in0=po[:, 0:NF], scalar=small[:, 6, bass.ds(k, 1)],
                                                     in1=xj(k), op0=ALU.mult, op1=ALU.add).then_inc(C["ev"].sem, 1)
                        elif n == 3:
                            dve.tensor_scalar(acc[:, bass.ds(k * (4 * NF), NF + 1)], po[:, 0:NF + 1],
                                              attr[:, bass.ds(k, 1)], 1 / math.sqrt(960.0), ALU.mult,
                                              ALU.mult).then_inc(C["ev"].sem, 1)
                        else:
                            dve.tensor_scalar(hT[r][0:96, 128:256], bank(6 + r, 96, 0, 128),
                                              math.sqrt(3.0 / 128) / R3 / math.sqrt(32.0), None, ALU.mult).then_inc(C["mv"].sem, 1)
                    if n == 2 and within(j - 2, BLOCKS):
                        wait(dve, C["fin"], j - 1)
                        dve.scalar_tensor_tensor(out=xj(j - 2), in0=bank(4 + q, P, 0, NF), scalar=0.0, in1=xj(j - 2),
                                                 op0=ALU.max, op1=ALU.add).then_inc(C["ev"].sem, 1)
                if n == 2:
                    dve.wait_ge(s_lw, 16 * len(late))
                    for m, f in sum_factors(2):
                        ins = dve.tensor_scalar(m, m, f, None, ALU.mult)
                    ins.then_inc(s_lf, 1)
                if n == 1:
                    link(dve.tensor_scalar(small[:, 6, :], attr[:, :], 0.125 / math.sqrt(96.0), None, ALU.mult))
                pipeline(dve, BLOCKS, 3, 2, 2 if n == 2 else 1, combine)
                wait(dve, C["ev"], BLOCKS)
                if n < 3:
                    statistics(n + 1)
                    prep(n + 1)

            conv = acc[:, 0:BLOCKS * 4 * NF].rearrange("p (j c) -> p j c", j=BLOCKS)
            sc = side[:, :].rearrange("p (j c) -> p j c", j=BLOCKS)[:, :, 0:NF]
            x3 = x[:, :].rearrange("p (j c) -> p j c", j=BLOCKS)
            big = 12582912.0
            wait(dve, s_p[3]["side"], BLOCKS)
            link(dve.tensor_scalar(scratch(2), conv[:, :, 0], 0.1, None, ALU.mult))
            link(dve.tensor_scalar(scratch(3), scratch(2), 1 / (2 * math.pi), big, ALU.mult, ALU.add))
            link(dve.tensor_scalar(scratch(3), scratch(3), -big, None, ALU.add))
            link(dve.scalar_tensor_tensor(out=scratch(2), in0=scratch(3), scalar=-6.28125, in1=scratch(2),
                                          op0=ALU.mult, op1=ALU.add))
            link(dve.scalar_tensor_tensor(out=scratch(2), in0=scratch(3), scalar=-(2 * math.pi - 6.28125),
                                          in1=scratch(2), op0=ALU.mult, op1=ALU.add))
            link(dve.tensor_scalar(scratch(2), scratch(2), 3.1415925, -3.1415925, ALU.min, ALU.max))
            link(dve.scalar_tensor_tensor(out=scratch(3), in0=scratch(2), scalar=-1.0, in1=scratch(2),
                                          op0=ALU.mult, op1=ALU.max))
            dve.tensor_scalar(scratch(3), scratch(3), -1.0, math.pi / 2, ALU.mult, ALU.add).then_inc(s_trig, 1)
            dve.wait_ge(s_trig, 2)
            shape = [P, BLOCKS, NF]
            link(dve.tensor_tensor(sc, sc, scratch(5).unsqueeze(2).to_broadcast(shape), ALU.mult))
            link(dve.tensor_tensor(x3, x3, sc, ALU.add))
            link(dve.tensor_tensor(conv[:, :, 1:NF + 1], conv[:, :, 1:NF + 1],
                                   scratch(4).unsqueeze(2).to_broadcast(shape), ALU.mult))
            dve.tensor_tensor(x3, x3, conv[:, :, 1:NF + 1], ALU.add).then_inc(s_fin, 1)

        @block.tensor
        def _(pe):
            pe.wait_ge(s_const, 1)
            pe.wait_ge(s_w, 16 * len(loads))
            pe.wait_ge(s_wf, N_SCALED)

            def prep(n):
                if n == 2:
                    return
                S = s_p[n]
                ns = LAYERS[n].tab_side

                def body(j, half, q):
                    if within(j, BLOCKS):
                        wait(pe, S["h"], j + 1)
                        pe.sem_inc(s_apart["pe"], 1)
                        pe.transpose(bank(2 + q, 64, 0, 128), hbuf[q][:, 0:64], ident[:, :])
                        pe.transpose(bank(4 + q, 96, 0, 128), hbuf[q][:, 64:NF], ident[:, :]).then_inc(S["ht"].sem, 1)
                    if within(j - 1, BLOCKS):
                        r = 1 - q
                        wait(pe, S["hts"], j)
                        wait(pe, S["htv"], j)
                        wait(pe, S["tab"], j - 2)
                        wait(pe, S["side"], j - 2)
                        pe.sem_inc(s_apart["pe"], 1)
                        hs, hv = hT[r][0:64, 0:128], hT[r][0:96, 128:256]
                        pe.matmul(bank(6 + r, P, 0, 64), hs, wps[n][:, 0:64], start=True, stop=True, skip_group_check=True)
                        pe.matmul(bank(6 + r, P, 64, 160), hv, wpv[n][:, 0:96], start=False, stop=True, skip_group_check=True)
                        pe.matmul(bank(r, P, 0, ns), hs, wps[n][:, 64:64 + ns], start=True, stop=True, skip_group_check=True)
                        pe.matmul(bank(r, P, ns, 96 + ns), hv, wpv[n][:, 96:192], start=False, stop=True,
                                  skip_group_check=True).then_inc(S["m"].sem, 1)
                pipeline(pe, BLOCKS, 3, 2, 1, body)

            prep(0)
            for o in range(2):
                if o == 0:
                    wait(pe, s_p[0]["side"], BLOCKS)
                else:
                    pe.wait_ge(s_tb[0], 1)
                pe.wait_ge(s_cnt[o], BINS)
                pe.matmul(bank(0, P, 0, BINS), tri, count, start=True, stop=True)
                pe.matmul(bank(0, P, 128, 128 + BINS), ones, count, start=True, stop=True).then_inc(s_cum[o], 1)

            for n in range(4):
                L, S, C = LAYERS[n], s_e[n], s_c[n]
                pe.wait_ge(s_pos[1], 1)
                if n:
                    wait(pe, s_c[n - 1]["ev"], BLOCKS)
                if n != 2:
                    wait(pe, s_p[n]["side"], BLOCKS)
                    wait(pe, s_p[n]["tab"], BLOCKS)

                def turn(g, half, q, n=n, S=S):
                    wait(pe, S[f"rows{q}"], (half + 1) * (32 if n == 0 else 16))
                    pe.sem_inc(s_apart["pe"], 1)
                    if n == 0:
                        for p in range(4):
                            i = pe.transpose(bank(0, P, 128 * p, 128 * p + 128), rows_a(q)[0][:, 128 * p:128 * p + 128], ident[:, :])
                    else:
                        for p in range(2):
                            i = pe.transpose(bank(0, P, 128 * p, 128 * p + 128), rows_b(q)[:, 128 * p:128 * p + 128], ident[:, :])
                    i.then_inc(S["tr"].sem, 1)

                def hidden(g, n=n, S=S):
                    wait(pe, S["tc"], g + 1)
                    if n == 0:
                        i = pe.matmul(bank(2, P, 0, 512), w1[0][:, :], attrT[:, 0:512], start=True, stop=True)
                    elif n == 1:
                        for k in range(4):
                            i = pe.matmul(bank(2 + k // 2, 100, 256 * (k % 2), 256 * (k % 2) + 256), w1[1][:, k, :],
                                          attrT[:, 0:256], start=True, stop=True)
                    else:
                        for k in range(2):
                            i = pe.matmul(bank(2, P, 256 * k, 256 * k + 256), w1[3][:, k, :], attrT[:, 0:256],
                                          start=True, stop=True)
                    i.then_inc(S["m1"].sem, 1)

                def hidden_of(u, q, n=n):
                    if n == 0:
                        return hidT[q][:, 128 * (u // 2):128 * (u // 2) + 128], w2[0][:, u % 2, :]
                    quad, k = u // 4, u % 4
                    if n == 1:
                        a = (k * 2 + quad) * 128
                        return hidT[q][0:100, a:a + 128], w2[1][0:100, :]
                    a = (k // 2 * 2 + quad) * 128
                    return hidT[q][:, a:a + 128], w2[3][:, k % 2, :]

                def edges(g, half, q, n=n, L=L, S=S, turn=turn, hidden=hidden, hidden_of=hidden_of):
                    lag = LAG_SC if L.mlp else 0
                    for u in range(0, GT, 2):
                        m = g * GT + u
                        if L.mlp and within(m, TILES):
                            if u == 0:
                                wait(pe, S["hid"], g + 1)
                            for h in range(2):
                                hid, w = hidden_of(u + h, q)
                                pe.matmul(bank(4 + u // 2 % 2, P, 224 * h, 224 * h + L.wcols), hid, w,
                                          start=True, stop=True, skip_group_check=True).then_inc(S["w"].sem, 1)
                        if within(m - lag, TILES):
                            v = (u - lag) % GT
                            b = v // 2 % 2
                            qv = q if u >= lag else 1 - q
                            if v == 0:
                                wait(pe, S["sel"], g + 1)
                                if not L.mlp:
                                    wait(pe, S[f"ga{q}"], half * (16 * GT) + 16 * GT)
                            if L.mlp:
                                wait(pe, S["prod"], m - lag + 2)
                            wait(pe, S["fl"], m - lag - RING + 2)
                            for h in range(2):
                                out = bank(6 + b, P, 256 * h, 256 * h + L.width)
                                if n == 2:
                                    ins = pe.matmul(out, sel[qv][:, v + h, 0:128], gath[qv][:, v + h, :],
                                                    start=True, stop=True, skip_group_check=True)
                                else:
                                    a = (2 * b + h) * (416 if n == 0 else 320)
                                    end = a + NF + L.width
                                    pe.matmul(out, sel[qv][:, v + h, 96:224], prod[:, a + NF:end], start=True, stop=False,
                                              skip_group_check=True)
                                    ins = pe.matmul(bank(6 + b, P, 256 * h, 256 * h + NF), sel[qv][:, v + h, 0:128],
                                                    prod[:, a:a + NF], start=False, stop=True, skip_group_check=True)
                                ins.then_inc(S["sc"].sem, 1)
                        if L.mlp and within(g + 1, GROUPS):
                            if u == 0:
                                turn(g + 1, half + q, 1 - q)
                            if u == 4:
                                hidden(g + 1)
                        if is_static(g) and g == GROUPS and u == lag - 2:
                            break
                if L.mlp:
                    turn(0, 0, 0)
                    hidden(0)
                pipeline(pe, GROUPS, 2, 2, 1 if L.mlp else 0, edges)

                wait(pe, S["fl"], TILES)
                if n:
                    pe.wait_ge(s_lw, 16 * len(late))
                if n == 2:
                    pe.wait_ge(s_lf, 1)
                order = sum_products(n)

                def combine(j, half, q, n=n, L=L, C=C, order=order):
                    if within(j, BLOCKS):
                        wait(pe, C["stg"], j + 1)
                        wait(pe, C["ca"], j)
                        wait(pe, C["cd"], j)
                        pe.sem_inc(s_apart["pe"], 1)
                        for c, (a, b) in enumerate(L.chunks):
                            for i in range(4):
                                ins = pe.transpose(bank(c, b - a, 128 * i, 128 * i + 128),
                                                   stg[q][:, L.width * i + a:L.width * i + b], ident[:, :])
                        ins.then_inc(C["trn"].sem, 1)
                    if within(j - 1, BLOCKS):
                        r = 1 - q
                        wait(pe, C["ca"], j)
                        wait(pe, C["cd"], j)
                        if n != 2:
                            wait(pe, C["ev"], j - 2)
                        pe.sem_inc(s_apart["pe"], 1)

                        def sums(c, k, rows_):
                            return sumT[r][0:rows_, c, 128 * k:128 * k + 128]
                        if n == 2:
                            for lo, hi, b0, terms in ((0, 64, 2, [(0, 0)] + [(1, k) for k in (1, 2, 3)]),
                                                      (64, 160, 6, [(0, k) for k in (1, 2, 3)] + [(1, k) for k in range(4)])):
                                for i, (c, k) in enumerate(terms):
                                    rr = 64 if c == 0 else 96
                                    ins = pe.matmul(bank(b0 + r, hi - lo, 0, 128), wsum[2][0:rr, c, k, lo:hi], sums(c, k, rr),
                                                    start=(i == 0), stop=(i == len(terms) - 1))
                            ins.then_inc(C["big"].sem, 1)
                        else:
                            for i, (c, k, rr, lo, hi) in enumerate(order):
                                ins = pe.matmul(bank(2 + r, P, lo, hi), sums(c, k, rr), wsum[n][0:rr, c, k, lo:hi],
                                                start=(i == 0), stop=(i == len(order) - 1), skip_group_check=True)
                            ins.then_inc(C["big"].sem, 1)
                    if n == 2 and within(j - 2, BLOCKS):
                        wait(pe, C["ms"], j - 1)
                        wait(pe, C["mv"], j - 1)
                        wait(pe, C["ev"], j - 3)
                        pe.sem_inc(s_apart["pe"], 1)
                        pe.matmul(bank(4 + q, P, 0, 64), hT[q][0:64, 0:128], w2s[:, :], start=True, stop=True,
                                  skip_group_check=True)
                        pe.matmul(bank(4 + q, P, 64, NF), hT[q][0:96, 128:256], w2v[:, :], start=False, stop=True,
                                  skip_group_check=True).then_inc(C["fin"].sem, 1)
                pipeline(pe, BLOCKS, 3, 2, 2 if n == 2 else 1, combine)
                if n < 3:
                    prep(n + 1)


_WEIGHTS = ["L0_gnn_W_skip0", "L0_gnn_W_skip1", "L0_gnn_W_nl0", "L0_gnn_W_nl1", "L0_gnn_W_fc1", "L0_gnn_W_fc2",
            "L0_gnn_W_out_s", "L0_gnn_W_out_v", "L1_gnn_W_si0", "L1_gnn_W_si1", "L1_gnn_W_l1_0", "L1_gnn_W_l1_1",
            "L1_gnn_W_l2_00", "L1_gnn_W_l2_10", "L1_gnn_W_l2_01", "L1_gnn_W_l2_11", "L1_gnn_W_fc1", "L1_gnn_W_fc2",
            "L2_gnn_W1", "L2_gnn_W2", "L2_gnn_W3", "L2_gnn_W4", "L2_gnn_W5", "L2_gnn_Ws", "L2_gnn_Wv",
            "L3_gnn_W_sc_s", "L3_gnn_W_sc_v", "L3_gnn_W1_s", "L3_gnn_W1_v", "L3_gnn_W2_s", "L3_gnn_W2_v", "L3_gnn_W3",
            "L3_gnn_fcW1", "L3_gnn_fcW2"]


def _feature_order(np):
    return np.concatenate([np.arange(S0), S0 + (np.arange(V1)[None, :] * 3 + np.arange(3)[:, None]).ravel()])


def kernel(**inputs):
    import numpy as np
    import concourse.bacc as bacc
    from concourse.bass_utils import run_bass_kernel_spmd

    def padded(a, n, value):
        a = np.asarray(a)
        return np.concatenate([a, np.full((n - a.shape[0],) + a.shape[1:], value, a.dtype)])

    def rows_of(parts, width):
        rows = np.concatenate([np.asarray(inputs[k]) for k in parts], axis=1)
        out = np.zeros((P * COLS, width), rows.dtype)
        out[:EDGES, :rows.shape[1]] = rows
        return out.reshape(P, COLS * width)

    order = _feature_order(np)
    arrays = {
        "x": padded(np.asarray(inputs["x"])[:, order], NPAD, 0),
        "node_vec1": padded(inputs["node_vec1"], NPAD, 0),
        "skey": padded(inputs["src"], P * COLS, PAD_NODE).reshape(P, COLS),
        "dkey": padded(inputs["dst"], P * COLS, PAD_NODE).reshape(P, COLS),
        "edge_attr_3": padded(inputs["edge_attr_3"], P * COLS, 1).reshape(P, COLS * 3),
        "rows_a": rows_of(["edge_attr_64"], A_W),
        "rows_b": rows_of(["edge_attr_10", "edge_attr_8", "edge_attr_4"], B_W),
    }
    for k in _WEIGHTS:
        arrays[k] = np.ascontiguousarray(inputs[k])
    nc = bacc.Bacc("TRN2", target_bir_lowering=False, num_devices=1)
    t = {k: nc.dram_tensor(f"in_{k}", a.shape, mybir.dt.from_np(a.dtype), kind="ExternalInput").ap()
         for k, a in arrays.items()}
    t["out"] = nc.dram_tensor("out_x", (NPAD, NF), F32, kind="ExternalOutput").ap()
    gnn_program(nc, t)
    r = run_bass_kernel_spmd(nc, [{f"in_{k}": a for k, a in arrays.items()}], core_ids=[0])
    got = np.asarray(r.results[0]["out_x"])
    back = np.argsort(order)
    return got[:NODES][:, back]
```

```python
import math
from contextlib import ExitStack

import concourse.bass as bass
from concourse import mybir

F32 = mybir.dt.float32
I32 = mybir.dt.int32
I16 = mybir.dt.int16
BF16 = mybir.dt.bfloat16
ALU = mybir.AluOpType
ACT = mybir.ActivationFunctionType
AX_X = mybir.AxisListType.X
DVE, POOL, SP = mybir.EngineType.DVE, mybir.EngineType.Pool, mybir.EngineType.SP

P = 128
NODES, EDGES = 3125, 100000
S0, V1 = 64, 32
NF = S0 + 3 * V1
BLOCKS = -(-NODES // P)
NPAD = BLOCKS * P
BIN = 32
BINS = NPAD // BIN
PAD_NODE = -(-NODES // BIN) * BIN
COLS = -(-EDGES // P)
GT = 8
FULL_BINS = PAD_NODE // BIN
MAX_TILES = (EDGES + FULL_BINS * (P - 1)) // P + 1
GROUPS = -(-MAX_TILES // GT)
TILES = GROUPS * GT
SLOTS = TILES * P
CHUNK = 23
CHUNKS = COLS // CHUNK
TCOLS = -(-TILES // P)
LAG_SC, LAG_FL = 2, 4
RING = 4

A_EF, A_SH, A_IDX, A_KEY, A_W = 0, 64, 67, 68, 69
B_10, B_8, B_4, B_IDX, B_KEY, B_W = 0, 10, 18, 22, 23, 32

N_SCALED = 10 + 3
EPS = 1e-5
R2, R3 = math.sqrt(2.0), math.sqrt(3.0)
assert COLS % CHUNK == 0 and CHUNKS % 2 == 0 and GROUPS % 2 == 0
SEGMENTS = (0, 6, 18, CHUNKS)
SPREAD = TCOLS * P // (CHUNKS - 2)
assert SPREAD * (CHUNKS - 2) == TCOLS * P and 2 * SPREAD % GT == 0
PREP_FROM = SEGMENTS[2]


def is_static(v):
    return isinstance(v, int)


def within(v, n):
    return not is_static(v) or 0 <= v < n


class Signal:

    def __init__(self, sem, base):
        self.sem, self.base = sem, base


def wait(eng, signal, value):
    if is_static(value) and value <= 0:
        return
    if isinstance(signal, Signal):
        eng.wait_ge(signal.sem, value + signal.base)
    else:
        eng.wait_ge(signal, value)


def pipeline(eng, n, first, last, extra, body):
    for s in range(first):
        body(s, s // 2, s % 2)
    assert (n - first - last) % 2 == 0
    with eng.Fori(0, (n - first - last) // 2) as i:
        for u in range(first, first + 2):
            body(i * 2 + u, i + u // 2, u % 2)
    for s in range(n - last, n + extra):
        body(s, s // 2, s % 2)


def pairs(eng, a, b, body):
    assert a % 2 == 0 and b % 2 == 0
    with eng.Fori(0, (b - a) // 2) as i:
        for u in range(2):
            body(i * 2 + (a + u), i + a // 2, u)


class Layer:

    def __init__(self, n):
        self.n = n
        self.rowsA = n == 0
        self.mlp = n != 2
        self.width = 256 if n == 0 else 160
        self.wcols = 224 if n == 0 else 192
        self.chunks = [(0, 128), (128, 256)] if n == 0 else [(0, 64), (64, 160)]
        self.out = {0: 192, 1: 160, 2: 160, 3: 161}[n]
        self.tab_side = 96 if n == 0 else 64


LAYERS = [Layer(n) for n in range(4)]


def sum_weights(n):
    put = []
    if n == 0:
        put.append(("L0_gnn_W_out_s", 0, 64, 0, 0, 0, 0, 1.0))
        for i in range(3):
            put.append(("L0_gnn_W_out_v", 64, 96, 0 if i < 2 else 1, 0, (64, 96, 0)[i], 96 + 32 * i, 1.0))
            put.append(("L0_gnn_W_out_s", 64, 96, 0, 1 + i, 32 * i, 0, 1.0))
            put.append(("L0_gnn_W_out_v", 0, 64, 1, 1 + i, 64, 96 + 32 * i, 1.0))
            for j in range(3):
                if j != i:
                    sign = 1.0 if i == (j + 1) % 3 else -1.0
                    put.append(("L0_gnn_W_out_v", 96, 128, 0 if j == 0 else 1, 1 + i, (96, 0, 32)[j],
                                96 + 32 * (3 - i - j), sign))
        return put
    if n == 2:
        put.append(("L2_gnn_W1", 0, 64, 0, 0, 0, 0, 1.0))
        for i in range(3):
            put.append(("L2_gnn_W4", 0, 32, 1, 0, 32 * i, 64 + 32 * i, 1.0))
            put.append(("L2_gnn_W3", 0, 64, 0, 1 + i, 0, 64 + 32 * i, 1.0))
            put.append(("L2_gnn_W2", 0, 32, 1, 1 + i, 32 * i, 0, 1.0 / R3))
            for j in range(3):
                if j != i:
                    sign = 1.0 if i == (j + 1) % 3 else -1.0
                    put.append(("L2_gnn_W5", 0, 32, 1, 1 + i, 32 * j, 64 + 32 * (3 - i - j), sign / R2))
        return put
    if n == 1:
        ws, wv, o = (("L1_gnn_W_l2_00", 0), ("L1_gnn_W_l2_10", 0)), (("L1_gnn_W_l2_01", 0), ("L1_gnn_W_l2_11", 0)), 0
    else:
        ws, wv, o = (("L3_gnn_W2_s", 0), ("L3_gnn_W2_s", 64)), (("L3_gnn_W2_v", 0), ("L3_gnn_W2_v", 64)), 1
        put.append(("L3_gnn_W3", 0, 64, 0, 0, 0, 0, 1.0))
    put.append((ws[0][0], 0, 64, 0, 0, 0, o, 1.0))
    for i in range(3):
        put.append((wv[1][0], wv[1][1], wv[1][1] + 32, 1, 0, 32 * i, o + 64 + 32 * i, 1.0))
        put.append((wv[0][0], 0, 64, 0, 1 + i, 0, o + 64 + 32 * i, 1.0))
        put.append((ws[1][0], ws[1][1], ws[1][1] + 32, 1, 1 + i, 32 * i, o, 1.0))
        if n == 3:
            put.append(("L3_gnn_W3", 64, 96, 1, 1 + i, 32 * i, 0, 1.0))
    return put


def sum_products(n):
    if n == 0:
        return ([(0, 0, 128, 0, 192), (1, 0, 32, 160, 192)] + [(0, k, 128, 0, 192) for k in (1, 2, 3)]
                + [(1, k, 128, 96, 192) for k in (1, 2, 3)])
    o = 1 if n == 3 else 0
    return ([(0, 0, 64, 0, o + 64)] + [(0, k, 64, o + 32 + 32 * k, o + 64 + 32 * k) for k in (1, 2, 3)]
            + [(1, 0, 96, o + 64, o + 160)] + [(1, k, 96, 0, o + 64) for k in (1, 2, 3)])


def gnn_program(nc, t):
    ctx = ExitStack()
    with ctx:
        def sb(name, shape, dt=F32):
            return ctx.enter_context(nc.sbuf_tensor(name, shape, dt))

        def sem(name):
            return ctx.enter_context(nc.semaphore(name))

        rows_dram = [nc.dram_tensor("rows_a", (SLOTS, A_W), F32).ap(),
                     nc.dram_tensor("rows_b", (TCOLS * P * P, B_W), F32).ap()]
        given_dram = nc.dram_tensor("rows_given", (P * COLS + P, B_W), F32).ap()
        starts_dram = nc.dram_tensor("tile_starts", (TCOLS * P,), I32).ap()
        first_node_dram = nc.dram_tensor("tile_first_node", (TCOLS * P,), F32).ap()
        table_dram = [nc.dram_tensor(f"table_{n}", (NPAD, NF), F32).ap() for n in range(4)]
        bins_dram = [nc.dram_tensor(f"tile_bins_{o}", (TCOLS * P,), I32).ap() for o in range(2)]

        x = sb("x", [P, BLOCKS * NF])
        attr = sb("attr", [P, BLOCKS])
        side = sb("side", [P, BLOCKS * 192])
        acc = sb("acc", [P, BINS * 256])
        ident = sb("ident", [P, P])
        iota_bin = sb("iota_bin", [P, BIN])
        iota_bins = sb("iota_bins", [P, BINS])
        tile_bins = sb("tile_bins_row", [1, RING + TCOLS * P], I32)
        w1 = {0: sb("w1_0", [P, P]), 1: sb("w1_1", [P, 4, 100]), 3: sb("w1_3", [P, 2, P])}
        w2 = {0: sb("w2_0", [P, 2, 224]), 1: sb("w2_1", [P, 192]), 3: sb("w2_3", [P, 2, 192])}
        wsum = {0: sb("wsum_0", [P, 2, 4, LAYERS[0].out])}
        tail = BINS * 256
        for n in (1, 2, 3):
            tail -= 8 * LAYERS[n].out
            wsum[n] = acc[:, tail:tail + 8 * LAYERS[n].out].rearrange("p (c k o) -> p c k o", c=2, k=4)
        first_node = acc[:, BINS * LAYERS[1].width:BINS * LAYERS[1].width + TCOLS * P]
        assert tail >= BINS * LAYERS[1].width + TCOLS * P
        wps = {n: sb(f"wps_{n}", [S0, 2 * S0 if n else S0 + 96]) for n in (0, 1, 3)}
        wpv = {n: sb(f"wpv_{n}", [96, 192]) for n in (0, 1, 3)}
        w2s, w2v = sb("w2s", [S0, S0]), sb("w2v", [96, 96])
        rows = [sb(f"rows_{q}", [P, GT, A_W]) for q in range(2)]
        gath = [sb(f"gath_{q}", [P, GT, NF]) for q in range(2)]
        sel = [sb(f"sel_{q}", [P, GT, 224]) for q in range(2)]
        onehot = sb("onehot", [P, GT, BIN])
        prod = sb("prod", [P, 3 * 416 + 704])
        attrT = sb("attrT", [P, 512])
        hidT = [sb(f"hidT_{q}", [P, 1024]) for q in range(2)]
        stg = [sel[q][:, :, :].rearrange("p t c -> p (t c)")[:, 0:4 * 256] for q in range(2)]
        sumT = [gath[q][:, :, :].rearrange("p t c -> p (t c)")[:, 0:1024].rearrange("p (c m) -> p c m", c=2) for q in range(2)]
        tmp, hbuf, trow, hT = ([prod[:, 768 * q + a:768 * q + b] for q in range(2)]
                               for a, b in ((0, 192), (192, 352), (352, 512), (512, 768)))
        stats = sb("stats", [P, BLOCKS, 6])
        small = sb("small", [P, 12, BLOCKS])

        pb = [ctx.enter_context(nc.psum_tensor(f"bank_{i}", [P, 512], F32)) for i in range(6)]
        wide = ctx.enter_context(nc.psum_tensor("bank_67", [P, 1024], F32))
        pb += [wide[:, 0:512], wide[:, 512:1024]]

        def bank(i, p, a, b):
            return pb[i][0:p, a:b]

        used = [0]

        def carve(words):
            a = used[0]
            used[0] += words
            assert used[0] <= BINS * 256
            return acc[:, a:a + words]

        even = COLS + COLS % 2
        key_i = [carve(COLS).bitcast(I32) for _ in range(2)]
        key_next = carve(COLS).bitcast(I32)
        key_f = carve(COLS)
        pos_f = carve(COLS)
        pos_i = [carve(COLS).bitcast(I32) for _ in range(2)]
        int_a, int_b = carve(COLS).bitcast(I32), carve(COLS).bitcast(I32)
        bin_h = [carve(even // 2).bitcast(BF16)[:, 0:COLS] for _ in range(2)]
        eq = carve(even // 2).bitcast(I16)[:, 0:COLS]
        zero_h = carve(even // 2).bitcast(I16)[:, 0:COLS]
        sh = carve(3 * COLS)
        sh2 = carve(3 * COLS)
        norm = carve(COLS)
        tri, ones = carve(P), carve(P)
        count, ntile, first_tile, bins_f, bins_z, pad = (carve(BINS) for _ in range(6))
        base = [carve(BINS) for _ in range(2)]
        by_tile = carve(TCOLS * BINS)
        tile_pad, tile_node = carve(TCOLS), carve(TCOLS)
        tile_start = carve(TCOLS).bitcast(I32)
        starts_row = carve(TCOLS * P).bitcast(I32)
        falls, unsorted = carve(1), carve(1).bitcast(I32)
        bins_i = carve(BINS).bitcast(I32)
        tile_id, tile_bin = carve(TCOLS), carve(TCOLS)
        tile_bin_i = carve(TCOLS).bitcast(I32)
        stage = [[carve(CHUNK * w) for _ in range(2)] for w in (A_W, B_W)]
        pos_r = [carve(CHUNK).bitcast(I32) for _ in range(2)]
        blank = [carve(GT * w) for w in (A_W, B_W)]

        s_in = sem("s_in")
        s_nodes = sem("s_nodes")
        s_wz = sem("s_wz")
        s_w = sem("s_w")
        s_wf = sem("s_wf")
        s_const = sem("s_const")
        s_cz = sem("s_cz")
        s_blank = sem("s_blank")
        s_init = sem("s_init")
        s_lz = sem("s_lz")
        s_lw = sem("s_lw")
        s_lf = sem("s_lf")
        s_bz = sem("s_bz")
        s_chain = sem("s_chain")
        s_sq = sem("s_sq")
        s_rt = sem("s_rt")
        s_cnt = [sem(f"s_cnt{o}") for o in range(2)]
        s_cum = [sem(f"s_cum{o}") for o in range(2)]
        s_eq = [sem(f"s_eq{o}") for o in range(2)]
        s_scan = [sem(f"s_scan{o}") for o in range(2)]
        s_pick = [sem(f"s_pick{o}") for o in range(2)]
        s_tb = [sem(f"s_tb{o}") for o in range(2)]
        s_tbd = [sem(f"s_tbd{o}") for o in range(2)]
        s_tbs = [sem(f"s_tbs{o}") for o in range(2)]
        s_pos = [sem(f"s_pos{o}") for o in range(2)]
        s_falls = sem("s_falls")
        s_flag_sum = sem("s_flag_sum")
        s_again = sem("s_again")
        s_flag = sem("s_flag")
        s_start = sem("s_start")
        s_startd = sem("s_startd")
        s_starts = sem("s_starts")
        s_nodes_of = sem("s_nodes_of")
        s_stage = [[sem(f"s_stage{o}{q}") for q in range(2)] for o in range(2)]
        s_fill = [sem(f"s_fill{o}") for o in range(2)]
        s_given = [sem(f"s_given{q}") for q in range(2)]
        s_empty = sem("s_empty")
        s_scat = [sem(f"s_scat{q}") for q in range(2)]
        s_copy = [sem(f"s_copy{q}") for q in range(2)]
        s_ranked = sem("s_ranked")
        s_placed = sem("s_placed")
        s_gp = sem("s_gp")

        def signals(names, n):
            return {k: Signal(sem(f"s_{k}_{n}"), 0) for k in names.split()}

        s_p = [signals("ht hts htv m tab" if n != 2 else "", n)
               for n in range(4)]
        s_e = [signals("rows0 rows1 ga0 ga1 zero" + (" tr tc m1 hid w prod" if n != 2 else ""), n) for n in range(4)]
        s_c = [signals({0: "t1 sig t2", 2: "ms mv fin"}.get(n, ""), n) for n in range(4)]
        for names, where, each in (("stat h side", s_p, BLOCKS), ("var root rstd", s_p, 1), ("td0", s_p, 16 * ((BLOCKS + 1) // 2)),
                                   ("td1", s_p, 16 * (BLOCKS // 2)), ("oh sel", s_e, GROUPS), ("key", s_e[1:], GROUPS), ("sc fl", s_e, TILES), ("stg trn ca cd big ev", s_c, BLOCKS)):
            for k in names.split():
                shared = sem(f"s_{k}")
                for n in range(len(where)):
                    where[n][k] = Signal(shared, each * n)
        s_apart = {e: sem(f"s_apart_{e}") for e in ("pool", "pe", "dve", "sp")}
        s_fin = sem("s_fin")
        s_trig = sem("s_trig")
        s_out = sem("s_out")

        loads = []
        for half in range(2):
            loads.append((w1[0][64 * half:64 * half + 64, 64 * half:64 * half + 64], t["L0_gnn_W_fc1"]))
            loads.append((w2[0][64 * half:64 * half + 64, half, :], t["L0_gnn_W_fc2"]))
            loads.append((w2[3][64 * half:64 * half + 64, half, :], t["L3_gnn_fcW2"]))
        for i in range(4):
            loads.append((w1[1][32 * i + B_10:32 * i + B_10 + 10, i, :], t["L1_gnn_W_fc1"]))
            loads.append((w1[3][32 * i + B_8:32 * i + B_8 + 8, i // 2, 64 * (i % 2):64 * (i % 2) + 64], t["L3_gnn_fcW1"]))
        loads.append((w2[1][0:100, :], t["L1_gnn_W_fc2"]))
        late = []
        for n in range(4):
            for name, a, b, c, k, r, col, _factor in sum_weights(n):
                (late if n else loads).append((wsum[n][r:r + b - a, c, k, col:col + t[name].shape[1]], t[name][a:b, :]))
        for n, (ts, tv, ks, kv) in {0: ("L0_gnn_W_nl0", "L0_gnn_W_nl1", "L0_gnn_W_skip0", "L0_gnn_W_skip1"),
                                    1: ("L1_gnn_W_l1_0", "L1_gnn_W_l1_1", "L1_gnn_W_si0", "L1_gnn_W_si1"),
                                    3: ("L3_gnn_W1_s", "L3_gnn_W1_v", "L3_gnn_W_sc_s", "L3_gnn_W_sc_v")}.items():
            loads.append((wps[n][:, 0:64], t[ts]))
            loads.append((wps[n][:, 64:64 + LAYERS[n].tab_side], t[ks]))
            for i in range(3):
                loads.append((wpv[n][32 * i:32 * i + 32, 32 * i:32 * i + 32], t[tv]))
                loads.append((wpv[n][32 * i:32 * i + 32, 96 + 32 * i:128 + 32 * i], t[kv]))
        loads.append((w2s[:, :], t["L2_gnn_Ws"]))
        for i in range(3):
            loads.append((w2v[32 * i:32 * i + 32, 32 * i:32 * i + 32], t["L2_gnn_Wv"]))

        def sum_factors(n):
            return [(wsum[n][r:r + b - a, c, k, col:col + t[name].shape[1]], f)
                    for name, a, b, c, k, r, col, f in sum_weights(n) if f != 1.0]

        def by_bin(a):
            return a.rearrange("p (b k m) -> p k b m", b=4, k=4)

        def by_kind(a):
            return a.rearrange("p (k b m) -> p k b m", b=4, k=4)

        def rows_a(q):
            flat = rows[q][:, :, :].rearrange("p t c -> p (t c)")
            return flat[:, 0:GT * 64], flat[:, GT * 64:GT * A_W].rearrange("p (t c) -> p t c", t=GT)

        def rows_b(q):
            return rows[q][:, :, :].rearrange("p t c -> p (t c)")[:, 0:GT * B_W]

        def scratch(i):
            return small[:, i, :]

        RSTD, NMR = 0, 1

        def xj(j, n=1):
            return x[:, bass.ds(j * NF, n * NF)]

        def sj(j):
            return side[:, bass.ds(j * 192, 192)]

        block = ctx.enter_context(nc.Block())

        @block.sync
        def _(sp):
            sp.dma_start(key_i[0], t["skey"]).then_inc(s_in, 16)
            sp.dma_start(sh, t["edge_attr_3"]).then_inc(s_in, 16)
            sp.dma_start(key_i[1], t["dkey"][0:P * COLS].rearrange("(p c) -> p c", p=P)).then_inc(s_in, 16)
            sp.dma_start(key_next, t["dkey"][1:P * COLS + 1].rearrange("(p c) -> p c", p=P)).then_inc(s_in, 16)

            def given(c, half, q):
                if within(c, CHUNKS):
                    wait(sp, s_given[q], half * 16)
                    sp.sem_inc(s_apart["sp"], 1)
                    sp.dma_start(stage[1][q], t["rows_b"][:, bass.ds(c * (CHUNK * B_W), CHUNK * B_W)]).then_inc(s_stage[1][q], 16)
                if within(c - 1, CHUNKS):
                    wait(sp, s_fill[1], c * 2)
                    sp.sem_inc(s_apart["sp"], 1)
                    sp.dma_start(given_dram[0:P * COLS, :].rearrange("(p c) w -> p (c w)", p=P)[:, bass.ds((c - 1) * (CHUNK * B_W), CHUNK * B_W)],
                                 stage[1][1 - q]).then_inc(s_given[1 - q], 16)
            sp.wait_ge(s_in, 64)
            pipeline(sp, CHUNKS, 2, 0, 1, given)
            sp.dma_start(x[:, :].rearrange("p (j c) -> p j c", j=BLOCKS),
                         t["x"].rearrange("(j p) c -> p j c", p=P)).then_inc(s_nodes, 16)
            with nc.allow_non_contiguous_dma(reason="one word per node"):
                sp.dma_start(attr[:, :], t["node_vec1"].rearrange("(j p) c -> p (j c)", p=P)).then_inc(s_nodes, 16)

            def tables(n):
                S = s_p[n]

                def body(j, half, q):
                    if n == 2:
                        wait(sp, S["h"], j + 1)
                    else:
                        wait(sp, S["tab"], j + 1)
                    sp.sem_inc(s_apart["sp"], 1)
                    src = hbuf[q] if n == 2 else trow[q]
                    sp.dma_start(table_dram[n].rearrange("(j p) c -> p j c", p=P)[:, bass.ds(j, 1), :],
                                 src[:, :].unsqueeze(1)).then_inc(S[f"td{q}"].sem, 16)
                pipeline(sp, BLOCKS, 3, 0, 0, body)

            def bins_out(o):
                sp.wait_ge(s_tb[o], 1)
                with nc.allow_non_contiguous_dma(reason="one word per tile"):
                    sp.dma_start(bins_dram[o].rearrange("(c p) -> p c", p=P), tile_bin_i).then_inc(s_tbd[o], 16)
                sp.wait_ge(s_tbd[o], 16)

            def bins_in(o):
                if o:
                    wait(sp, s_e[0]["fl"], TILES)
                sp.wait_ge(s_bz, 1)
                sp.dma_start(tile_bins[0:1, RING:], bins_dram[o].rearrange("(a c) -> a c", a=1)).then_inc(s_tbs[o], 16)

            def starts():
                sp.wait_ge(s_start, 1)
                with nc.allow_non_contiguous_dma(reason="one word per tile"):
                    sp.dma_start(starts_dram.rearrange("(c p) -> p c", p=P), tile_start).then_inc(s_startd, 16)
                    sp.dma_start(first_node_dram.rearrange("(c p) -> p c", p=P), tile_node).then_inc(s_startd, 16)
                sp.wait_ge(s_startd, 32)
                sp.dma_start(starts_row[0:1, :], starts_dram.rearrange("(a c) -> a c", a=1)).then_inc(s_starts, 16)
                sp.wait_ge(s_starts, 16)

            def stage_rows(c, half, q):
                wait(sp, s_scat[q], half * (16 * CHUNK))
                sp.sem_inc(s_apart["sp"], 1)
                sp.dma_start(stage[0][q], t["rows_a"][:, bass.ds(c * (CHUNK * A_W), CHUNK * A_W)]).then_inc(s_stage[0][q], 16)

            tiles_b = rows_dram[1].rearrange("(g p t) c -> p g t c", p=P, t=GT)

            def copy_tiles(half, q):
                for v in range(SPREAD):
                    u = SPREAD * q + v
                    _, (start,) = nc.values_load_multi_w_load_instructions(
                        starts_row[0:1, bass.ds((half - 1) * (2 * SPREAD) + u, 1)], engines=(SP,),
                        min_val=0, max_val=P * COLS,
                        skip_runtime_bounds_check_because="clamped to the number of edges")
                    sp.dma_start(tiles_b[:, bass.ds((half - 1) * (2 * SPREAD // GT) + u // GT, 1), u % GT, :],
                                 given_dram[bass.ds(start, P), :].unsqueeze(1)).then_inc(s_copy[q], 16)

            def edge_rows(n):
                S, L = s_e[n], LAYERS[n]
                o, w = (0, A_W) if L.rowsA else (1, B_W)
                if n == 0:
                    for q in range(2):
                        sp.wait_ge(s_scat[q], 16 * CHUNK * (CHUNKS // 2))
                src = rows_dram[o].rearrange("(g p t) c -> p g (t c)", p=P, t=GT)

                def body(g, half, q):
                    wait(sp, S[f"ga{q}"], half * (16 * GT))
                    sp.sem_inc(s_apart["sp"], 1)
                    wait(sp, S["sel"], g - 1)
                    sp.sem_inc(s_apart["sp"], 1)
                    if L.mlp:
                        wait(sp, S["tr"], g - 1)
                    sp.sem_inc(s_apart["sp"], 1)
                    if L.rowsA:
                        one = src[:, bass.ds(g, 1), :].rearrange("p g (t c) -> p (g t) c", t=GT)
                        ef, rest = rows_a(q)
                        sp.dma_start(ef.rearrange("p (t c) -> p t c", t=GT), one[:, :, 0:A_SH]).then_inc(S[f"rows{q}"].sem, 16)
                        sp.dma_start(rest, one[:, :, A_SH:A_W]).then_inc(S[f"rows{q}"].sem, 16)
                    else:
                        sp.dma_start(rows_b(q).unsqueeze(1), src[:, bass.ds(g, 1), :]).then_inc(S[f"rows{q}"].sem, 16)
                if n:
                    sp.wait_ge(s_placed, 1)
                    wait(sp, s_e[n - 1]["sel"], GROUPS)
                    wait(sp, s_e[n - 1]["ga0"], 16 * GT * (GROUPS // 2))
                    wait(sp, s_e[n - 1]["ga1"], 16 * GT * (GROUPS // 2))
                    if LAYERS[n - 1].mlp:
                        wait(sp, s_e[n - 1]["tr"], GROUPS)
                pipeline(sp, GROUPS, 2, 0, 0, body)

            bins_out(0)
            for c in range(2):
                stage_rows(c, 0, c)
            bins_out(1)
            starts()
            for q in range(2):
                sp.wait_ge(s_given[q], 16 * (CHUNKS // 2))
            sp.wait_ge(s_empty, 16)

            def rows_and_tiles(c, half, q):
                stage_rows(c, half, q)
                copy_tiles(half, q)
            pairs(sp, 2, CHUNKS, rows_and_tiles)
            bins_in(0)
            edge_rows(0)
            bins_in(1)
            wait(sp, s_c[0]["stg"], BLOCKS)
            sp.dma_start(first_node, first_node_dram.rearrange("(a c) -> a c", a=1).to_broadcast([P, TCOLS * P])).then_inc(s_nodes_of, 16)
            sp.wait_ge(s_lz, 1)
            for dst, src in late:
                sp.dma_start(dst, src).then_inc(s_lw, 16)
            for n in range(1, 4):
                tables(n)
                edge_rows(n)
            sp.wait_ge(s_fin, 1)
            sp.dma_start(t["out"].rearrange("(j p) c -> p j c", p=P),
                         x[:, :].rearrange("p (j c) -> p j c", j=BLOCKS)).then_inc(s_out, 16)
            sp.wait_ge(s_out, 16)
            for n in range(4):
                for q in range(2):
                    wait(sp, s_p[n][f"td{q}"], 16 * ((BLOCKS + 1 - q) // 2))

        @block.gpsimd
        def _(pool):
            for o, w in enumerate((A_W, B_W)):
                pool.memset(blank[o], 0.0).then_inc(s_blank, 1)
            pool.wait_ge(s_blank, 2)
            for o, (w, k) in enumerate(((A_W, A_KEY), (B_W, B_KEY))):
                pool.memset(blank[o].rearrange("p (t c) -> p t c", t=GT)[:, :, k:k + 1], -1.0).then_inc(s_blank, 1)
            pool.memset(ident[:, :], 0.0).then_inc(s_cz, 1)
            pool.memset(tri, 1.0).then_inc(s_cz, 1)
            pool.memset(ones, 1.0)
            pool.memset(bins_z, 0.0)
            pool.memset(zero_h, 0)
            pool.iota(iota_bin[:, :], pattern=[[1, BIN]], base=0, channel_multiplier=0,
                      allow_small_or_imprecise_dtypes=True)
            pool.iota(iota_bins[:, :], pattern=[[1, BINS]], base=0, channel_multiplier=0,
                      allow_small_or_imprecise_dtypes=True)
            pool.iota(tile_id, pattern=[[P, TCOLS]], base=0, channel_multiplier=1,
                      allow_small_or_imprecise_dtypes=True)
            pool.wait_ge(s_cz, 2)
            pool.affine_select(out=ident[:, :], in_=ident[:, :], compare_op=ALU.not_equal, fill=1.0, base=0,
                               pattern=[[-1, P]], channel_multiplier=1)
            pool.affine_select(out=tri, in_=tri, compare_op=ALU.is_gt, fill=0.0, base=0,
                               pattern=[[1, P]], channel_multiplier=-1).then_inc(s_const, 1)
            pool.memset(tile_bins[:, :], 0).then_inc(s_bz, 1)
            for ws in (w1, w2, wps, wpv):
                for m in ws.values():
                    pool.memset(m[...], 0.0)
            pool.memset(wsum[0][...], 0.0)
            pool.memset(w2v[:, :], 0.0).then_inc(s_wz, 1)
            pool.wait_ge(s_wz, 1)
            for dst, src in loads:
                pool.dma_start(dst, src).then_inc(s_w, 16)
            pool.wait_ge(s_w, 16 * len(loads))
            fac = [(w2[0][:, :, 64:128], R3), (w2[0][:, :, 192:224], R3 / R2),
                   (w2[1][:, 0:160], 0.1), (w2[1][:, 160:192], 0.1 / R3),
                   (w2[3][:, :, 0:160], 1 / 8), (w2[3][:, :, 160:192], 1 / 8 / R3),
                   (wps[1][:, :], 1 / 8), (wps[3][:, :], 1 / 8),
                   (wpv[1][:, :], 1 / math.sqrt(32)), (wpv[3][:, :], 1 / math.sqrt(32))]
            assert len(fac) + len(sum_factors(0)) == N_SCALED
            for i, (m, f) in enumerate(fac + sum_factors(0)):
                wait(pool, s_wf, i)
                pool.tensor_scalar(m, m, f, None, ALU.mult).then_inc(s_wf, 1)

            pool.wait_ge(s_wf, N_SCALED)
            pool.wait_ge(s_init, 16)

            def scatter(c, half, q):
                pool.wait_ge(s_fill[0], c * 4 + 4)
                pool.sem_inc(s_apart["pool"], 1)
                for u in range(CHUNK):
                    pool.indirect_dma_start(
                        rows_dram[0][:, :], bass.IndirectOffsetOnAxis(ap=pos_r[q][:, u:u + 1], axis=0),
                        stage[0][q][:, u * A_W:(u + 1) * A_W], None).then_inc(s_scat[q], 16)
            pipeline(pool, CHUNKS, 2, 0, 0, scatter)
            for q in range(2):
                pool.wait_ge(s_scat[q], 16 * CHUNK * (CHUNKS // 2))
                pool.wait_ge(s_copy[q], 16 * SPREAD * (CHUNKS // 2 - 1))
            pool.wait_ge(s_flag, 1)
            _, (flag,) = nc.values_load_multi_w_load_instructions(
                unsorted[0:1, 0:1], engines=(POOL,), min_val=0, max_val=P * COLS,
                skip_runtime_bounds_check_because="a count of edges")
            with pool.If(flag != 0):
                pool.wait_ge(s_pos[1], 1)
                pool.dma_start(rows_dram[1].rearrange("(g p t) c -> p g (t c)", p=P, t=GT),
                               blank[1].unsqueeze(1).to_broadcast([P, TCOLS * P // GT, GT * B_W])).then_inc(s_gp, 16)
                pool.wait_ge(s_gp, 16)
                with pool.Fori(0, CHUNKS) as c:
                    pool.dma_start(stage[1][0], given_dram[0:P * COLS, :].rearrange("(p c) w -> p (c w)", p=P)[:, bass.ds(c * (CHUNK * B_W), CHUNK * B_W)]).then_inc(s_gp, 16)
                    pool.tensor_copy(pos_r[0], pos_i[1][:, bass.ds(c * CHUNK, CHUNK)]).then_inc(s_gp, 1)
                    pool.wait_ge(s_gp, c * (17 + 16 * CHUNK) + 33)
                    pool.sem_inc(s_apart["pool"], 1)
                    for u in range(CHUNK):
                        pool.indirect_dma_start(
                            rows_dram[1][:, :], bass.IndirectOffsetOnAxis(ap=pos_r[0][:, u:u + 1], axis=0),
                            stage[1][0][:, u * B_W:(u + 1) * B_W], None).then_inc(s_gp, 16)
                    pool.wait_ge(s_gp, c * (17 + 16 * CHUNK) + 33 + 16 * CHUNK)
            pool.sem_inc(s_placed, 1)
            pool.wait_ge(s_ranked, 1)

            for n in range(4):
                L, S = LAYERS[n], s_e[n]
                if n:
                    wait(pool, s_c[n - 1]["stg"], BLOCKS)
                else:
                    pool.wait_ge(s_tbd[0], 16)
                    pool.wait_ge(s_tbd[1], 16)
                    pool.wait_ge(s_startd, 32)
                pool.memset(acc[:, 0:BINS * L.width], 0.0).then_inc(S["zero"].sem, 1)
                if n == 1:
                    pool.memset(acc[:, tail:], 0.0).then_inc(s_lz, 1)
                for q in range(2):
                    wait(pool, s_p[n][f"td{q}"], 16 * ((BLOCKS + 1 - q) // 2))
                if n:
                    wait(pool, s_e[n - 1]["sc"], TILES)

                def body(g, half, q, n=n, L=L, S=S):
                    wait(pool, S[f"rows{q}"], (half + 1) * (32 if n == 0 else 16))
                    wait(pool, S["prod"] if L.mlp else S["sc"], (g - 1) * GT)
                    pool.sem_inc(s_apart["pool"], 1)
                    first, w = (GT * 64 + A_IDX - A_SH, A_W - A_SH) if L.rowsA else (B_IDX, B_W)
                    flat = rows[q][:, :, :].rearrange("p t c -> p (t c)")
                    for u in range(GT):
                        pool.indirect_dma_start(
                            gath[q][:, u, :], None, table_dram[n][:, :],
                            bass.IndirectOffsetOnAxis(ap=flat[:, u * w + first:u * w + first + 1].bitcast(I32), axis=0)).then_inc(S[f"ga{q}"].sem, 16)
                pipeline(pool, GROUPS, 2, 0, 0, body)

                C = s_c[n]
                wait(pool, S["fl"], TILES)
                w4 = 4 * L.width

                def stage_sums(j, half, q, C=C, w4=w4):
                    wait(pool, C["trn"], j - 1)
                    pool.sem_inc(s_apart["pool"], 1)
                    pool.tensor_copy(stg[q][:, 0:w4], acc[:, bass.ds(j * w4, w4)]).then_inc(C["stg"].sem, 1)
                pipeline(pool, BLOCKS, 3, 2, 0, stage_sums)

        @block.scalar
        def _(act):
            act.wait_ge(s_blank, 4)
            act.dma_start(given_dram[P * COLS:, :], blank[1][:, 0:B_W]).then_inc(s_empty, 16)
            act.dma_start(rows_dram[0].rearrange("(g p t) c -> p g (t c)", p=P, t=GT),
                          blank[0].unsqueeze(1).to_broadcast([P, GROUPS, GT * A_W])).then_inc(s_init, 16)
            act.wait_ge(s_sq, 1)
            act.activation(norm, norm, ACT.Sqrt).then_inc(s_rt, 1)

            def complete(c, half, q):
                wait(act, s_stage[1][q], half * 16 + 16)
                st = stage[1][q].rearrange("p (u c) -> p u c", c=B_W)
                at = bass.ds(c * CHUNK, CHUNK)
                act.activation(st[:, :, B_IDX:B_IDX + 1].bitcast(I32), key_i[0][:, at].unsqueeze(2),
                               ACT.Copy).then_inc(s_fill[1], 1)
                act.activation(st[:, :, B_KEY:B_KEY + 1], key_i[1][:, at].unsqueeze(2), ACT.Copy).then_inc(s_fill[1], 1)
            act.wait_ge(s_in, 64)
            pairs(act, 0, CHUNKS, complete)

            def prep(n):
                S = s_p[n]
                wait(act, S["var"], 1)
                act.activation(scratch(4), scratch(4), ACT.Sqrt).then_inc(S["root"].sem, 1)
                wait(act, S["rstd"], 1)

                def body(j, half, q):
                    if within(j, BLOCKS):
                        if n == 2:
                            wait(act, S[f"td{q}"], half * 16)
                            wait(act, S["side"], j - 1)
                        else:
                            wait(act, S["ht"], j - 1)
                        act.activation(hbuf[q][:, :], xj(j), ACT.Relu, bias=small[:, NMR, bass.ds(j, 1)],
                                       scale=small[:, RSTD, bass.ds(j, 1)]).then_inc(S["h"].sem, 1)
                    if n != 2 and within(j - 1, BLOCKS):
                        wait(act, S["ht"], j)
                        act.activation(hT[1 - q][0:96, 128:256], bank(5 - q, 96, 0, 128), ACT.Copy).then_inc(S["htv"].sem, 1)
                    if n != 2 and within(j - 2, BLOCKS):
                        wait(act, S["m"], j - 1)
                        wait(act, S[f"td{q}"], half * 16 - 16)
                        act.activation(trow[q][:, :], bank(6 + q, P, 0, NF), ACT.Copy,
                                       scale=1.0 if n == 0 else attr[:, bass.ds(j - 2, 1)]).then_inc(S["tab"].sem, 1)
                        if n == 0:
                            wait(act, S["tab"], j - 1)
                            act.dma_start(table_dram[0].rearrange("(j p) c -> p j c", p=P)[:, bass.ds(j - 2, 1), :],
                                          trow[q][:, :].unsqueeze(1)).then_inc(S[f"td{q}"].sem, 16)
                return body

            def prep_all(n):
                pipeline(act, BLOCKS, 3, 2, 2, prep(n))

            def fill(c, half, q):
                wait(act, s_stage[0][q], half * 16 + 16)
                st = stage[0][q].rearrange("p (u c) -> p u c", c=A_W)
                at = bass.ds(c * CHUNK, CHUNK)
                act.activation(st[:, :, A_SH:A_SH + 3],
                               sh[:, bass.ds(c * (3 * CHUNK), 3 * CHUNK)].rearrange("p (u c) -> p u c", c=3),
                               ACT.Copy).then_inc(s_fill[0], 1)
                act.activation(st[:, :, A_IDX:A_IDX + 1].bitcast(I32), key_i[1][:, at].unsqueeze(2),
                               ACT.Copy).then_inc(s_fill[0], 1)
                act.activation(st[:, :, A_KEY:A_KEY + 1], key_f[:, at].unsqueeze(2), ACT.Copy).then_inc(s_fill[0], 1)
                act.activation(pos_r[q], pos_i[0][:, at], ACT.Copy).then_inc(s_fill[0], 1)

            act.wait_ge(s_pos[0], 1)
            pairs(act, 0, SEGMENTS[1], fill)
            act.wait_ge(s_pos[0], 2)
            pairs(act, SEGMENTS[1], SEGMENTS[2], fill)
            act.wait_ge(s_pos[0], 3)
            act.wait_ge(s_nodes, 32)
            prep_step = prep(0)

            def fill_and_prep(c, half, q):
                fill(c, half, q)
                step, at = (c - PREP_FROM) * 2, (c - PREP_FROM)
                for v in range(2):
                    if not is_static(c) or step + v < BLOCKS + 2:
                        prep_step(step + v, at, v)
            for c in range(PREP_FROM, PREP_FROM + 2):
                fill_and_prep(c, c // 2, c % 2)
            last = PREP_FROM + (BLOCKS - 1) // 2 // 2 * 2
            pairs(act, PREP_FROM + 2, last, fill_and_prep)
            for c in range(last, last + 2):
                fill_and_prep(c, c // 2, c % 2)
            pairs(act, last + 2, CHUNKS, fill)

            for n in range(4):
                L, S, C = LAYERS[n], s_e[n], s_c[n]
                if L.mlp:
                    tcols = 512 if n == 0 else 256
                    hrows = 100 if n == 1 else P

                    def body(g, half, q, n=n, S=S, tcols=tcols, hrows=hrows):
                        wait(act, S["tr"], g + 1)
                        act.activation(attrT[:, 0:tcols], bank(0, P, 0, tcols), ACT.Copy).then_inc(S["tc"].sem, 1)
                        wait(act, S["m1"], g + 1)
                        for b in range(2 if n == 1 else 1):
                            i = act.activation(hidT[q][0:hrows, 512 * b:512 * b + 512], bank(2 + b, hrows, 0, 512),
                                               ACT.Silu if n == 3 else ACT.Relu,
                                               scale={0: 1.0, 1: R2 / math.sqrt(10.0), 3: 1 / math.sqrt(8.0)}[n])
                        i.then_inc(S["hid"].sem, 1)
                    pipeline(act, GROUPS, 2, 2, 0, body)

                (a0, a1) = L.chunks[0]

                def combine(j, half, q, n=n, C=C, a0=a0, a1=a1):
                    if within(j, BLOCKS):
                        wait(act, C["trn"], j + 1)
                        act.activation(by_kind(sumT[q][0:a1 - a0, 0, :]), by_bin(bank(0, a1 - a0, 0, 512)), ACT.Copy).then_inc(C["ca"].sem, 1)
                    if within(j - 1, BLOCKS):
                        if n == 0:
                            wait(act, C["t1"], j)
                            act.activation(hbuf[1 - q][:, 0:96], tmp[1 - q][:, 0:96], ACT.Sigmoid).then_inc(C["sig"].sem, 1)
                        if n == 2:
                            wait(act, C["big"], j)
                            act.activation(hT[1 - q][0:64, 0:128], bank(3 - q, 64, 0, 128), ACT.Copy,
                                           scale=1 / math.sqrt(96.0) / 8).then_inc(C["ms"].sem, 1)
                pipeline(act, BLOCKS, 3, 2, 1, combine)
                if n < 3:
                    prep_all(n + 1)
            act.wait_ge(s_trig, 1)
            act.activation(scratch(4), scratch(2), ACT.Sin)
            act.activation(scratch(5), scratch(3), ACT.Sin).then_inc(s_trig, 1)

        @block.vector
        def _(dve):
            links = [0]

            def link(ins):
                links[0] += 1
                ins.then_inc(s_chain, 1)
                dve.wait_ge(s_chain, links[0])

            dve.wait_ge(s_in, 64)
            sh3 = sh.rearrange("p (e c) -> p e c", c=3)
            link(dve.tensor_tensor(sh2, sh, sh, ALU.mult))
            dve.tensor_reduce(norm, sh2.rearrange("p (e c) -> p e c", c=3), AX_X, ALU.add).then_inc(s_sq, 1)
            dve.wait_ge(s_rt, 1)
            link(dve.reciprocal(norm, norm))
            link(dve.tensor_tensor(sh3, sh3, norm.unsqueeze(2).to_broadcast([P, COLS, 3]), ALU.mult))

            def statistics(n):
                S = s_p[n]
                with dve.Fori(0, BLOCKS) as j:
                    dve.bn_stats(stats[:, bass.ds(j, 1), :].rearrange("p j c -> p (j c)"), xj(j)).then_inc(S["stat"].sem, 1)
                wait(dve, S["stat"], BLOCKS)
                me, ve, mo, vo = (stats[:, :, i] for i in (1, 2, 4, 5))
                link(dve.tensor_tensor(scratch(2), me, mo, ALU.add))
                link(dve.tensor_tensor(scratch(3), me, mo, ALU.subtract))
                link(dve.tensor_tensor(scratch(4), ve, vo, ALU.add))
                link(dve.tensor_tensor(scratch(3), scratch(3), scratch(3), ALU.mult))
                link(dve.tensor_scalar(scratch(4), scratch(4), 1 / NF, EPS, ALU.mult, ALU.add))
                dve.scalar_tensor_tensor(out=scratch(4), in0=scratch(3), scalar=0.25, in1=scratch(4),
                                         op0=ALU.mult, op1=ALU.add).then_inc(S["var"].sem, 1)
                wait(dve, S["root"], 1)
                link(dve.reciprocal(scratch(RSTD), scratch(4)))
                dve.scalar_tensor_tensor(out=scratch(NMR), in0=scratch(2), scalar=-0.5, in1=scratch(RSTD),
                                         op0=ALU.mult, op1=ALU.mult).then_inc(S["rstd"].sem, 1)

            def prep(n):
                S = s_p[n]

                def body(j, half, q):
                    if n == 2:
                        if within(j, BLOCKS):
                            wait(dve, S["h"], j + 1)
                            dve.tensor_tensor(xj(j), xj(j), hbuf[q][:, :], ALU.add).then_inc(S["side"].sem, 1)
                        return
                    if within(j - 1, BLOCKS):
                        wait(dve, S["ht"], j)
                        dve.tensor_copy(hT[1 - q][0:64, 0:128], bank(3 - q, 64, 0, 128)).then_inc(S["hts"].sem, 1)
                    if within(j - 2, BLOCKS):
                        wait(dve, S["m"], j - 1)
                        if n == 0:
                            dve.tensor_copy(sj(j - 2), bank(q, P, 0, 192)).then_inc(S["side"].sem, 1)
                        elif n == 1:
                            dve.scalar_tensor_tensor(out=xj(j - 2), in0=bank(q, P, 0, NF),
                                                     scalar=attr[:, bass.ds(j - 2, 1)], in1=xj(j - 2),
                                                     op0=ALU.mult, op1=ALU.add).then_inc(S["side"].sem, 1)
                        else:
                            dve.tensor_scalar(side[:, bass.ds((j - 2) * 192, NF)], bank(q, P, 0, NF),
                                              attr[:, bass.ds(j - 2, 1)], None, ALU.mult).then_inc(S["side"].sem, 1)
                pipeline(dve, BLOCKS, 3, 2, 2, body)

            def places(o):
                link(dve.tensor_scalar(int_a, key_i[o], 5, None, ALU.arith_shift_right))
                link(dve.tensor_copy(bin_h[o], int_a))
                if o == 0:
                    link(dve.tensor_scalar(int_b, key_i[o], BIN - 1, None, ALU.bitwise_and))
                    link(dve.tensor_copy(key_f, int_b))
                with dve.Fori(0, BINS) as b:
                    dve.tensor_scalar(eq, bin_h[o], iota_bins[:, bass.ds(b, 1)], 0.0, ALU.is_equal, ALU.add,
                                      accum_out=count[:, bass.ds(b, 1)]).then_inc(s_cnt[o], 1)
                    dve.wait_ge(s_cnt[o], b + 1)
                dve.wait_ge(s_cum[o], 1)
                link(dve.tensor_scalar(bins_i, bank(0, P, 128, 128 + BINS), float(P - 1), None, ALU.add))
                link(dve.tensor_scalar(bins_i, bins_i, 7, None, ALU.arith_shift_right))
                link(dve.tensor_copy(ntile, bins_i))
                if o:
                    link(dve.scalar_tensor_tensor(out=pad, in0=ntile, scalar=float(P), in1=bank(0, P, 128, 128 + BINS),
                                                  op0=ALU.mult, op1=ALU.subtract))
                link(dve.tensor_tensor_scan(first_tile, ntile, bins_z, 0.0, ALU.add, ALU.add))
                link(dve.tensor_tensor(first_tile, first_tile, ntile, ALU.subtract))
                link(dve.tensor_scalar(bins_f, first_tile, float(P), -1.0, ALU.mult, ALU.add))
                link(dve.tensor_tensor(base[o], bins_f, bank(0, P, 0, BINS), ALU.add))
                for c in range(TCOLS):
                    link(dve.tensor_scalar(bins_f, first_tile, tile_id[:, c:c + 1], 0.0, ALU.is_le, ALU.add,
                                           accum_out=tile_bin[:, c:c + 1]))
                if o:
                    dve.wait_ge(s_tbd[0], 16)
                dve.tensor_scalar(tile_bin_i, tile_bin, -1.0, None, ALU.add).then_inc(s_tb[o], 1)
                if o:
                    shape = [P, TCOLS, BINS]
                    tiles = by_tile.rearrange("p (c b) -> p c b", c=TCOLS)
                    link(dve.tensor_scalar(tile_node, tile_bin, float(BIN), -float(BIN), ALU.mult, ALU.add))
                    link(dve.tensor_tensor(first_tile, first_tile, ntile, ALU.add))
                    link(dve.tensor_tensor(tiles, first_tile.unsqueeze(1).to_broadcast(shape),
                                           tile_id.unsqueeze(2).to_broadcast(shape), ALU.is_le))
                    link(dve.tensor_tensor(tiles, tiles, pad.unsqueeze(1).to_broadcast(shape), ALU.mult))
                    link(dve.tensor_reduce(tile_pad, tiles, AX_X, ALU.add))
                    link(dve.scalar_tensor_tensor(out=tile_pad, in0=tile_id, scalar=float(P), in1=tile_pad,
                                                  op0=ALU.mult, op1=ALU.subtract))
                    dve.tensor_scalar(tile_start, tile_pad, float(P * COLS), 0.0, ALU.min, ALU.max).then_inc(s_start, 1)

            links_of_rank = [0, 0]

            def rank(o, a, b, carry):
                w, done = b - a, links_of_rank[o]
                with dve.Fori(0, BINS) as i:
                    bin_base = base[o][:, bass.ds(i, 1)]
                    dve.tensor_scalar(eq[:, a:b], bin_h[o][:, a:b], iota_bins[:, bass.ds(i, 1)], None,
                                      ALU.is_equal).then_inc(s_eq[o], 1)
                    dve.wait_ge(s_eq[o], i + (done + 1))
                    dve.tensor_tensor_scan(wide[:, 0:w], eq[:, a:b], zero_h[:, a:b], bin_base,
                                           ALU.add, ALU.add).then_inc(s_scan[o], 1)
                    dve.wait_ge(s_scan[o], i + (done + 1))
                    dve.sem_inc(s_apart["dve"], 1)
                    if carry:
                        dve.tensor_copy(bin_base, wide[:, w - 1:w])
                    dve.copy_predicated(pos_f[:, a:b], eq[:, a:b], wide[:, 0:w]).then_inc(s_pick[o], 1)
                    dve.wait_ge(s_pick[o], i + (done + 1))
                links_of_rank[o] += BINS

            def positions(o, a, b):
                ia, ib, out = int_a[:, a:b], int_b[:, a:b], pos_i[o][:, a:b]
                link(dve.tensor_copy(ia, pos_f[:, a:b]))
                link(dve.tensor_scalar(out, ia, 10, 10, ALU.arith_shift_right, ALU.logical_shift_left))
                link(dve.tensor_scalar(ib, ia, P - 1, 3, ALU.bitwise_and, ALU.logical_shift_left))
                link(dve.tensor_tensor(out, out, ib, ALU.bitwise_or))
                link(dve.tensor_scalar(ib, ia, 7, GT - 1, ALU.arith_shift_right, ALU.bitwise_and))
                dve.tensor_tensor(out, out, ib, ALU.bitwise_or).then_inc(s_pos[o], 1)

            dve.wait_ge(s_const, 1)
            link(dve.memset(pos_f, 0.0))
            places(0)

            def segment(i):
                a, b = SEGMENTS[i] * CHUNK, SEGMENTS[i + 1] * CHUNK
                rank(0, a, b, b < COLS)
                positions(0, a, b)
                dve.wait_ge(s_pos[0], i + 1)
            segment(0)
            link(dve.tensor_tensor(int_a, key_i[1], key_next, ALU.is_gt))
            link(dve.tensor_copy(sh2[:, 0:COLS], int_a))
            dve.tensor_reduce(falls, sh2[:, 0:COLS], AX_X, ALU.add).then_inc(s_falls, 1)
            places(1)
            dve.wait_ge(s_flag_sum, 1)
            dve.tensor_copy(unsorted[0:1, :], bank(1, 1, 0, 1)).then_inc(s_flag, 1)
            segment(1)
            segment(2)
            dve.wait_ge(s_nodes, 32)
            statistics(0)
            prep(0)
            dve.wait_ge(s_flag, 1)
            _, (flag,) = nc.values_load_multi_w_load_instructions(
                unsorted[0:1, 0:1], engines=(DVE,), min_val=0, max_val=P * COLS,
                skip_runtime_bounds_check_because="a count of edges")
            wait(dve, s_p[0]["tab"], BLOCKS)
            with dve.If(flag != 0):
                dve.memset(pos_f, 0.0).then_inc(s_again, 1)
                dve.wait_ge(s_again, 1)
                rank(1, 0, COLS, False)
                dve.tensor_copy(int_a, pos_f).then_inc(s_again, 1)
                dve.wait_ge(s_again, 2)
                dve.tensor_scalar(pos_i[1], int_a, 10, 10, ALU.arith_shift_right, ALU.logical_shift_left)
                dve.tensor_scalar(int_b, int_a, P - 1, 3, ALU.bitwise_and, ALU.logical_shift_left).then_inc(s_again, 1)
                dve.wait_ge(s_again, 3)
                dve.tensor_tensor(pos_i[1], pos_i[1], int_b, ALU.bitwise_or).then_inc(s_again, 1)
                dve.wait_ge(s_again, 4)
                dve.tensor_scalar(int_b, int_a, 7, GT - 1, ALU.arith_shift_right, ALU.bitwise_and).then_inc(s_again, 1)
                dve.wait_ge(s_again, 5)
                dve.tensor_tensor(pos_i[1], pos_i[1], int_b, ALU.bitwise_or).then_inc(s_pos[1], 1)
                dve.wait_ge(s_pos[1], 1)
            dve.sem_inc(s_ranked, 1)

            for n in range(4):
                L, S, C = LAYERS[n], s_e[n], s_c[n]
                o = 0 if L.rowsA else 1
                wait(dve, S["zero"], 1)
                if n != 2:
                    for q in range(2):
                        link(dve.memset(sel[q][:, :, 32:128], 0.0))
                dve.wait_ge(s_tbs[o], 16)
                if n:
                    dve.wait_ge(s_nodes_of, 16)

                def select(g, half, q, n=n, L=L, S=S):
                    wait(dve, S[f"rows{q}"], (half + 1) * (32 if n == 0 else 16))
                    if L.rowsA:
                        r = rows_a(q)[1]
                        key, e0, e1 = r[:, :, A_KEY - A_SH], None, r[:, :, 0:3]
                    else:
                        r = rows_b(q).rearrange("p (t c) -> p t c", c=B_W)
                        e0, e1 = r[:, :, B_4], r[:, :, B_4 + 1:B_4 + 4]
                        key = small[:, 7 + q, 0:GT]
                        dve.tensor_tensor(key, r[:, :, B_KEY], first_node[:, bass.ds(g * GT, GT)],
                                          ALU.subtract).then_inc(S["key"].sem, 1)
                        wait(dve, S["key"], g + 1)
                    nodes = iota_bin[:, :].unsqueeze(1).to_broadcast([P, GT, BIN])
                    hot = sel[q][:, :, 0:BIN] if n == 0 else onehot[:, :, :]
                    dve.tensor_tensor(hot, nodes, key.unsqueeze(2).to_broadcast([P, GT, BIN]),
                                      ALU.is_equal).then_inc(S["oh"].sem, 1)
                    wait(dve, S["oh"], g + 1)
                    if n == 2:
                        dve.tensor_tensor(sel[q][:, :, 0:128].rearrange("p t (k b) -> p t k b", k=4),
                                          hot.unsqueeze(2).to_broadcast([P, GT, 4, BIN]),
                                          r[:, :, B_4:B_4 + 4].unsqueeze(3).to_broadcast([P, GT, 4, BIN]),
                                          ALU.mult).then_inc(S["sel"].sem, 1)
                        return
                    if n:
                        dve.tensor_tensor(sel[q][:, :, 0:BIN], hot, e0.unsqueeze(2).to_broadcast([P, GT, BIN]), ALU.mult)
                    dve.tensor_tensor(sel[q][:, :, 128:224].rearrange("p t (k b) -> p t k b", k=3),
                                      hot.unsqueeze(2).to_broadcast([P, GT, 3, BIN]),
                                      e1.unsqueeze(3).to_broadcast([P, GT, 3, BIN]), ALU.mult).then_inc(S["sel"].sem, 1)

                def edges(g, half, q, n=n, L=L, S=S, o=o, select=select):
                    _, at = nc.values_load_multi_w_load_instructions(
                        tile_bins[0:1, bass.ds(g * GT, GT)], engines=(DVE,), min_val=0, max_val=BINS - 1,
                        skip_runtime_bounds_check_because="counts of at most BINS bins, less one")
                    for u in range(0, GT, 2):
                        m = g * GT + u
                        b = u // 2 % 2
                        if within(m - LAG_FL, TILES):
                            wait(dve, S["sc"], m - LAG_FL + 2)
                            for h in range(2):
                                wait(dve, S["fl"], m - LAG_FL + h)
                                sums = acc[:, bass.ds(at[u + h] * L.width, L.width)]
                                dve.tensor_tensor(sums, sums, bank(6 + b, P, 256 * h, 256 * h + L.width),
                                                  ALU.add).then_inc(S["fl"].sem, 1)
                        if L.mlp and within(m, TILES):
                            if u == 0:
                                wait(dve, S[f"ga{q}"], half * (16 * GT) + 16 * GT)
                            wait(dve, S["w"], m + 2)
                            for h in range(2):
                                wt = bank(4 + b, P, 224 * h, 224 * h + L.wcols)
                                xs = gath[q][:, u + h, 0:S0]
                                xv = gath[q][:, u + h, S0:NF].rearrange("p (c m) -> p c m", c=3)
                                nv = (L.wcols - 128) // V1
                                a = (2 * b + h) * (416 if n == 0 else 320)
                                if n == 0:
                                    ps = prod[:, a:a + 704].rearrange("p (a c) -> p a c", a=2)[:, :, 0:S0]
                                    pv = prod[:, a + S0:a + S0 + 288].rearrange("p (w c m) -> p w c m", w=3, c=3)
                                else:
                                    both = prod[:, a:a + 320].rearrange("p (w c) -> p w c", w=2)
                                    ps, pv = both[:, :, 0:S0], both[:, :, S0:NF].rearrange("p w (c m) -> p w c m", c=3)
                                dve.tensor_tensor(ps, wt[:, 0:128].rearrange("p (w c) -> p w c", w=2),
                                                  xs.unsqueeze(1).to_broadcast([P, 2, S0]), ALU.mult)
                                ins = dve.tensor_tensor(pv, wt[:, 128:L.wcols].rearrange("p (w m) -> p w m", w=nv)
                                                        .unsqueeze(2).to_broadcast([P, nv, 3, V1]),
                                                        xv.unsqueeze(1).to_broadcast([P, nv, 3, V1]), ALU.mult)
                                ins.then_inc(S["prod"].sem, 1)
                        if u == LAG_FL and within(g + 1, GROUPS):
                            select(g + 1, half + q, 1 - q)
                        if is_static(g) and g == GROUPS and u == LAG_FL - 2:
                            break
                select(0, 0, 0)
                pipeline(dve, GROUPS, 2, 2, 1, edges)

                (b0, b1) = L.chunks[1]

                def combine(j, half, q, n=n, L=L, C=C, b0=b0, b1=b1):
                    if within(j, BLOCKS):
                        wait(dve, C["trn"], j + 1)
                        dve.tensor_copy(by_kind(sumT[q][0:b1 - b0, 1, :]), by_bin(bank(1, b1 - b0, 0, 512))).then_inc(C["cd"].sem, 1)
                    if within(j - 1, BLOCKS):
                        k, r = j - 1, 1 - q
                        po = pb[2 + r]
                        wait(dve, C["big"], j)
                        if n == 0:
                            dve.scalar_tensor_tensor(out=tmp[r][:, :], in0=po[:, 0:192], scalar=1 / 32.0, in1=sj(k),
                                                     op0=ALU.mult, op1=ALU.add).then_inc(C["t1"].sem, 1)
                            wait(dve, C["sig"], j)
                            dve.tensor_tensor(trow[r][:, 0:64], tmp[r][:, 0:64], hbuf[r][:, 0:64], ALU.mult)
                            dve.tensor_tensor(trow[r][:, 64:NF].rearrange("p (c m) -> p c m", c=3),
                                              tmp[r][:, 96:192].rearrange("p (c m) -> p c m", c=3),
                                              hbuf[r][:, 64:96].unsqueeze(1).to_broadcast([P, 3, V1]),
                                              ALU.mult).then_inc(C["t2"].sem, 1)
                            wait(dve, C["t2"], j)
                            dve.tensor_tensor(xj(k), xj(k), trow[r][:, :], ALU.add).then_inc(C["ev"].sem, 1)
                        elif n == 1:
                            dve.scalar_tensor_tensor(out=xj(k), in0=po[:, 0:NF], scalar=small[:, 6, bass.ds(k, 1)],
                                                     in1=xj(k), op0=ALU.mult, op1=ALU.add).then_inc(C["ev"].sem, 1)
                        elif n == 3:
                            dve.tensor_scalar(acc[:, bass.ds(k * (4 * NF), NF + 1)], po[:, 0:NF + 1],
                                              attr[:, bass.ds(k, 1)], 1 / math.sqrt(960.0), ALU.mult,
                                              ALU.mult).then_inc(C["ev"].sem, 1)
                        else:
                            dve.tensor_scalar(hT[r][0:96, 128:256], bank(6 + r, 96, 0, 128),
                                              math.sqrt(3.0 / 128) / R3 / math.sqrt(32.0), None, ALU.mult).then_inc(C["mv"].sem, 1)
                    if n == 2 and within(j - 2, BLOCKS):
                        wait(dve, C["fin"], j - 1)
                        dve.scalar_tensor_tensor(out=xj(j - 2), in0=bank(4 + q, P, 0, NF), scalar=0.0, in1=xj(j - 2),
                                                 op0=ALU.max, op1=ALU.add).then_inc(C["ev"].sem, 1)
                if n == 2:
                    dve.wait_ge(s_lw, 16 * len(late))
                    for m, f in sum_factors(2):
                        ins = dve.tensor_scalar(m, m, f, None, ALU.mult)
                    ins.then_inc(s_lf, 1)
                if n == 1:
                    link(dve.tensor_scalar(small[:, 6, :], attr[:, :], 0.125 / math.sqrt(96.0), None, ALU.mult))
                pipeline(dve, BLOCKS, 3, 2, 2 if n == 2 else 1, combine)
                wait(dve, C["ev"], BLOCKS)
                if n < 3:
                    statistics(n + 1)
                    prep(n + 1)

            conv = acc[:, 0:BLOCKS * 4 * NF].rearrange("p (j c) -> p j c", j=BLOCKS)
            sc = side[:, :].rearrange("p (j c) -> p j c", j=BLOCKS)[:, :, 0:NF]
            x3 = x[:, :].rearrange("p (j c) -> p j c", j=BLOCKS)
            big = 12582912.0
            wait(dve, s_p[3]["side"], BLOCKS)
            link(dve.tensor_scalar(scratch(2), conv[:, :, 0], 0.1, None, ALU.mult))
            link(dve.tensor_scalar(scratch(3), scratch(2), 1 / (2 * math.pi), big, ALU.mult, ALU.add))
            link(dve.tensor_scalar(scratch(3), scratch(3), -big, None, ALU.add))
            link(dve.scalar_tensor_tensor(out=scratch(2), in0=scratch(3), scalar=-6.28125, in1=scratch(2),
                                          op0=ALU.mult, op1=ALU.add))
            link(dve.scalar_tensor_tensor(out=scratch(2), in0=scratch(3), scalar=-(2 * math.pi - 6.28125),
                                          in1=scratch(2), op0=ALU.mult, op1=ALU.add))
            link(dve.tensor_scalar(scratch(2), scratch(2), 3.1415925, -3.1415925, ALU.min, ALU.max))
            link(dve.scalar_tensor_tensor(out=scratch(3), in0=scratch(2), scalar=-1.0, in1=scratch(2),
                                          op0=ALU.mult, op1=ALU.max))
            dve.tensor_scalar(scratch(3), scratch(3), -1.0, math.pi / 2, ALU.mult, ALU.add).then_inc(s_trig, 1)
            dve.wait_ge(s_trig, 2)
            shape = [P, BLOCKS, NF]
            link(dve.tensor_tensor(sc, sc, scratch(5).unsqueeze(2).to_broadcast(shape), ALU.mult))
            link(dve.tensor_tensor(x3, x3, sc, ALU.add))
            link(dve.tensor_tensor(conv[:, :, 1:NF + 1], conv[:, :, 1:NF + 1],
                                   scratch(4).unsqueeze(2).to_broadcast(shape), ALU.mult))
            dve.tensor_tensor(x3, x3, conv[:, :, 1:NF + 1], ALU.add).then_inc(s_fin, 1)

        @block.tensor
        def _(pe):
            pe.wait_ge(s_const, 1)

            def prep(n):
                if n == 2:
                    return
                S = s_p[n]
                ns = LAYERS[n].tab_side

                def body(j, half, q):
                    if within(j, BLOCKS):
                        wait(pe, S["h"], j + 1)
                        pe.sem_inc(s_apart["pe"], 1)
                        pe.transpose(bank(2 + q, 64, 0, 128), hbuf[q][:, 0:64], ident[:, :])
                        pe.transpose(bank(4 + q, 96, 0, 128), hbuf[q][:, 64:NF], ident[:, :]).then_inc(S["ht"].sem, 1)
                    if within(j - 1, BLOCKS):
                        r = 1 - q
                        wait(pe, S["hts"], j)
                        wait(pe, S["htv"], j)
                        wait(pe, S["tab"], j - 2)
                        wait(pe, S["side"], j - 2)
                        pe.sem_inc(s_apart["pe"], 1)
                        hs, hv = hT[r][0:64, 0:128], hT[r][0:96, 128:256]
                        pe.matmul(bank(6 + r, P, 0, 64), hs, wps[n][:, 0:64], start=True, stop=True, skip_group_check=True)
                        pe.matmul(bank(6 + r, P, 64, 160), hv, wpv[n][:, 0:96], start=False, stop=True, skip_group_check=True)
                        pe.matmul(bank(r, P, 0, ns), hs, wps[n][:, 64:64 + ns], start=True, stop=True, skip_group_check=True)
                        pe.matmul(bank(r, P, ns, 96 + ns), hv, wpv[n][:, 96:192], start=False, stop=True,
                                  skip_group_check=True).then_inc(S["m"].sem, 1)
                pipeline(pe, BLOCKS, 3, 2, 1, body)

            for o in range(2):
                if o:
                    pe.wait_ge(s_falls, 1)
                    pe.matmul(bank(1, 1, 0, 1), falls, ones[:, 0:1], start=True, stop=True).then_inc(s_flag_sum, 1)
                    pe.wait_ge(s_tb[0], 1)
                pe.wait_ge(s_cnt[o], BINS)
                pe.matmul(bank(0, P, 0, BINS), tri, count, start=True, stop=True)
                pe.matmul(bank(0, P, 128, 128 + BINS), ones, count, start=True, stop=True).then_inc(s_cum[o], 1)
            pe.wait_ge(s_flag, 1)
            pe.wait_ge(s_start, 1)
            pe.wait_ge(s_pos[0], 3)
            pe.wait_ge(s_w, 16 * len(loads))
            pe.wait_ge(s_wf, N_SCALED)
            prep(0)

            for n in range(4):
                L, S, C = LAYERS[n], s_e[n], s_c[n]
                pe.wait_ge(s_ranked, 1)
                if n:
                    wait(pe, s_c[n - 1]["ev"], BLOCKS)
                if n != 2:
                    wait(pe, s_p[n]["side"], BLOCKS)
                    wait(pe, s_p[n]["tab"], BLOCKS)

                def turn(g, half, q, n=n, S=S):
                    wait(pe, S[f"rows{q}"], (half + 1) * (32 if n == 0 else 16))
                    pe.sem_inc(s_apart["pe"], 1)
                    if n == 0:
                        for p in range(4):
                            i = pe.transpose(bank(0, P, 128 * p, 128 * p + 128), rows_a(q)[0][:, 128 * p:128 * p + 128], ident[:, :])
                    else:
                        for p in range(2):
                            i = pe.transpose(bank(0, P, 128 * p, 128 * p + 128), rows_b(q)[:, 128 * p:128 * p + 128], ident[:, :])
                    i.then_inc(S["tr"].sem, 1)

                def hidden(g, n=n, S=S):
                    wait(pe, S["tc"], g + 1)
                    if n == 0:
                        i = pe.matmul(bank(2, P, 0, 512), w1[0][:, :], attrT[:, 0:512], start=True, stop=True)
                    elif n == 1:
                        for k in range(4):
                            i = pe.matmul(bank(2 + k // 2, 100, 256 * (k % 2), 256 * (k % 2) + 256), w1[1][:, k, :],
                                          attrT[:, 0:256], start=True, stop=True)
                    else:
                        for k in range(2):
                            i = pe.matmul(bank(2, P, 256 * k, 256 * k + 256), w1[3][:, k, :], attrT[:, 0:256],
                                          start=True, stop=True)
                    i.then_inc(S["m1"].sem, 1)

                def hidden_of(u, q, n=n):
                    if n == 0:
                        return hidT[q][:, 128 * (u // 2):128 * (u // 2) + 128], w2[0][:, u % 2, :]
                    quad, k = u // 4, u % 4
                    if n == 1:
                        a = (k * 2 + quad) * 128
                        return hidT[q][0:100, a:a + 128], w2[1][0:100, :]
                    a = (k // 2 * 2 + quad) * 128
                    return hidT[q][:, a:a + 128], w2[3][:, k % 2, :]

                def edges(g, half, q, n=n, L=L, S=S, turn=turn, hidden=hidden, hidden_of=hidden_of):
                    lag = LAG_SC if L.mlp else 0
                    for u in range(0, GT, 2):
                        m = g * GT + u
                        if L.mlp and within(m, TILES):
                            if u == 0:
                                wait(pe, S["hid"], g + 1)
                            for h in range(2):
                                hid, w = hidden_of(u + h, q)
                                pe.matmul(bank(4 + u // 2 % 2, P, 224 * h, 224 * h + L.wcols), hid, w,
                                          start=True, stop=True, skip_group_check=True).then_inc(S["w"].sem, 1)
                        if within(m - lag, TILES):
                            v = (u - lag) % GT
                            b = v // 2 % 2
                            qv = q if u >= lag else 1 - q
                            if v == 0:
                                wait(pe, S["sel"], g + 1)
                                if not L.mlp:
                                    wait(pe, S[f"ga{q}"], half * (16 * GT) + 16 * GT)
                            if L.mlp:
                                wait(pe, S["prod"], m - lag + 2)
                            wait(pe, S["fl"], m - lag - RING + 2)
                            for h in range(2):
                                out = bank(6 + b, P, 256 * h, 256 * h + L.width)
                                if n == 2:
                                    ins = pe.matmul(out, sel[qv][:, v + h, 0:128], gath[qv][:, v + h, :],
                                                    start=True, stop=True, skip_group_check=True)
                                else:
                                    a = (2 * b + h) * (416 if n == 0 else 320)
                                    end = a + NF + L.width
                                    pe.matmul(out, sel[qv][:, v + h, 96:224], prod[:, a + NF:end], start=True, stop=False,
                                              skip_group_check=True)
                                    ins = pe.matmul(bank(6 + b, P, 256 * h, 256 * h + NF), sel[qv][:, v + h, 0:128],
                                                    prod[:, a:a + NF], start=False, stop=True, skip_group_check=True)
                                ins.then_inc(S["sc"].sem, 1)
                        if L.mlp and within(g + 1, GROUPS):
                            if u == 0:
                                turn(g + 1, half + q, 1 - q)
                            if u == 4:
                                hidden(g + 1)
                        if is_static(g) and g == GROUPS and u == lag - 2:
                            break
                if L.mlp:
                    turn(0, 0, 0)
                    hidden(0)
                pipeline(pe, GROUPS, 2, 2, 1 if L.mlp else 0, edges)

                wait(pe, S["fl"], TILES)
                if n:
                    pe.wait_ge(s_lw, 16 * len(late))
                if n == 2:
                    pe.wait_ge(s_lf, 1)
                order = sum_products(n)

                def combine(j, half, q, n=n, L=L, C=C, order=order):
                    if within(j, BLOCKS):
                        wait(pe, C["stg"], j + 1)
                        wait(pe, C["ca"], j)
                        wait(pe, C["cd"], j)
                        pe.sem_inc(s_apart["pe"], 1)
                        for c, (a, b) in enumerate(L.chunks):
                            for i in range(4):
                                ins = pe.transpose(bank(c, b - a, 128 * i, 128 * i + 128),
                                                   stg[q][:, L.width * i + a:L.width * i + b], ident[:, :])
                        ins.then_inc(C["trn"].sem, 1)
                    if within(j - 1, BLOCKS):
                        r = 1 - q
                        wait(pe, C["ca"], j)
                        wait(pe, C["cd"], j)
                        if n != 2:
                            wait(pe, C["ev"], j - 2)
                        pe.sem_inc(s_apart["pe"], 1)

                        def sums(c, k, rows_):
                            return sumT[r][0:rows_, c, 128 * k:128 * k + 128]
                        if n == 2:
                            for lo, hi, b0, terms in ((0, 64, 2, [(0, 0)] + [(1, k) for k in (1, 2, 3)]),
                                                      (64, 160, 6, [(0, k) for k in (1, 2, 3)] + [(1, k) for k in range(4)])):
                                for i, (c, k) in enumerate(terms):
                                    rr = 64 if c == 0 else 96
                                    ins = pe.matmul(bank(b0 + r, hi - lo, 0, 128), wsum[2][0:rr, c, k, lo:hi], sums(c, k, rr),
                                                    start=(i == 0), stop=(i == len(terms) - 1))
                            ins.then_inc(C["big"].sem, 1)
                        else:
                            for i, (c, k, rr, lo, hi) in enumerate(order):
                                ins = pe.matmul(bank(2 + r, P, lo, hi), sums(c, k, rr), wsum[n][0:rr, c, k, lo:hi],
                                                start=(i == 0), stop=(i == len(order) - 1), skip_group_check=True)
                            ins.then_inc(C["big"].sem, 1)
                    if n == 2 and within(j - 2, BLOCKS):
                        wait(pe, C["ms"], j - 1)
                        wait(pe, C["mv"], j - 1)
                        wait(pe, C["ev"], j - 3)
                        pe.sem_inc(s_apart["pe"], 1)
                        pe.matmul(bank(4 + q, P, 0, 64), hT[q][0:64, 0:128], w2s[:, :], start=True, stop=True,
                                  skip_group_check=True)
                        pe.matmul(bank(4 + q, P, 64, NF), hT[q][0:96, 128:256], w2v[:, :], start=False, stop=True,
                                  skip_group_check=True).then_inc(C["fin"].sem, 1)
                pipeline(pe, BLOCKS, 3, 2, 2 if n == 2 else 1, combine)
                if n < 3:
                    prep(n + 1)


_WEIGHTS = ["L0_gnn_W_skip0", "L0_gnn_W_skip1", "L0_gnn_W_nl0", "L0_gnn_W_nl1", "L0_gnn_W_fc1", "L0_gnn_W_fc2",
            "L0_gnn_W_out_s", "L0_gnn_W_out_v", "L1_gnn_W_si0", "L1_gnn_W_si1", "L1_gnn_W_l1_0", "L1_gnn_W_l1_1",
            "L1_gnn_W_l2_00", "L1_gnn_W_l2_10", "L1_gnn_W_l2_01", "L1_gnn_W_l2_11", "L1_gnn_W_fc1", "L1_gnn_W_fc2",
            "L2_gnn_W1", "L2_gnn_W2", "L2_gnn_W3", "L2_gnn_W4", "L2_gnn_W5", "L2_gnn_Ws", "L2_gnn_Wv",
            "L3_gnn_W_sc_s", "L3_gnn_W_sc_v", "L3_gnn_W1_s", "L3_gnn_W1_v", "L3_gnn_W2_s", "L3_gnn_W2_v", "L3_gnn_W3",
            "L3_gnn_fcW1", "L3_gnn_fcW2"]


def _feature_order(np):
    return np.concatenate([np.arange(S0), S0 + (np.arange(V1)[None, :] * 3 + np.arange(3)[:, None]).ravel()])


def kernel(**inputs):
    import numpy as np
    import concourse.bacc as bacc
    from concourse.bass_utils import run_bass_kernel_spmd

    def padded(a, n, value):
        a = np.asarray(a)
        return np.concatenate([a, np.full((n - a.shape[0],) + a.shape[1:], value, a.dtype)])

    def rows_of(parts, width):
        rows = np.concatenate([np.asarray(inputs[k]) for k in parts], axis=1)
        out = np.zeros((P * COLS, width), rows.dtype)
        out[:EDGES, :rows.shape[1]] = rows
        return out.reshape(P, COLS * width)

    order = _feature_order(np)
    arrays = {
        "x": padded(np.asarray(inputs["x"])[:, order], NPAD, 0),
        "node_vec1": padded(inputs["node_vec1"], NPAD, 0),
        "skey": padded(inputs["src"], P * COLS, PAD_NODE).reshape(P, COLS),
        "dkey": padded(inputs["dst"], P * COLS + 1, PAD_NODE),
        "edge_attr_3": padded(inputs["edge_attr_3"], P * COLS, 1).reshape(P, COLS * 3),
        "rows_a": rows_of(["edge_attr_64"], A_W),
        "rows_b": rows_of(["edge_attr_10", "edge_attr_8", "edge_attr_4"], B_W),
    }
    for k in _WEIGHTS:
        arrays[k] = np.ascontiguousarray(inputs[k])
    nc = bacc.Bacc("TRN2", target_bir_lowering=False, num_devices=1)
    t = {k: nc.dram_tensor(f"in_{k}", a.shape, mybir.dt.from_np(a.dtype), kind="ExternalInput").ap()
         for k, a in arrays.items()}
    t["out"] = nc.dram_tensor("out_x", (NPAD, NF), F32, kind="ExternalOutput").ap()
    gnn_program(nc, t)
    r = run_bass_kernel_spmd(nc, [{f"in_{k}": a for k, a in arrays.items()}], core_ids=[0])
    got = np.asarray(r.results[0]["out_x"])
    back = np.argsort(order)
    return got[:NODES][:, back]
```

```python
import math
from contextlib import ExitStack

import concourse.bass as bass
from concourse import mybir

F32 = mybir.dt.float32
I32 = mybir.dt.int32
I16 = mybir.dt.int16
BF16 = mybir.dt.bfloat16
ALU = mybir.AluOpType
ACT = mybir.ActivationFunctionType
AX_X = mybir.AxisListType.X
DVE, POOL, SP, ACTIVATION = mybir.EngineType.DVE, mybir.EngineType.Pool, mybir.EngineType.SP, mybir.EngineType.Activation

P = 128
NODES, EDGES = 3125, 100000
S0, V1 = 64, 32
NF = S0 + 3 * V1
BLOCKS = -(-NODES // P)
NPAD = BLOCKS * P
BIN = 32
BINS = NPAD // BIN
PAD_NODE = -(-NODES // BIN) * BIN
COLS = -(-EDGES // P)
GT = 8
FULL_BINS = PAD_NODE // BIN
MAX_TILES = (EDGES + FULL_BINS * (P - 1)) // P + 1
HALF = GT // 2
GROUPS = -(-MAX_TILES // GT)
TILES = GROUPS * GT
SLOTS = TILES * P
CHUNK = 23
CHUNKS = COLS // CHUNK
TCOLS = -(-TILES // P)
LAG_SC, LAG_FL = 2, 4
RING = 4

A_EF, A_SH, A_IDX, A_KEY, A_W = 0, 64, 67, 68, 69
B_10, B_8, B_4, B_IDX, B_KEY, B_W = 0, 10, 18, 22, 23, 32

N_SCALED = 10 + 3
EPS = 1e-5
STORES = 5
assert BLOCKS % STORES == 0
R2, R3 = math.sqrt(2.0), math.sqrt(3.0)
assert COLS % CHUNK == 0 and CHUNKS % 2 == 0 and GROUPS % 2 == 0
SEGMENTS = (0, 6, 18, CHUNKS)
COPY_FROM = SEGMENTS[1]
SPREAD = TCOLS * P // (CHUNKS - COPY_FROM)
assert SPREAD * (CHUNKS - COPY_FROM) == TCOLS * P and SPREAD % (2 * GT) == 0
WAYS = 4
assert BINS % WAYS == 0
PREP_FROM = SEGMENTS[2]


def is_static(v):
    return isinstance(v, int)


def within(v, n):
    return not is_static(v) or 0 <= v < n


class Signal:

    def __init__(self, sem, base):
        self.sem, self.base = sem, base


def wait(eng, signal, value):
    if is_static(value) and value <= 0:
        return
    if isinstance(signal, Signal):
        eng.wait_ge(signal.sem, value + signal.base)
    else:
        eng.wait_ge(signal, value)


def pipeline(eng, n, first, last, extra, body):
    for s in range(first):
        body(s, s // 2, s % 2)
    assert (n - first - last) % 2 == 0
    with eng.Fori(0, (n - first - last) // 2) as i:
        for u in range(first, first + 2):
            body(i * 2 + u, i + u // 2, u % 2)
    for s in range(n - last, n + extra):
        body(s, s // 2, s % 2)


def pairs(eng, a, b, body):
    assert a % 2 == 0 and b % 2 == 0
    with eng.Fori(0, (b - a) // 2) as i:
        for u in range(2):
            body(i * 2 + (a + u), i + a // 2, u)


class Layer:

    def __init__(self, n):
        self.n = n
        self.rowsA = n == 0
        self.mlp = n != 2
        self.width = 256 if n == 0 else 160
        self.wcols = 224 if n == 0 else 192
        self.chunks = [(0, 128), (128, 256)] if n == 0 else [(0, 64), (64, 160)]
        self.out = {0: 192, 1: 160, 2: 160, 3: 161}[n]
        self.tab_side = 96 if n == 0 else 64


LAYERS = [Layer(n) for n in range(4)]


def sum_weights(n):
    put = []
    if n == 0:
        put.append(("L0_gnn_W_out_s", 0, 64, 0, 0, 0, 0, 1.0))
        for i in range(3):
            put.append(("L0_gnn_W_out_v", 64, 96, 0 if i < 2 else 1, 0, (64, 96, 0)[i], 96 + 32 * i, 1.0))
            put.append(("L0_gnn_W_out_s", 64, 96, 0, 1 + i, 32 * i, 0, 1.0))
            put.append(("L0_gnn_W_out_v", 0, 64, 1, 1 + i, 64, 96 + 32 * i, 1.0))
            for j in range(3):
                if j != i:
                    sign = 1.0 if i == (j + 1) % 3 else -1.0
                    put.append(("L0_gnn_W_out_v", 96, 128, 0 if j == 0 else 1, 1 + i, (96, 0, 32)[j],
                                96 + 32 * (3 - i - j), sign))
        return put
    if n == 2:
        put.append(("L2_gnn_W1", 0, 64, 0, 0, 0, 0, 1.0))
        for i in range(3):
            put.append(("L2_gnn_W4", 0, 32, 1, 0, 32 * i, 64 + 32 * i, 1.0))
            put.append(("L2_gnn_W3", 0, 64, 0, 1 + i, 0, 64 + 32 * i, 1.0))
            put.append(("L2_gnn_W2", 0, 32, 1, 1 + i, 32 * i, 0, 1.0 / R3))
            for j in range(3):
                if j != i:
                    sign = 1.0 if i == (j + 1) % 3 else -1.0
                    put.append(("L2_gnn_W5", 0, 32, 1, 1 + i, 32 * j, 64 + 32 * (3 - i - j), sign / R2))
        return put
    if n == 1:
        ws, wv, o = (("L1_gnn_W_l2_00", 0), ("L1_gnn_W_l2_10", 0)), (("L1_gnn_W_l2_01", 0), ("L1_gnn_W_l2_11", 0)), 0
    else:
        ws, wv, o = (("L3_gnn_W2_s", 0), ("L3_gnn_W2_s", 64)), (("L3_gnn_W2_v", 0), ("L3_gnn_W2_v", 64)), 1
        put.append(("L3_gnn_W3", 0, 64, 0, 0, 0, 0, 1.0))
    put.append((ws[0][0], 0, 64, 0, 0, 0, o, 1.0))
    for i, (k, r) in enumerate(((1, 0), (1, 64), (0, 64))):
        put.append((wv[0][0], 0, 64, 0, k, r, o + 64 + 32 * i, 1.0))
        put.append((wv[1][0], wv[1][1], wv[1][1] + 32, 1, 0, 32 * i, o + 64 + 32 * i, 1.0))
        put.append((ws[1][0], ws[1][1], ws[1][1] + 32, 1, 1, 32 * i, o, 1.0))
        if n == 3:
            put.append(("L3_gnn_W3", 64, 96, 1, 1, 32 * i, 0, 1.0))
    return put


def sum_products(n):
    if n == 0:
        return ([(0, 0, 128, 0, 192), (1, 0, 32, 160, 192)] + [(0, k, 128, 0, 192) for k in (1, 2, 3)]
                + [(1, k, 128, 96, 192) for k in (1, 2, 3)])
    o = 1 if n == 3 else 0
    return [(0, 0, 128, 0, o + 160), (0, 1, 128, o + 64, o + 128), (1, 0, 96, o + 64, o + 160), (1, 1, 96, 0, o + 64)]


def gnn_program(nc, t):
    ctx = ExitStack()
    with ctx:
        def sb(name, shape, dt=F32):
            return ctx.enter_context(nc.sbuf_tensor(name, shape, dt))

        def sem(name):
            return ctx.enter_context(nc.semaphore(name))

        rows_dram = [nc.dram_tensor("rows_a", (SLOTS, A_W), F32).ap(),
                     nc.dram_tensor("rows_b", (TCOLS * P * P, B_W), F32).ap()]
        given_dram = nc.dram_tensor("rows_given", (P * COLS + P, B_W), F32).ap()
        starts_dram = nc.dram_tensor("tile_starts", (TCOLS * P,), I32).ap()
        first_node_dram = nc.dram_tensor("tile_first_node", (TCOLS * P,), F32).ap()
        table_dram = [nc.dram_tensor(f"table_{n}", (NPAD, NF), F32).ap() for n in range(4)]
        bins_dram = [nc.dram_tensor(f"tile_bins_{o}", (TCOLS * P,), I32).ap() for o in range(2)]

        x = sb("x", [P, BLOCKS * NF])
        attr = sb("attr", [P, BLOCKS])
        side = sb("side", [P, BLOCKS * 192])
        acc = sb("acc", [P, BINS * 256])
        ident = sb("ident", [P, P])
        iota_bin = sb("iota_bin", [P, BIN])
        iota_bins = sb("iota_bins", [P, BINS])
        tile_bins = sb("tile_bins_row", [1, RING + TCOLS * P], I32)
        w1 = {0: sb("w1_0", [P, P]), 1: sb("w1_1", [P, 4, 100]), 3: sb("w1_3", [P, 2, P])}
        w2 = {0: sb("w2_0", [P, 2, 224]), 1: sb("w2_1", [P, 192]), 3: sb("w2_3", [P, 2, 192])}
        wsum = {0: sb("wsum_0", [P, 2, 4, LAYERS[0].out])}
        tail = BINS * 256
        for n in (1, 2, 3):
            tail -= 8 * LAYERS[n].out
            wsum[n] = acc[:, tail:tail + 8 * LAYERS[n].out].rearrange("p (c k o) -> p c k o", c=2, k=4)
        first_node = acc[:, BINS * LAYERS[1].width:BINS * LAYERS[1].width + TCOLS * P]
        table_at = BINS * LAYERS[1].width + TCOLS * P
        table = acc[:, table_at:table_at + BLOCKS * NF]
        assert tail >= table_at + BLOCKS * NF
        wps = {n: sb(f"wps_{n}", [S0, 2 * S0 if n else S0 + 96]) for n in (0, 1, 3)}
        wpv = {n: sb(f"wpv_{n}", [96, 192]) for n in (0, 1, 3)}
        w2s, w2v = sb("w2s", [S0, S0]), sb("w2v", [96, 96])
        rows = [sb(f"rows_{q}", [P, GT, A_W]) for q in range(2)]
        gath = [sb(f"gath_{q}", [P, GT, NF]) for q in range(2)]
        sel = [sb(f"sel_{q}", [P, GT, 224]) for q in range(2)]
        onehot = sb("onehot", [P, GT, BIN])
        prod = sb("prod", [P, 3 * 416 + 704])
        attrT = sb("attrT", [P, 512])
        hidT = [sb(f"hidT_{q}", [P, 1024]) for q in range(2)]
        stg = [sel[q][:, :, :].rearrange("p t c -> p (t c)")[:, 0:4 * 256] for q in range(2)]
        sumT = [gath[q][:, :, :].rearrange("p t c -> p (t c)")[:, 0:1024].rearrange("p (c m) -> p c m", c=2) for q in range(2)]
        tmp, hbuf, trow, hT = ([prod[:, 768 * q + a:768 * q + b] for q in range(2)]
                               for a, b in ((0, 192), (192, 352), (352, 512), (512, 768)))
        stats = sb("stats", [P, BLOCKS, 6])
        small = sb("small", [P, 12, BLOCKS])

        pb = [ctx.enter_context(nc.psum_tensor(f"bank_{i}", [P, 512], F32)) for i in range(6)]
        wide = ctx.enter_context(nc.psum_tensor("bank_67", [P, 1024], F32))
        pb += [wide[:, 0:512], wide[:, 512:1024]]

        def bank(i, p, a, b):
            return pb[i][0:p, a:b]

        used = [0]

        def carve(words):
            a = used[0]
            used[0] += words
            assert used[0] <= BINS * 256
            return acc[:, a:a + words]

        even = COLS + COLS % 2
        key_i = [carve(COLS).bitcast(I32) for _ in range(2)]
        key_next = carve(COLS).bitcast(I32)
        key_f = carve(COLS)
        pos_i = [carve(COLS).bitcast(I32) for _ in range(2)]
        int_a, int_b = carve(COLS).bitcast(I32), carve(COLS).bitcast(I32)
        bin_h = [carve(even // 2).bitcast(BF16)[:, 0:COLS] for _ in range(2)]
        eq = [carve(even // 2).bitcast(I16)[:, 0:COLS] for _ in range(WAYS)]
        zero_h = carve(even // 2).bitcast(I16)[:, 0:COLS]
        sh = carve(3 * COLS)
        sh2 = carve(3 * COLS)
        norm = carve(COLS)
        pos_f = [sh2[:, k * COLS:k * COLS + COLS] for k in range(3)] + [carve(COLS)]
        tri, ones = carve(P), carve(P)
        count, ntile, first_tile, bins_f, bins_z, pad = (carve(BINS) for _ in range(6))
        base = [carve(BINS) for _ in range(2)]
        by_tile = carve(TCOLS * BINS)
        tile_pad, tile_node = carve(TCOLS), carve(TCOLS)
        tile_start = carve(TCOLS).bitcast(I32)
        starts_row = carve(TCOLS * P).bitcast(I32)
        falls, unsorted = carve(1), carve(1).bitcast(I32)
        bins_i = carve(BINS).bitcast(I32)
        tile_id, tile_bin = carve(TCOLS), carve(TCOLS)
        tile_bin_i = carve(TCOLS).bitcast(I32)
        stage = [[carve(CHUNK * w) for _ in range(2)] for w in (A_W, B_W)]
        pos_r = [carve(CHUNK).bitcast(I32) for _ in range(2)]
        blank = [carve(GT * w) for w in (A_W, B_W)]

        s_in = sem("s_in")
        s_nodes = sem("s_nodes")
        s_wz = sem("s_wz")
        s_w = sem("s_w")
        s_wf = sem("s_wf")
        s_const = sem("s_const")
        s_cz = sem("s_cz")
        s_blank = sem("s_blank")
        s_init = sem("s_init")
        s_lz = sem("s_lz")
        s_lw = sem("s_lw")
        s_lf = sem("s_lf")
        s_bz = sem("s_bz")
        s_chain = sem("s_chain")
        s_sq = sem("s_sq")
        s_rt = sem("s_rt")
        s_cnt = [sem(f"s_cnt{o}") for o in range(2)]
        s_cum = [sem(f"s_cum{o}") for o in range(2)]
        s_eq = [sem(f"s_eq{o}") for o in range(2)]
        s_scan = [sem(f"s_scan{o}") for o in range(2)]
        s_pick = [sem(f"s_pick{o}") for o in range(2)]
        s_tb = [sem(f"s_tb{o}") for o in range(2)]
        s_tbd = [sem(f"s_tbd{o}") for o in range(2)]
        s_tbs = [sem(f"s_tbs{o}") for o in range(2)]
        s_pos = [sem(f"s_pos{o}") for o in range(2)]
        s_falls = sem("s_falls")
        s_flag_sum = sem("s_flag_sum")
        s_again = sem("s_again")
        s_flag = sem("s_flag")
        s_start = sem("s_start")
        s_startd = sem("s_startd")
        s_starts = sem("s_starts")
        s_nodes_of = sem("s_nodes_of")
        s_stage = [[sem(f"s_stage{o}{q}") for q in range(2)] for o in range(2)]
        s_fill = [sem(f"s_fill{o}") for o in range(2)]
        s_given = [sem(f"s_given{q}") for q in range(2)]
        s_empty = sem("s_empty")
        s_scat = [sem(f"s_scat{q}") for q in range(2)]
        s_copy = [sem("s_copy_sp"), sem("s_copy_act")]
        s_ranked = sem("s_ranked")
        s_placed = sem("s_placed")
        s_gp = sem("s_gp")
        s_gd = sem("s_gd")

        def signals(names, n):
            return {k: Signal(sem(f"s_{k}_{n}"), 0) for k in names.split()}

        s_p = [signals("ht hts m tab" if n != 2 else "", n)
               for n in range(4)]
        s_e = [signals("rows0 rows1" + (" zero" if n else "") + (" tr tc m1 hid w prod" if n != 2 else ""), n) for n in range(4)]
        s_c = [signals({0: "t1 sig t2", 2: "ms mv fin"}.get(n, ""), n) for n in range(4)]
        for names, where, each in (("stat h side", s_p, BLOCKS), ("var root rstd", s_p, 1), ("td0", s_p[:1], 0), ("td1", s_p[:1], 0),
                                   ("oh sel", s_e, GROUPS), ("key", s_e[1:], GROUPS), ("td", s_p[1:], 16 * STORES),
                                   ("ga00 ga01 ga10 ga11", s_e, 16 * HALF * (GROUPS // 2)), ("sc fl", s_e, TILES), ("stg stga trn ca cd big ev", s_c, BLOCKS)):
            for k in names.split():
                shared = sem(f"s_{k}")
                for n in range(len(where)):
                    where[n][k] = Signal(shared, each * n)
        s_apart = {e: sem(f"s_apart_{e}") for e in ("pool", "pe", "dve", "sp")}
        s_fin = sem("s_fin")
        s_trig = sem("s_trig")
        s_out = sem("s_out")

        loads = []
        for half in range(2):
            loads.append((w1[0][64 * half:64 * half + 64, 64 * half:64 * half + 64], t["L0_gnn_W_fc1"]))
            loads.append((w2[0][64 * half:64 * half + 64, half, :], t["L0_gnn_W_fc2"]))
            loads.append((w2[3][64 * half:64 * half + 64, half, :], t["L3_gnn_fcW2"]))
        for i in range(4):
            loads.append((w1[1][32 * i + B_10:32 * i + B_10 + 10, i, :], t["L1_gnn_W_fc1"]))
            loads.append((w1[3][32 * i + B_8:32 * i + B_8 + 8, i // 2, 64 * (i % 2):64 * (i % 2) + 64], t["L3_gnn_fcW1"]))
        loads.append((w2[1][0:100, :], t["L1_gnn_W_fc2"]))
        late = []
        for n in range(4):
            for name, a, b, c, k, r, col, _factor in sum_weights(n):
                (late if n else loads).append((wsum[n][r:r + b - a, c, k, col:col + t[name].shape[1]], t[name][a:b, :]))
        for n, (ts, tv, ks, kv) in {0: ("L0_gnn_W_nl0", "L0_gnn_W_nl1", "L0_gnn_W_skip0", "L0_gnn_W_skip1"),
                                    1: ("L1_gnn_W_l1_0", "L1_gnn_W_l1_1", "L1_gnn_W_si0", "L1_gnn_W_si1"),
                                    3: ("L3_gnn_W1_s", "L3_gnn_W1_v", "L3_gnn_W_sc_s", "L3_gnn_W_sc_v")}.items():
            loads.append((wps[n][:, 0:64], t[ts]))
            loads.append((wps[n][:, 64:64 + LAYERS[n].tab_side], t[ks]))
            for i in range(3):
                loads.append((wpv[n][32 * i:32 * i + 32, 32 * i:32 * i + 32], t[tv]))
                loads.append((wpv[n][32 * i:32 * i + 32, 96 + 32 * i:128 + 32 * i], t[kv]))
        loads.append((w2s[:, :], t["L2_gnn_Ws"]))
        for i in range(3):
            loads.append((w2v[32 * i:32 * i + 32, 32 * i:32 * i + 32], t["L2_gnn_Wv"]))

        def sum_factors(n):
            return [(wsum[n][r:r + b - a, c, k, col:col + t[name].shape[1]], f)
                    for name, a, b, c, k, r, col, f in sum_weights(n) if f != 1.0]

        def by_bin(a):
            return a.rearrange("p (b k m) -> p k b m", b=4, k=4)

        def by_kind(a):
            return a.rearrange("p (k b m) -> p k b m", b=4, k=4)

        def rows_a(q):
            flat = rows[q][:, :, :].rearrange("p t c -> p (t c)")
            return flat[:, 0:GT * 64], flat[:, GT * 64:GT * A_W].rearrange("p (t c) -> p t c", t=GT)

        def rows_b(q):
            return rows[q][:, :, :].rearrange("p t c -> p (t c)")[:, 0:GT * B_W]

        def scratch(i):
            return small[:, i, :]

        RSTD, NMR = 0, 1

        def xj(j, n=1):
            return x[:, bass.ds(j * NF, n * NF)]

        def sj(j):
            return side[:, bass.ds(j * 192, 192)]

        tiles_b = rows_dram[1].rearrange("(g p t) c -> p g t c", p=P, t=GT)

        def copy_tiles(eng, kind, part, c):
            for v in range(0, SPREAD // 2, GT):
                u = part * (SPREAD // 2) + v
                _, start = nc.values_load_multi_w_load_instructions(
                    starts_row[0:1, bass.ds((c - COPY_FROM) * SPREAD + u, GT)], engines=(kind,),
                    min_val=0, max_val=P * COLS, skip_runtime_bounds_check_because="clamped to the number of edges")
                for w in range(GT):
                    eng.dma_start(tiles_b[:, bass.ds((c - COPY_FROM) * (SPREAD // GT) + u // GT, 1), w, :],
                                  given_dram[bass.ds(start[w], P), :].unsqueeze(1)).then_inc(s_copy[part], 16)

        block = ctx.enter_context(nc.Block())

        @block.sync
        def _(sp):
            sp.dma_start(key_i[0], t["skey"]).then_inc(s_in, 16)
            sp.dma_start(sh, t["edge_attr_3"]).then_inc(s_in, 16)
            sp.dma_start(key_i[1], t["dkey"][0:P * COLS].rearrange("(p c) -> p c", p=P)).then_inc(s_in, 16)
            sp.dma_start(key_next, t["dkey"][1:P * COLS + 1].rearrange("(p c) -> p c", p=P)).then_inc(s_in, 16)

            def given(c, half, q):
                if within(c, CHUNKS):
                    wait(sp, s_given[q], half * 16)
                    sp.sem_inc(s_apart["sp"], 1)
                    sp.dma_start(stage[1][q], t["rows_b"][:, bass.ds(c * (CHUNK * B_W), CHUNK * B_W)]).then_inc(s_stage[1][q], 16)
                if within(c - 1, CHUNKS):
                    wait(sp, s_fill[1], c * 2)
                    sp.sem_inc(s_apart["sp"], 1)
                    sp.dma_start(given_dram[0:P * COLS, :].rearrange("(p c) w -> p (c w)", p=P)[:, bass.ds((c - 1) * (CHUNK * B_W), CHUNK * B_W)],
                                 stage[1][1 - q]).then_inc(s_given[1 - q], 16)
            sp.wait_ge(s_in, 64)
            pipeline(sp, CHUNKS, 2, 0, 1, given)
            sp.dma_start(x[:, :].rearrange("p (j c) -> p j c", j=BLOCKS),
                         t["x"].rearrange("(j p) c -> p j c", p=P)).then_inc(s_nodes, 16)
            with nc.allow_non_contiguous_dma(reason="one word per node"):
                sp.dma_start(attr[:, :], t["node_vec1"].rearrange("(j p) c -> p (j c)", p=P)).then_inc(s_nodes, 16)

            def tables(n):
                S, m = s_p[n], BLOCKS // STORES
                for i in range(STORES):
                    wait(sp, S["h"] if n == 2 else S["tab"], m * (i + 1))
                    sp.dma_start(table_dram[n].rearrange("(j p) c -> p j c", p=P)[:, m * i:m * (i + 1), :],
                                 table[:, m * i * NF:m * (i + 1) * NF].rearrange("p (j c) -> p j c", j=m)).then_inc(S["td"].sem, 16)

            def bins_out(o):
                sp.wait_ge(s_tb[o], 1)
                with nc.allow_non_contiguous_dma(reason="one word per tile"):
                    sp.dma_start(bins_dram[o].rearrange("(c p) -> p c", p=P), tile_bin_i).then_inc(s_tbd[o], 16)
                sp.wait_ge(s_tbd[o], 16)

            def bins_in(o):
                if o:
                    wait(sp, s_e[0]["fl"], TILES)
                sp.wait_ge(s_bz, 1)
                sp.dma_start(tile_bins[0:1, RING:], bins_dram[o].rearrange("(a c) -> a c", a=1)).then_inc(s_tbs[o], 16)

            def starts():
                sp.wait_ge(s_start, 1)
                with nc.allow_non_contiguous_dma(reason="one word per tile"):
                    sp.dma_start(starts_dram.rearrange("(c p) -> p c", p=P), tile_start).then_inc(s_startd, 16)
                    sp.dma_start(first_node_dram.rearrange("(c p) -> p c", p=P), tile_node).then_inc(s_startd, 16)
                sp.wait_ge(s_startd, 32)
                sp.dma_start(starts_row[0:1, :], starts_dram.rearrange("(a c) -> a c", a=1)).then_inc(s_starts, 16)
                sp.wait_ge(s_starts, 16)

            def stage_rows(c, half, q):
                wait(sp, s_scat[q], half * (16 * CHUNK))
                sp.sem_inc(s_apart["sp"], 1)
                sp.dma_start(stage[0][q], t["rows_a"][:, bass.ds(c * (CHUNK * A_W), CHUNK * A_W)]).then_inc(s_stage[0][q], 16)

            def edge_rows(n):
                S, L = s_e[n], LAYERS[n]
                o, w = (0, A_W) if L.rowsA else (1, B_W)
                if n == 0:
                    for q in range(2):
                        sp.wait_ge(s_scat[q], 16 * CHUNK * (CHUNKS // 2))
                src = rows_dram[o].rearrange("(g p t) c -> p g (t c)", p=P, t=GT)

                def body(g, half, q):
                    for h in range(2):
                        wait(sp, S[f"ga{q}{h}"], half * (16 * HALF))
                        sp.sem_inc(s_apart["sp"], 1)
                    wait(sp, S["sel"], g - 1)
                    sp.sem_inc(s_apart["sp"], 1)
                    if L.mlp:
                        wait(sp, S["tr"], g - 1)
                    sp.sem_inc(s_apart["sp"], 1)
                    if L.rowsA:
                        one = src[:, bass.ds(g, 1), :].rearrange("p g (t c) -> p (g t) c", t=GT)
                        ef, rest = rows_a(q)
                        sp.dma_start(ef.rearrange("p (t c) -> p t c", t=GT), one[:, :, 0:A_SH]).then_inc(S[f"rows{q}"].sem, 16)
                        sp.dma_start(rest, one[:, :, A_SH:A_W]).then_inc(S[f"rows{q}"].sem, 16)
                    else:
                        sp.dma_start(rows_b(q).unsqueeze(1), src[:, bass.ds(g, 1), :]).then_inc(S[f"rows{q}"].sem, 16)
                if n:
                    sp.wait_ge(s_placed, 1)
                    wait(sp, s_e[n - 1]["sel"], GROUPS)
                    for h in ("00", "01", "10", "11"):
                        wait(sp, s_e[n - 1]["ga" + h], 16 * HALF * (GROUPS // 2))
                    if LAYERS[n - 1].mlp:
                        wait(sp, s_e[n - 1]["tr"], GROUPS)
                pipeline(sp, GROUPS, 2, 0, 0, body)

            bins_out(0)
            for c in range(2):
                stage_rows(c, 0, c)
            pairs(sp, 2, COPY_FROM, stage_rows)
            bins_out(1)
            starts()
            for q in range(2):
                sp.wait_ge(s_given[q], 16 * (CHUNKS // 2))
            sp.wait_ge(s_empty, 16)

            def rows_and_tiles(c, half, q):
                stage_rows(c, half, q)
                copy_tiles(sp, SP, 0, c)
            pairs(sp, COPY_FROM, CHUNKS, rows_and_tiles)
            bins_in(0)
            edge_rows(0)
            bins_in(1)
            wait(sp, s_c[0]["stg"], BLOCKS)
            wait(sp, s_c[0]["stga"], BLOCKS)
            sp.dma_start(first_node, first_node_dram.rearrange("(a c) -> a c", a=1).to_broadcast([P, TCOLS * P])).then_inc(s_nodes_of, 16)
            sp.wait_ge(s_lz, 1)
            for dst, src in late:
                sp.dma_start(dst, src).then_inc(s_lw, 16)
            for n in range(1, 4):
                tables(n)
                edge_rows(n)
            sp.wait_ge(s_fin, 1)
            sp.dma_start(t["out"].rearrange("(j p) c -> p j c", p=P),
                         x[:, :].rearrange("p (j c) -> p j c", j=BLOCKS)).then_inc(s_out, 16)
            sp.wait_ge(s_out, 16)
            for q in range(2):
                wait(sp, s_p[0][f"td{q}"], 16 * ((BLOCKS + 1 - q) // 2))
            for n in range(1, 4):
                wait(sp, s_p[n]["td"], 16 * STORES)

        @block.gpsimd
        def _(pool):
            for o, w in enumerate((A_W, B_W)):
                pool.memset(blank[o], 0.0).then_inc(s_blank, 1)
            pool.wait_ge(s_blank, 2)
            for o, (w, k) in enumerate(((A_W, A_KEY), (B_W, B_KEY))):
                pool.memset(blank[o].rearrange("p (t c) -> p t c", t=GT)[:, :, k:k + 1], -1.0).then_inc(s_blank, 1)
            pool.memset(ident[:, :], 0.0).then_inc(s_cz, 1)
            pool.memset(tri, 1.0).then_inc(s_cz, 1)
            pool.memset(ones, 1.0)
            pool.memset(bins_z, 0.0)
            pool.memset(zero_h, 0)
            pool.iota(iota_bin[:, :], pattern=[[1, BIN]], base=0, channel_multiplier=0,
                      allow_small_or_imprecise_dtypes=True)
            pool.iota(iota_bins[:, :], pattern=[[1, BINS]], base=0, channel_multiplier=0,
                      allow_small_or_imprecise_dtypes=True)
            pool.iota(tile_id, pattern=[[P, TCOLS]], base=0, channel_multiplier=1,
                      allow_small_or_imprecise_dtypes=True)
            pool.wait_ge(s_cz, 2)
            pool.affine_select(out=ident[:, :], in_=ident[:, :], compare_op=ALU.not_equal, fill=1.0, base=0,
                               pattern=[[-1, P]], channel_multiplier=1)
            pool.affine_select(out=tri, in_=tri, compare_op=ALU.is_gt, fill=0.0, base=0,
                               pattern=[[1, P]], channel_multiplier=-1).then_inc(s_const, 1)
            pool.memset(tile_bins[:, :], 0).then_inc(s_bz, 1)
            for ws in (w1, w2, wps, wpv):
                for m in ws.values():
                    pool.memset(m[...], 0.0)
            pool.memset(wsum[0][...], 0.0)
            pool.memset(w2v[:, :], 0.0).then_inc(s_wz, 1)
            pool.wait_ge(s_wz, 1)
            for dst, src in loads:
                pool.dma_start(dst, src).then_inc(s_w, 16)
            pool.wait_ge(s_w, 16 * len(loads))
            fac = [(w2[0][:, :, 64:128], R3), (w2[0][:, :, 192:224], R3 / R2),
                   (w2[1][:, 0:160], 0.1), (w2[1][:, 160:192], 0.1 / R3),
                   (w2[3][:, :, 0:160], 1 / 8), (w2[3][:, :, 160:192], 1 / 8 / R3),
                   (wps[1][:, :], 1 / 8), (wps[3][:, :], 1 / 8),
                   (wpv[1][:, :], 1 / math.sqrt(32)), (wpv[3][:, :], 1 / math.sqrt(32))]
            assert len(fac) + len(sum_factors(0)) == N_SCALED
            for i, (m, f) in enumerate(fac + sum_factors(0)):
                wait(pool, s_wf, i)
                pool.tensor_scalar(m, m, f, None, ALU.mult).then_inc(s_wf, 1)

            pool.wait_ge(s_wf, N_SCALED)
            pool.wait_ge(s_init, 16)

            def scatter(c, half, q):
                pool.wait_ge(s_fill[0], c * 4 + 4)
                pool.sem_inc(s_apart["pool"], 1)
                for u in range(CHUNK):
                    pool.indirect_dma_start(
                        rows_dram[0][:, :], bass.IndirectOffsetOnAxis(ap=pos_r[q][:, u:u + 1], axis=0),
                        stage[0][q][:, u * A_W:(u + 1) * A_W], None).then_inc(s_scat[q], 16)
            pipeline(pool, CHUNKS, 2, 0, 0, scatter)
            for q in range(2):
                pool.wait_ge(s_scat[q], 16 * CHUNK * (CHUNKS // 2))
                pool.wait_ge(s_copy[q], 16 * TCOLS * P // 2)
            pool.wait_ge(s_flag, 1)
            _, (flag,) = nc.values_load_multi_w_load_instructions(
                unsorted[0:1, 0:1], engines=(POOL,), min_val=0, max_val=P * COLS,
                skip_runtime_bounds_check_because="a count of edges")
            with pool.If(flag != 0):
                pool.wait_ge(s_pos[1], 1)
                pool.dma_start(rows_dram[1].rearrange("(g p t) c -> p g (t c)", p=P, t=GT),
                               blank[1].unsqueeze(1).to_broadcast([P, TCOLS * P // GT, GT * B_W])).then_inc(s_gd, 16)
                pool.wait_ge(s_gd, 16)
                with pool.Fori(0, CHUNKS) as c:
                    pool.dma_start(stage[1][0], given_dram[0:P * COLS, :].rearrange("(p c) w -> p (c w)", p=P)[:, bass.ds(c * (CHUNK * B_W), CHUNK * B_W)]).then_inc(s_gd, 16)
                    pool.tensor_copy(pos_r[0], pos_i[1][:, bass.ds(c * CHUNK, CHUNK)]).then_inc(s_gp, 1)
                    pool.wait_ge(s_gp, c + 1)
                    pool.sem_inc(s_apart["pool"], 1)
                    pool.wait_ge(s_gd, c * (16 + 16 * CHUNK) + 32)
                    pool.sem_inc(s_apart["pool"], 1)
                    for u in range(CHUNK):
                        pool.indirect_dma_start(
                            rows_dram[1][:, :], bass.IndirectOffsetOnAxis(ap=pos_r[0][:, u:u + 1], axis=0),
                            stage[1][0][:, u * B_W:(u + 1) * B_W], None).then_inc(s_gd, 16)
                    pool.wait_ge(s_gd, c * (16 + 16 * CHUNK) + (32 + 16 * CHUNK))
            pool.sem_inc(s_placed, 1)

            for n in range(4):
                L, S = LAYERS[n], s_e[n]
                if n:
                    wait(pool, s_c[n - 1]["stg"], BLOCKS)
                    wait(pool, s_c[n - 1]["stga"], BLOCKS)
                    pool.memset(acc[:, 0:BINS * L.width], 0.0).then_inc(S["zero"].sem, 1)
                if n == 1:
                    pool.memset(acc[:, tail:], 0.0).then_inc(s_lz, 1)
                if n:
                    wait(pool, s_p[n]["td"], 16 * STORES)
                else:
                    for q in range(2):
                        wait(pool, s_p[n][f"td{q}"], 16 * ((BLOCKS + 1 - q) // 2))
                if n:
                    wait(pool, s_e[n - 1]["sc"], TILES)

                def body(g, half, q, n=n, L=L, S=S):
                    wait(pool, S[f"rows{q}"], (half + 1) * (32 if n == 0 else 16))
                    first, w = (GT * 64 + A_IDX - A_SH, A_W - A_SH) if L.rowsA else (B_IDX, B_W)
                    flat = rows[q][:, :, :].rearrange("p t c -> p (t c)")
                    for u in range(GT):
                        if u % HALF == 0:
                            wait(pool, S["prod"] if L.mlp else S["sc"], g * GT + (u + HALF - 2 * GT))
                            pool.sem_inc(s_apart["pool"], 1)
                        pool.indirect_dma_start(
                            gath[q][:, u, :], None, table_dram[n][:, :],
                            bass.IndirectOffsetOnAxis(ap=flat[:, u * w + first:u * w + first + 1].bitcast(I32), axis=0)).then_inc(S[f"ga{q}{u // HALF}"].sem, 16)
                pipeline(pool, GROUPS, 2, 0, 0, body)

                C = s_c[n]
                wait(pool, S["fl"], TILES)
                w2_ = 2 * L.width

                def stage_sums(j, half, q, C=C, w2_=w2_):
                    wait(pool, C["trn"], j - 1)
                    pool.sem_inc(s_apart["pool"], 1)
                    pool.tensor_copy(stg[q][:, 0:w2_], acc[:, bass.ds(j * (2 * w2_), w2_)]).then_inc(C["stg"].sem, 1)
                pipeline(pool, BLOCKS, 3, 2, 0, stage_sums)

        @block.scalar
        def _(act):
            act.wait_ge(s_blank, 4)
            act.dma_start(given_dram[P * COLS:, :], blank[1][:, 0:B_W]).then_inc(s_empty, 16)
            act.dma_start(rows_dram[0].rearrange("(g p t) c -> p g (t c)", p=P, t=GT),
                          blank[0].unsqueeze(1).to_broadcast([P, GROUPS, GT * A_W])).then_inc(s_init, 16)
            act.wait_ge(s_sq, 1)
            act.activation(norm, norm, ACT.Sqrt).then_inc(s_rt, 1)

            def complete(c, half, q):
                wait(act, s_stage[1][q], half * 16 + 16)
                st = stage[1][q].rearrange("p (u c) -> p u c", c=B_W)
                at = bass.ds(c * CHUNK, CHUNK)
                act.activation(st[:, :, B_IDX:B_IDX + 1].bitcast(I32), key_i[0][:, at].unsqueeze(2),
                               ACT.Copy).then_inc(s_fill[1], 1)
                act.activation(st[:, :, B_KEY:B_KEY + 1], key_i[1][:, at].unsqueeze(2), ACT.Copy).then_inc(s_fill[1], 1)
            act.wait_ge(s_in, 64)
            pairs(act, 0, CHUNKS, complete)

            def prep(n):
                S = s_p[n]
                wait(act, S["var"], 1)
                act.activation(scratch(4), scratch(4), ACT.Sqrt).then_inc(S["root"].sem, 1)
                wait(act, S["rstd"], 1)

                def body(j, half, q):
                    if within(j, BLOCKS):
                        if n != 2:
                            wait(act, S["ht"], j - 1)
                        h = table[:, bass.ds(j * NF, NF)] if n == 2 else hbuf[q][:, :]
                        act.activation(h, xj(j), ACT.Relu, bias=small[:, NMR, bass.ds(j, 1)],
                                       scale=small[:, RSTD, bass.ds(j, 1)]).then_inc(S["h"].sem, 1)
                    if n != 2 and within(j - 2, BLOCKS):
                        wait(act, S["m"], j - 1)
                        if n == 0:
                            wait(act, S[f"td{q}"], half * 16 - 16)
                        row = trow[q][:, :] if n == 0 else table[:, bass.ds((j - 2) * NF, NF)]
                        act.activation(row, bank(6 + q, P, 0, NF), ACT.Copy,
                                       scale=1.0 if n == 0 else attr[:, bass.ds(j - 2, 1)]).then_inc(S["tab"].sem, 1)
                        if n == 0:
                            wait(act, S["tab"], j - 1)
                            act.dma_start(table_dram[0].rearrange("(j p) c -> p j c", p=P)[:, bass.ds(j - 2, 1), :],
                                          trow[q][:, :].unsqueeze(1)).then_inc(S[f"td{q}"].sem, 16)
                return body

            def prep_all(n):
                pipeline(act, BLOCKS, 3, 2, 2, prep(n))

            def fill(c, half, q):
                wait(act, s_stage[0][q], half * 16 + 16)
                st = stage[0][q].rearrange("p (u c) -> p u c", c=A_W)
                at = bass.ds(c * CHUNK, CHUNK)
                act.activation(st[:, :, A_SH:A_SH + 3],
                               sh[:, bass.ds(c * (3 * CHUNK), 3 * CHUNK)].rearrange("p (u c) -> p u c", c=3),
                               ACT.Copy).then_inc(s_fill[0], 1)
                act.activation(st[:, :, A_IDX:A_IDX + 1].bitcast(I32), key_i[1][:, at].unsqueeze(2),
                               ACT.Copy).then_inc(s_fill[0], 1)
                act.activation(st[:, :, A_KEY:A_KEY + 1], key_f[:, at].unsqueeze(2), ACT.Copy).then_inc(s_fill[0], 1)
                act.activation(pos_r[q], pos_i[0][:, at], ACT.Copy).then_inc(s_fill[0], 1)

            act.wait_ge(s_pos[0], 1)
            pairs(act, 0, SEGMENTS[1], fill)
            act.wait_ge(s_pos[0], 2)
            act.wait_ge(s_empty, 16)
            for q in range(2):
                act.wait_ge(s_given[q], 16 * (CHUNKS // 2))
            act.wait_ge(s_starts, 16)

            def fill_and_copy(c, half, q):
                fill(c, half, q)
                copy_tiles(act, ACTIVATION, 1, c)
            pairs(act, SEGMENTS[1], SEGMENTS[2], fill_and_copy)
            act.wait_ge(s_pos[0], 3)
            act.wait_ge(s_nodes, 32)
            prep_step = prep(0)

            def fill_and_prep(c, half, q):
                fill_and_copy(c, half, q)
                step, at = (c - PREP_FROM) * 2, (c - PREP_FROM)
                for v in range(2):
                    if not is_static(c) or step + v < BLOCKS + 2:
                        prep_step(step + v, at, v)
            for c in range(PREP_FROM, PREP_FROM + 2):
                fill_and_prep(c, c // 2, c % 2)
            last = PREP_FROM + (BLOCKS - 1) // 2 // 2 * 2
            pairs(act, PREP_FROM + 2, last, fill_and_prep)
            for c in range(last, last + 2):
                fill_and_prep(c, c // 2, c % 2)
            pairs(act, last + 2, CHUNKS, fill_and_copy)

            for n in range(4):
                L, S, C = LAYERS[n], s_e[n], s_c[n]
                if L.mlp:
                    tcols = 512 if n == 0 else 256
                    hrows = 100 if n == 1 else P

                    def body(g, half, q, n=n, S=S, tcols=tcols, hrows=hrows):
                        wait(act, S["tr"], g + 1)
                        act.activation(attrT[:, 0:tcols], bank(0, P, 0, tcols), ACT.Copy).then_inc(S["tc"].sem, 1)
                        wait(act, S["m1"], g + 1)
                        for b in range(2 if n == 1 else 1):
                            i = act.activation(hidT[q][0:hrows, 512 * b:512 * b + 512], bank(2 + b, hrows, 0, 512),
                                               ACT.Silu if n == 3 else ACT.Relu,
                                               scale={0: 1.0, 1: R2 / math.sqrt(10.0), 3: 1 / math.sqrt(8.0)}[n])
                        i.then_inc(S["hid"].sem, 1)
                    pipeline(act, GROUPS, 2, 2, 0, body)

                (a0, a1) = L.chunks[0]

                def stage_sums(j, q, C=C, w2_=2 * L.width):
                    wait(act, C["trn"], j - 1)
                    act.activation(stg[q][:, w2_:2 * w2_], acc[:, bass.ds(j * (2 * w2_) + w2_, w2_)], ACT.Copy).then_inc(C["stga"].sem, 1)

                def combine(j, half, q, n=n, C=C, a0=a0, a1=a1, stage_sums=stage_sums):
                    if within(j + 1, BLOCKS):
                        stage_sums(j + 1, 1 - q)
                    if within(j, BLOCKS):
                        wait(act, C["trn"], j + 1)
                        if n % 2:
                            turned = by_bin(bank(0, S0, 0, 512))
                            act.activation(by_kind(sumT[q][0:S0, 0, :])[:, 0:2], turned[:, 0:2], ACT.Copy)
                            for k in range(2):
                                i = act.activation(by_kind(sumT[q][S0:P, 0, :])[:, k], turned[:, 3 - k], ACT.Copy)
                            i.then_inc(C["ca"].sem, 1)
                        else:
                            act.activation(by_kind(sumT[q][0:a1 - a0, 0, :]), by_bin(bank(0, a1 - a0, 0, 512)),
                                           ACT.Copy).then_inc(C["ca"].sem, 1)
                    if within(j - 1, BLOCKS):
                        if n == 0:
                            wait(act, C["t1"], j)
                            act.activation(hbuf[1 - q][:, 0:96], tmp[1 - q][:, 0:96], ACT.Sigmoid).then_inc(C["sig"].sem, 1)
                        if n == 2:
                            wait(act, C["big"], j)
                            act.activation(hT[1 - q][0:64, 0:128], bank(3 - q, 64, 0, 128), ACT.Copy,
                                           scale=1 / math.sqrt(96.0) / 8).then_inc(C["ms"].sem, 1)
                wait(act, S["fl"], TILES)
                stage_sums(0, 0)
                pipeline(act, BLOCKS, 3, 2, 1, combine)
                if n < 3:
                    prep_all(n + 1)
            act.wait_ge(s_trig, 1)
            act.activation(scratch(4), scratch(2), ACT.Sin)
            act.activation(scratch(5), scratch(3), ACT.Sin).then_inc(s_trig, 1)

        @block.vector
        def _(dve):
            links = [0]

            def link(ins):
                links[0] += 1
                ins.then_inc(s_chain, 1)
                dve.wait_ge(s_chain, links[0])

            dve.wait_ge(s_in, 64)
            sh3 = sh.rearrange("p (e c) -> p e c", c=3)
            link(dve.tensor_tensor(sh2, sh, sh, ALU.mult))
            dve.tensor_reduce(norm, sh2.rearrange("p (e c) -> p e c", c=3), AX_X, ALU.add).then_inc(s_sq, 1)
            dve.wait_ge(s_rt, 1)
            link(dve.reciprocal(norm, norm))
            link(dve.tensor_tensor(sh3, sh3, norm.unsqueeze(2).to_broadcast([P, COLS, 3]), ALU.mult))

            def block_statistics(n, j):
                dve.bn_stats(stats[:, bass.ds(j, 1), :].rearrange("p j c -> p (j c)"), xj(j)).then_inc(s_p[n]["stat"].sem, 1)

            def statistics(n):
                S = s_p[n]
                if n == 0:
                    with dve.Fori(0, BLOCKS) as j:
                        block_statistics(0, j)
                wait(dve, S["stat"], BLOCKS)
                me, ve, mo, vo = (stats[:, :, i] for i in (1, 2, 4, 5))
                link(dve.tensor_tensor(scratch(2), me, mo, ALU.add))
                link(dve.tensor_tensor(scratch(3), me, mo, ALU.subtract))
                link(dve.tensor_tensor(scratch(4), ve, vo, ALU.add))
                link(dve.tensor_tensor(scratch(3), scratch(3), scratch(3), ALU.mult))
                link(dve.tensor_scalar(scratch(4), scratch(4), 1 / NF, EPS, ALU.mult, ALU.add))
                dve.scalar_tensor_tensor(out=scratch(4), in0=scratch(3), scalar=0.25, in1=scratch(4),
                                         op0=ALU.mult, op1=ALU.add).then_inc(S["var"].sem, 1)
                wait(dve, S["root"], 1)
                link(dve.reciprocal(scratch(RSTD), scratch(4)))
                dve.scalar_tensor_tensor(out=scratch(NMR), in0=scratch(2), scalar=-0.5, in1=scratch(RSTD),
                                         op0=ALU.mult, op1=ALU.mult).then_inc(S["rstd"].sem, 1)

            def prep(n):
                S = s_p[n]

                def body(j, half, q):
                    if n == 2:
                        if within(j, BLOCKS):
                            wait(dve, S["h"], j + 1)
                            dve.tensor_tensor(xj(j), xj(j), table[:, bass.ds(j * NF, NF)], ALU.add).then_inc(S["side"].sem, 1)
                        return
                    if within(j - 1, BLOCKS):
                        wait(dve, S["ht"], j)
                        dve.tensor_copy(hT[1 - q][0:64, 0:128], bank(3 - q, 64, 0, 128))
                        dve.tensor_copy(hT[1 - q][0:96, 128:256], bank(5 - q, 96, 0, 128)).then_inc(S["hts"].sem, 1)
                    if within(j - 2, BLOCKS):
                        wait(dve, S["m"], j - 1)
                        if n == 0:
                            dve.tensor_copy(sj(j - 2), bank(q, P, 0, 192)).then_inc(S["side"].sem, 1)
                        elif n == 1:
                            dve.scalar_tensor_tensor(out=xj(j - 2), in0=bank(q, P, 0, NF),
                                                     scalar=attr[:, bass.ds(j - 2, 1)], in1=xj(j - 2),
                                                     op0=ALU.mult, op1=ALU.add).then_inc(S["side"].sem, 1)
                        else:
                            dve.tensor_scalar(side[:, bass.ds((j - 2) * 192, NF)], bank(q, P, 0, NF),
                                              attr[:, bass.ds(j - 2, 1)], None, ALU.mult).then_inc(S["side"].sem, 1)
                pipeline(dve, BLOCKS, 3, 2, 2, body)

            def places(o):
                link(dve.tensor_scalar(int_a, key_i[o], 5, None, ALU.arith_shift_right))
                link(dve.tensor_copy(bin_h[o], int_a))
                if o == 0:
                    link(dve.tensor_scalar(int_b, key_i[o], BIN - 1, None, ALU.bitwise_and))
                    link(dve.tensor_copy(key_f, int_b))
                with dve.Fori(0, BINS // WAYS) as i:
                    for k in range(WAYS):
                        dve.tensor_scalar(eq[k], bin_h[o], iota_bins[:, bass.ds(i * WAYS + k, 1)], 0.0, ALU.is_equal, ALU.add,
                                          accum_out=count[:, bass.ds(i * WAYS + k, 1)]).then_inc(s_cnt[o], 1)
                    dve.wait_ge(s_cnt[o], i * WAYS + WAYS)
                dve.wait_ge(s_cum[o], 1)
                link(dve.tensor_scalar(bins_i, bank(0, P, 128, 128 + BINS), float(P - 1), None, ALU.add))
                link(dve.tensor_scalar(bins_i, bins_i, 7, None, ALU.arith_shift_right))
                link(dve.tensor_copy(ntile, bins_i))
                if o:
                    link(dve.scalar_tensor_tensor(out=pad, in0=ntile, scalar=float(P), in1=bank(0, P, 128, 128 + BINS),
                                                  op0=ALU.mult, op1=ALU.subtract))
                link(dve.tensor_tensor_scan(first_tile, ntile, bins_z, 0.0, ALU.add, ALU.add))
                link(dve.tensor_tensor(first_tile, first_tile, ntile, ALU.subtract))
                link(dve.tensor_scalar(bins_f, first_tile, float(P), -1.0, ALU.mult, ALU.add))
                link(dve.tensor_tensor(base[o], bins_f, bank(0, P, 0, BINS), ALU.add))
                for c in range(TCOLS):
                    link(dve.tensor_scalar(bins_f, first_tile, tile_id[:, c:c + 1], 0.0, ALU.is_le, ALU.add,
                                           accum_out=tile_bin[:, c:c + 1]))
                if o:
                    dve.wait_ge(s_tbd[0], 16)
                dve.tensor_scalar(tile_bin_i, tile_bin, -1.0, None, ALU.add).then_inc(s_tb[o], 1)
                if o:
                    shape = [P, TCOLS, BINS]
                    tiles = by_tile.rearrange("p (c b) -> p c b", c=TCOLS)
                    link(dve.tensor_scalar(tile_node, tile_bin, float(BIN), -float(BIN), ALU.mult, ALU.add))
                    link(dve.tensor_tensor(first_tile, first_tile, ntile, ALU.add))
                    link(dve.tensor_tensor(tiles, first_tile.unsqueeze(1).to_broadcast(shape),
                                           tile_id.unsqueeze(2).to_broadcast(shape), ALU.is_le))
                    link(dve.tensor_tensor(tiles, tiles, pad.unsqueeze(1).to_broadcast(shape), ALU.mult))
                    link(dve.tensor_reduce(tile_pad, tiles, AX_X, ALU.add))
                    link(dve.scalar_tensor_tensor(out=tile_pad, in0=tile_id, scalar=float(P), in1=tile_pad,
                                                  op0=ALU.mult, op1=ALU.subtract))
                    dve.tensor_scalar(tile_start, tile_pad, float(P * COLS), 0.0, ALU.min, ALU.max).then_inc(s_start, 1)

            ranked = [0, 0]

            def rank(o, a, b, carry):
                w, done = b - a, ranked[o]
                with dve.Fori(0, BINS // WAYS) as i:
                    def bin_base(k):
                        return base[o][:, bass.ds(i * WAYS + k, 1)]
                    for k in range(WAYS):
                        dve.tensor_scalar(eq[k][:, a:b], bin_h[o][:, a:b], iota_bins[:, bass.ds(i * WAYS + k, 1)], None,
                                          ALU.is_equal).then_inc(s_eq[o], 1)
                    for k in range(WAYS):
                        dve.wait_ge(s_eq[o], i * WAYS + (done + k + 1))
                        dve.tensor_tensor_scan(bank(4 + k, P, 0, w), eq[k][:, a:b], zero_h[:, a:b], bin_base(k),
                                               ALU.add, ALU.add).then_inc(s_scan[o], 1)
                    for k in range(WAYS):
                        dve.wait_ge(s_scan[o], i * WAYS + (done + k + 1))
                        dve.sem_inc(s_apart["dve"], 1)
                        if carry:
                            dve.tensor_copy(bin_base(k), bank(4 + k, P, w - 1, w))
                        dve.copy_predicated(pos_f[k][:, a:b], eq[k][:, a:b], bank(4 + k, P, 0, w)).then_inc(s_pick[o], 1)
                    dve.wait_ge(s_pick[o], i * WAYS + (done + WAYS))
                ranked[o] += BINS

            def positions(o, a, b, link):
                ia, ib, out = int_a[:, a:b], int_b[:, a:b], pos_i[o][:, a:b]
                f = [p[:, a:b] for p in pos_f]
                dve.tensor_tensor(f[0], f[0], f[1], ALU.add)
                link(dve.tensor_tensor(f[2], f[2], f[3], ALU.add))
                link(dve.tensor_tensor(f[0], f[0], f[2], ALU.add))
                link(dve.tensor_copy(ia, f[0]))
                link(dve.tensor_scalar(out, ia, 10, 10, ALU.arith_shift_right, ALU.logical_shift_left))
                link(dve.tensor_scalar(ib, ia, P - 1, 3, ALU.bitwise_and, ALU.logical_shift_left))
                link(dve.tensor_tensor(out, out, ib, ALU.bitwise_or))
                link(dve.tensor_scalar(ib, ia, 7, GT - 1, ALU.arith_shift_right, ALU.bitwise_and))
                dve.tensor_tensor(out, out, ib, ALU.bitwise_or).then_inc(s_pos[o], 1)

            dve.wait_ge(s_const, 1)
            for p in pos_f:
                link(dve.memset(p, 0.0))
            places(0)

            def segment(i):
                a, b = SEGMENTS[i] * CHUNK, SEGMENTS[i + 1] * CHUNK
                rank(0, a, b, b < COLS)
                positions(0, a, b, link)
                dve.wait_ge(s_pos[0], i + 1)
            segment(0)
            link(dve.tensor_tensor(int_a, key_i[1], key_next, ALU.is_gt))
            link(dve.tensor_copy(norm, int_a))
            dve.tensor_reduce(falls, norm, AX_X, ALU.add).then_inc(s_falls, 1)
            places(1)
            dve.wait_ge(s_flag_sum, 1)
            dve.tensor_copy(unsorted[0:1, :], bank(1, 1, 0, 1)).then_inc(s_flag, 1)
            segment(1)
            segment(2)
            dve.wait_ge(s_nodes, 32)
            statistics(0)
            prep(0)
            dve.wait_ge(s_flag, 1)
            _, (flag,) = nc.values_load_multi_w_load_instructions(
                unsorted[0:1, 0:1], engines=(DVE,), min_val=0, max_val=P * COLS,
                skip_runtime_bounds_check_because="a count of edges")
            wait(dve, s_p[0]["tab"], BLOCKS)
            with dve.If(flag != 0):
                again = [0]

                def link_again(ins):
                    again[0] += 1
                    ins.then_inc(s_again, 1)
                    dve.wait_ge(s_again, again[0])
                for p in pos_f:
                    link_again(dve.memset(p, 0.0))
                rank(1, 0, COLS // 2, True)
                rank(1, COLS // 2, COLS, False)
                positions(1, 0, COLS, link_again)
                dve.wait_ge(s_pos[1], 1)
            dve.sem_inc(s_ranked, 1)

            for n in range(4):
                L, S, C = LAYERS[n], s_e[n], s_c[n]
                o = 0 if L.rowsA else 1
                if n:
                    wait(dve, S["zero"], 1)
                else:
                    dve.wait_ge(s_placed, 1)
                    dve.wait_ge(s_tbd[0], 16)
                    dve.wait_ge(s_tbd[1], 16)
                    dve.wait_ge(s_startd, 32)
                    link(dve.memset(acc[:, :], 0.0))
                if n != 2:
                    for q in range(2):
                        link(dve.memset(sel[q][:, :, 32:128], 0.0))
                dve.wait_ge(s_tbs[o], 16)
                if n:
                    dve.wait_ge(s_nodes_of, 16)

                def select(g, half, q, n=n, L=L, S=S):
                    wait(dve, S[f"rows{q}"], (half + 1) * (32 if n == 0 else 16))
                    if L.rowsA:
                        r = rows_a(q)[1]
                        key, e0, e1 = r[:, :, A_KEY - A_SH], None, r[:, :, 0:3]
                    else:
                        r = rows_b(q).rearrange("p (t c) -> p t c", c=B_W)
                        e0, e1 = r[:, :, B_4], r[:, :, B_4 + 1:B_4 + 4]
                        key = small[:, 7 + q, 0:GT]
                        dve.tensor_tensor(key, r[:, :, B_KEY], first_node[:, bass.ds(g * GT, GT)],
                                          ALU.subtract).then_inc(S["key"].sem, 1)
                        wait(dve, S["key"], g + 1)
                    nodes = iota_bin[:, :].unsqueeze(1).to_broadcast([P, GT, BIN])
                    hot = sel[q][:, :, 0:BIN] if n == 0 else onehot[:, :, :]
                    dve.tensor_tensor(hot, nodes, key.unsqueeze(2).to_broadcast([P, GT, BIN]),
                                      ALU.is_equal).then_inc(S["oh"].sem, 1)
                    wait(dve, S["oh"], g + 1)
                    if n == 2:
                        dve.tensor_tensor(sel[q][:, :, 0:128].rearrange("p t (k b) -> p t k b", k=4),
                                          hot.unsqueeze(2).to_broadcast([P, GT, 4, BIN]),
                                          r[:, :, B_4:B_4 + 4].unsqueeze(3).to_broadcast([P, GT, 4, BIN]),
                                          ALU.mult).then_inc(S["sel"].sem, 1)
                        return
                    if n:
                        dve.tensor_tensor(sel[q][:, :, 0:BIN], hot, e0.unsqueeze(2).to_broadcast([P, GT, BIN]), ALU.mult)
                    dve.tensor_tensor(sel[q][:, :, 128:224].rearrange("p t (k b) -> p t k b", k=3),
                                      hot.unsqueeze(2).to_broadcast([P, GT, 3, BIN]),
                                      e1.unsqueeze(3).to_broadcast([P, GT, 3, BIN]), ALU.mult).then_inc(S["sel"].sem, 1)

                def edges(g, half, q, n=n, L=L, S=S, o=o, select=select):
                    _, at = nc.values_load_multi_w_load_instructions(
                        tile_bins[0:1, bass.ds(g * GT, GT)], engines=(DVE,), min_val=0, max_val=BINS - 1,
                        skip_runtime_bounds_check_because="counts of at most BINS bins, less one")
                    for u in range(0, GT, 2):
                        m = g * GT + u
                        b = u // 2 % 2
                        for h in range(2):
                            if within(m - LAG_FL, TILES):
                                if h == 0:
                                    wait(dve, S["sc"], m - LAG_FL + 2)
                                wait(dve, S["fl"], m - LAG_FL + h)
                                sums = acc[:, bass.ds(at[u + h] * L.width, L.width)]
                                dve.tensor_tensor(sums, sums, bank(6 + b, P, 256 * h, 256 * h + L.width),
                                                  ALU.add).then_inc(S["fl"].sem, 1)
                            if not L.mlp or not within(m, TILES):
                                continue
                            if h == 0:
                                if u % HALF == 0:
                                    wait(dve, S[f"ga{q}{u // HALF}"], half * (16 * HALF) + 16 * HALF)
                                wait(dve, S["w"], m + 2)
                            wt = bank(4 + b, P, 224 * h, 224 * h + L.wcols)
                            xs = gath[q][:, u + h, 0:S0]
                            xv = gath[q][:, u + h, S0:NF].rearrange("p (c m) -> p c m", c=3)
                            nv = (L.wcols - 128) // V1
                            a = (2 * b + h) * (416 if n == 0 else 320)
                            if n == 0:
                                ps = prod[:, a:a + 704].rearrange("p (a c) -> p a c", a=2)[:, :, 0:S0]
                                pv = prod[:, a + S0:a + S0 + 288].rearrange("p (w c m) -> p w c m", w=3, c=3)
                            else:
                                both = prod[:, a:a + 320].rearrange("p (w c) -> p w c", w=2)
                                ps, pv = both[:, :, 0:S0], both[:, :, S0:NF].rearrange("p w (c m) -> p w c m", c=3)
                            dve.tensor_tensor(ps, wt[:, 0:128].rearrange("p (w c) -> p w c", w=2),
                                              xs.unsqueeze(1).to_broadcast([P, 2, S0]), ALU.mult)
                            dve.tensor_tensor(pv, wt[:, 128:L.wcols].rearrange("p (w m) -> p w m", w=nv)
                                              .unsqueeze(2).to_broadcast([P, nv, 3, V1]),
                                              xv.unsqueeze(1).to_broadcast([P, nv, 3, V1]),
                                              ALU.mult).then_inc(S["prod"].sem, 1)
                        if u == LAG_FL and within(g + 1, GROUPS):
                            select(g + 1, half + q, 1 - q)
                        if is_static(g) and g == GROUPS and u == LAG_FL - 2:
                            break
                select(0, 0, 0)
                pipeline(dve, GROUPS, 2, 2, 1, edges)

                (b0, b1) = L.chunks[1]

                def combine(j, half, q, n=n, L=L, C=C, b0=b0, b1=b1):
                    if within(j, BLOCKS):
                        wait(dve, C["trn"], j + 1)
                        if n % 2:
                            dve.tensor_copy(by_kind(sumT[q][0:96, 1, :])[:, 0], by_bin(bank(1, 96, 0, 512))[:, 0])
                            for i in range(3):
                                part = slice(V1 * i, V1 * i + V1)
                                ins = dve.tensor_copy(by_kind(sumT[q][part, 1, :])[:, 1], by_bin(pb[1][part, 0:512])[:, 1 + i])
                            ins.then_inc(C["cd"].sem, 1)
                        else:
                            dve.tensor_copy(by_kind(sumT[q][0:b1 - b0, 1, :]), by_bin(bank(1, b1 - b0, 0, 512))).then_inc(C["cd"].sem, 1)
                    if within(j - 1, BLOCKS):
                        k, r = j - 1, 1 - q
                        po = pb[2 + r]
                        wait(dve, C["big"], j)
                        if n == 0:
                            dve.scalar_tensor_tensor(out=tmp[r][:, :], in0=po[:, 0:192], scalar=1 / 32.0, in1=sj(k),
                                                     op0=ALU.mult, op1=ALU.add).then_inc(C["t1"].sem, 1)
                            wait(dve, C["sig"], j)
                            dve.tensor_tensor(trow[r][:, 0:64], tmp[r][:, 0:64], hbuf[r][:, 0:64], ALU.mult)
                            dve.tensor_tensor(trow[r][:, 64:NF].rearrange("p (c m) -> p c m", c=3),
                                              tmp[r][:, 96:192].rearrange("p (c m) -> p c m", c=3),
                                              hbuf[r][:, 64:96].unsqueeze(1).to_broadcast([P, 3, V1]),
                                              ALU.mult).then_inc(C["t2"].sem, 1)
                            wait(dve, C["t2"], j)
                            dve.tensor_tensor(xj(k), xj(k), trow[r][:, :], ALU.add).then_inc(C["ev"].sem, 1)
                        elif n == 1:
                            dve.scalar_tensor_tensor(out=xj(k), in0=po[:, 0:NF], scalar=small[:, 6, bass.ds(k, 1)],
                                                     in1=xj(k), op0=ALU.mult, op1=ALU.add).then_inc(C["ev"].sem, 1)
                        elif n == 3:
                            dve.tensor_scalar(acc[:, bass.ds(k * (4 * NF), NF + 1)], po[:, 0:NF + 1],
                                              attr[:, bass.ds(k, 1)], 1 / math.sqrt(960.0), ALU.mult,
                                              ALU.mult).then_inc(C["ev"].sem, 1)
                        else:
                            dve.tensor_scalar(hT[r][0:96, 128:256], bank(6 + r, 96, 0, 128),
                                              math.sqrt(3.0 / 128) / R3 / math.sqrt(32.0), None, ALU.mult).then_inc(C["mv"].sem, 1)
                    if n == 2 and within(j - 2, BLOCKS):
                        wait(dve, C["fin"], j - 1)
                        dve.scalar_tensor_tensor(out=xj(j - 2), in0=bank(4 + q, P, 0, NF), scalar=0.0, in1=xj(j - 2),
                                                 op0=ALU.max, op1=ALU.add).then_inc(C["ev"].sem, 1)
                    late_by = 3 if n == 2 else 2
                    if n < 3 and within(j - late_by, BLOCKS):
                        wait(dve, C["ev"], j - late_by + 1)
                        block_statistics(n + 1, j - late_by)
                if n == 2:
                    dve.wait_ge(s_lw, 16 * len(late))
                    for m, f in sum_factors(2):
                        ins = dve.tensor_scalar(m, m, f, None, ALU.mult)
                    ins.then_inc(s_lf, 1)
                if n == 1:
                    link(dve.tensor_scalar(small[:, 6, :], attr[:, :], 0.125 / math.sqrt(96.0), None, ALU.mult))
                pipeline(dve, BLOCKS, 3, 2, {0: 2, 1: 2, 2: 3, 3: 1}[n], combine)
                wait(dve, C["ev"], BLOCKS)
                if n < 3:
                    statistics(n + 1)
                    prep(n + 1)

            conv = acc[:, 0:BLOCKS * 4 * NF].rearrange("p (j c) -> p j c", j=BLOCKS)
            sc = side[:, :].rearrange("p (j c) -> p j c", j=BLOCKS)[:, :, 0:NF]
            x3 = x[:, :].rearrange("p (j c) -> p j c", j=BLOCKS)
            big = 12582912.0
            wait(dve, s_p[3]["side"], BLOCKS)
            link(dve.tensor_scalar(scratch(2), conv[:, :, 0], 0.1, None, ALU.mult))
            link(dve.tensor_scalar(scratch(3), scratch(2), 1 / (2 * math.pi), big, ALU.mult, ALU.add))
            link(dve.tensor_scalar(scratch(3), scratch(3), -big, None, ALU.add))
            link(dve.scalar_tensor_tensor(out=scratch(2), in0=scratch(3), scalar=-6.28125, in1=scratch(2),
                                          op0=ALU.mult, op1=ALU.add))
            link(dve.scalar_tensor_tensor(out=scratch(2), in0=scratch(3), scalar=-(2 * math.pi - 6.28125),
                                          in1=scratch(2), op0=ALU.mult, op1=ALU.add))
            link(dve.tensor_scalar(scratch(2), scratch(2), 3.1415925, -3.1415925, ALU.min, ALU.max))
            link(dve.scalar_tensor_tensor(out=scratch(3), in0=scratch(2), scalar=-1.0, in1=scratch(2),
                                          op0=ALU.mult, op1=ALU.max))
            dve.tensor_scalar(scratch(3), scratch(3), -1.0, math.pi / 2, ALU.mult, ALU.add).then_inc(s_trig, 1)
            dve.wait_ge(s_trig, 2)
            shape = [P, BLOCKS, NF]
            link(dve.tensor_tensor(sc, sc, scratch(5).unsqueeze(2).to_broadcast(shape), ALU.mult))
            link(dve.tensor_tensor(x3, x3, sc, ALU.add))
            link(dve.tensor_tensor(conv[:, :, 1:NF + 1], conv[:, :, 1:NF + 1],
                                   scratch(4).unsqueeze(2).to_broadcast(shape), ALU.mult))
            dve.tensor_tensor(x3, x3, conv[:, :, 1:NF + 1], ALU.add).then_inc(s_fin, 1)

        @block.tensor
        def _(pe):
            pe.wait_ge(s_const, 1)

            def prep(n):
                if n == 2:
                    return
                S = s_p[n]
                ns = LAYERS[n].tab_side

                def body(j, half, q):
                    if within(j, BLOCKS):
                        wait(pe, S["h"], j + 1)
                        pe.sem_inc(s_apart["pe"], 1)
                        pe.transpose(bank(2 + q, 64, 0, 128), hbuf[q][:, 0:64], ident[:, :])
                        pe.transpose(bank(4 + q, 96, 0, 128), hbuf[q][:, 64:NF], ident[:, :]).then_inc(S["ht"].sem, 1)
                    if within(j - 1, BLOCKS):
                        r = 1 - q
                        wait(pe, S["hts"], j)
                        wait(pe, S["tab"], j - 2)
                        wait(pe, S["side"], j - 2)
                        pe.sem_inc(s_apart["pe"], 1)
                        hs, hv = hT[r][0:64, 0:128], hT[r][0:96, 128:256]
                        pe.matmul(bank(6 + r, P, 0, 64), hs, wps[n][:, 0:64], start=True, stop=True, skip_group_check=True)
                        pe.matmul(bank(6 + r, P, 64, 160), hv, wpv[n][:, 0:96], start=False, stop=True, skip_group_check=True)
                        pe.matmul(bank(r, P, 0, ns), hs, wps[n][:, 64:64 + ns], start=True, stop=True, skip_group_check=True)
                        pe.matmul(bank(r, P, ns, 96 + ns), hv, wpv[n][:, 96:192], start=False, stop=True,
                                  skip_group_check=True).then_inc(S["m"].sem, 1)
                pipeline(pe, BLOCKS, 3, 2, 1, body)

            for o in range(2):
                if o:
                    pe.wait_ge(s_falls, 1)
                    pe.matmul(bank(1, 1, 0, 1), falls, ones[:, 0:1], start=True, stop=True).then_inc(s_flag_sum, 1)
                    pe.wait_ge(s_tb[0], 1)
                pe.wait_ge(s_cnt[o], BINS)
                pe.matmul(bank(0, P, 0, BINS), tri, count, start=True, stop=True)
                pe.matmul(bank(0, P, 128, 128 + BINS), ones, count, start=True, stop=True).then_inc(s_cum[o], 1)
            pe.wait_ge(s_flag, 1)
            pe.wait_ge(s_start, 1)
            pe.wait_ge(s_pos[0], 3)
            pe.wait_ge(s_w, 16 * len(loads))
            pe.wait_ge(s_wf, N_SCALED)
            prep(0)

            for n in range(4):
                L, S, C = LAYERS[n], s_e[n], s_c[n]
                pe.wait_ge(s_ranked, 1)
                if n:
                    wait(pe, s_c[n - 1]["ev"], BLOCKS)
                if n != 2:
                    wait(pe, s_p[n]["side"], BLOCKS)
                    wait(pe, s_p[n]["tab"], BLOCKS)

                def turn(g, half, q, n=n, S=S):
                    wait(pe, S[f"rows{q}"], (half + 1) * (32 if n == 0 else 16))
                    pe.sem_inc(s_apart["pe"], 1)
                    if n == 0:
                        for p in range(4):
                            i = pe.transpose(bank(0, P, 128 * p, 128 * p + 128), rows_a(q)[0][:, 128 * p:128 * p + 128], ident[:, :])
                    else:
                        for p in range(2):
                            i = pe.transpose(bank(0, P, 128 * p, 128 * p + 128), rows_b(q)[:, 128 * p:128 * p + 128], ident[:, :])
                    i.then_inc(S["tr"].sem, 1)

                def hidden(g, n=n, S=S):
                    wait(pe, S["tc"], g + 1)
                    if n == 0:
                        i = pe.matmul(bank(2, P, 0, 512), w1[0][:, :], attrT[:, 0:512], start=True, stop=True)
                    elif n == 1:
                        for k in range(4):
                            i = pe.matmul(bank(2 + k // 2, 100, 256 * (k % 2), 256 * (k % 2) + 256), w1[1][:, k, :],
                                          attrT[:, 0:256], start=True, stop=True)
                    else:
                        for k in range(2):
                            i = pe.matmul(bank(2, P, 256 * k, 256 * k + 256), w1[3][:, k, :], attrT[:, 0:256],
                                          start=True, stop=True)
                    i.then_inc(S["m1"].sem, 1)

                def hidden_of(u, q, n=n):
                    if n == 0:
                        return hidT[q][:, 128 * (u // 2):128 * (u // 2) + 128], w2[0][:, u % 2, :]
                    quad, k = u // 4, u % 4
                    if n == 1:
                        a = (k * 2 + quad) * 128
                        return hidT[q][0:100, a:a + 128], w2[1][0:100, :]
                    a = (k // 2 * 2 + quad) * 128
                    return hidT[q][:, a:a + 128], w2[3][:, k % 2, :]

                def edges(g, half, q, n=n, L=L, S=S, turn=turn, hidden=hidden, hidden_of=hidden_of):
                    lag = LAG_SC if L.mlp else 0
                    for u in range(0, GT, 2):
                        m = g * GT + u
                        if L.mlp and within(m, TILES):
                            if u == 0:
                                wait(pe, S["hid"], g + 1)
                            for h in range(2):
                                hid, w = hidden_of(u + h, q)
                                pe.matmul(bank(4 + u // 2 % 2, P, 224 * h, 224 * h + L.wcols), hid, w,
                                          start=True, stop=True, skip_group_check=True).then_inc(S["w"].sem, 1)
                        if within(m - lag, TILES):
                            v = (u - lag) % GT
                            b = v // 2 % 2
                            qv = q if u >= lag else 1 - q
                            if v == 0:
                                wait(pe, S["sel"], g + 1)
                            if not L.mlp and v % HALF == 0:
                                wait(pe, S[f"ga{q}{v // HALF}"], half * (16 * HALF) + 16 * HALF)
                            if L.mlp:
                                wait(pe, S["prod"], m - lag + 2)
                            wait(pe, S["fl"], m - lag - RING + 2)
                            for h in range(2):
                                out = bank(6 + b, P, 256 * h, 256 * h + L.width)
                                if n == 2:
                                    ins = pe.matmul(out, sel[qv][:, v + h, 0:128], gath[qv][:, v + h, :],
                                                    start=True, stop=True, skip_group_check=True)
                                else:
                                    a = (2 * b + h) * (416 if n == 0 else 320)
                                    end = a + NF + L.width
                                    pe.matmul(out, sel[qv][:, v + h, 96:224], prod[:, a + NF:end], start=True, stop=False,
                                              skip_group_check=True)
                                    ins = pe.matmul(bank(6 + b, P, 256 * h, 256 * h + NF), sel[qv][:, v + h, 0:128],
                                                    prod[:, a:a + NF], start=False, stop=True, skip_group_check=True)
                                ins.then_inc(S["sc"].sem, 1)
                        if L.mlp and within(g + 1, GROUPS):
                            if u == 0:
                                turn(g + 1, half + q, 1 - q)
                            if u == 4:
                                hidden(g + 1)
                        if is_static(g) and g == GROUPS and u == lag - 2:
                            break
                if L.mlp:
                    turn(0, 0, 0)
                    hidden(0)
                pipeline(pe, GROUPS, 2, 2, 1 if L.mlp else 0, edges)

                wait(pe, S["fl"], TILES)
                if n:
                    pe.wait_ge(s_lw, 16 * len(late))
                if n == 2:
                    pe.wait_ge(s_lf, 1)
                order = sum_products(n)

                def combine(j, half, q, n=n, L=L, C=C, order=order):
                    if within(j, BLOCKS):
                        wait(pe, C["stg"], j + 1)
                        wait(pe, C["stga"], j + 1)
                        wait(pe, C["ca"], j)
                        wait(pe, C["cd"], j)
                        pe.sem_inc(s_apart["pe"], 1)
                        for c, (a, b) in enumerate(L.chunks):
                            for i in range(4):
                                ins = pe.transpose(bank(c, b - a, 128 * i, 128 * i + 128),
                                                   stg[q][:, L.width * i + a:L.width * i + b], ident[:, :])
                        ins.then_inc(C["trn"].sem, 1)
                    if within(j - 1, BLOCKS):
                        r = 1 - q
                        wait(pe, C["ca"], j)
                        wait(pe, C["cd"], j)
                        if n != 2:
                            wait(pe, C["ev"], j - 2)
                        pe.sem_inc(s_apart["pe"], 1)

                        def sums(c, k, rows_):
                            return sumT[r][0:rows_, c, 128 * k:128 * k + 128]
                        if n == 2:
                            for lo, hi, b0, terms in ((0, 64, 2, [(0, 0)] + [(1, k) for k in (1, 2, 3)]),
                                                      (64, 160, 6, [(0, k) for k in (1, 2, 3)] + [(1, k) for k in range(4)])):
                                for i, (c, k) in enumerate(terms):
                                    rr = 64 if c == 0 else 96
                                    ins = pe.matmul(bank(b0 + r, hi - lo, 0, 128), wsum[2][0:rr, c, k, lo:hi], sums(c, k, rr),
                                                    start=(i == 0), stop=(i == len(terms) - 1))
                            ins.then_inc(C["big"].sem, 1)
                        else:
                            for i, (c, k, rr, lo, hi) in enumerate(order):
                                ins = pe.matmul(bank(2 + r, P, lo, hi), sums(c, k, rr), wsum[n][0:rr, c, k, lo:hi],
                                                start=(i == 0), stop=(i == len(order) - 1), skip_group_check=True)
                            ins.then_inc(C["big"].sem, 1)
                    if n == 2 and within(j - 2, BLOCKS):
                        wait(pe, C["ms"], j - 1)
                        wait(pe, C["mv"], j - 1)
                        wait(pe, C["ev"], j - 3)
                        pe.sem_inc(s_apart["pe"], 1)
                        pe.matmul(bank(4 + q, P, 0, 64), hT[q][0:64, 0:128], w2s[:, :], start=True, stop=True,
                                  skip_group_check=True)
                        pe.matmul(bank(4 + q, P, 64, NF), hT[q][0:96, 128:256], w2v[:, :], start=False, stop=True,
                                  skip_group_check=True).then_inc(C["fin"].sem, 1)
                pipeline(pe, BLOCKS, 3, 2, 2 if n == 2 else 1, combine)
                if n < 3:
                    prep(n + 1)


_WEIGHTS = ["L0_gnn_W_skip0", "L0_gnn_W_skip1", "L0_gnn_W_nl0", "L0_gnn_W_nl1", "L0_gnn_W_fc1", "L0_gnn_W_fc2",
            "L0_gnn_W_out_s", "L0_gnn_W_out_v", "L1_gnn_W_si0", "L1_gnn_W_si1", "L1_gnn_W_l1_0", "L1_gnn_W_l1_1",
            "L1_gnn_W_l2_00", "L1_gnn_W_l2_10", "L1_gnn_W_l2_01", "L1_gnn_W_l2_11", "L1_gnn_W_fc1", "L1_gnn_W_fc2",
            "L2_gnn_W1", "L2_gnn_W2", "L2_gnn_W3", "L2_gnn_W4", "L2_gnn_W5", "L2_gnn_Ws", "L2_gnn_Wv",
            "L3_gnn_W_sc_s", "L3_gnn_W_sc_v", "L3_gnn_W1_s", "L3_gnn_W1_v", "L3_gnn_W2_s", "L3_gnn_W2_v", "L3_gnn_W3",
            "L3_gnn_fcW1", "L3_gnn_fcW2"]


def _feature_order(np):
    return np.concatenate([np.arange(S0), S0 + (np.arange(V1)[None, :] * 3 + np.arange(3)[:, None]).ravel()])


def kernel(**inputs):
    import numpy as np
    import concourse.bacc as bacc
    from concourse.bass_utils import run_bass_kernel_spmd

    def padded(a, n, value):
        a = np.asarray(a)
        return np.concatenate([a, np.full((n - a.shape[0],) + a.shape[1:], value, a.dtype)])

    def rows_of(parts, width):
        rows = np.concatenate([np.asarray(inputs[k]) for k in parts], axis=1)
        out = np.zeros((P * COLS, width), rows.dtype)
        out[:EDGES, :rows.shape[1]] = rows
        return out.reshape(P, COLS * width)

    order = _feature_order(np)
    arrays = {
        "x": padded(np.asarray(inputs["x"])[:, order], NPAD, 0),
        "node_vec1": padded(inputs["node_vec1"], NPAD, 0),
        "skey": padded(inputs["src"], P * COLS, PAD_NODE).reshape(P, COLS),
        "dkey": padded(inputs["dst"], P * COLS + 1, PAD_NODE),
        "edge_attr_3": padded(inputs["edge_attr_3"], P * COLS, 1).reshape(P, COLS * 3),
        "rows_a": rows_of(["edge_attr_64"], A_W),
        "rows_b": rows_of(["edge_attr_10", "edge_attr_8", "edge_attr_4"], B_W),
    }
    for k in _WEIGHTS:
        arrays[k] = np.ascontiguousarray(inputs[k])
    nc = bacc.Bacc("TRN2", target_bir_lowering=False, num_devices=1)
    t = {k: nc.dram_tensor(f"in_{k}", a.shape, mybir.dt.from_np(a.dtype), kind="ExternalInput").ap()
         for k, a in arrays.items()}
    t["out"] = nc.dram_tensor("out_x", (NPAD, NF), F32, kind="ExternalOutput").ap()
    gnn_program(nc, t)
    r = run_bass_kernel_spmd(nc, [{f"in_{k}": a for k, a in arrays.items()}], core_ids=[0])
    got = np.asarray(r.results[0]["out_x"])
    back = np.argsort(order)
    return got[:NODES][:, back]
```
